# Optimizing a Trainium2 kernel written in Bass

```python
import numpy as np
import jax
import jax.numpy as jnp

def _softmax(x, axis=-1):
    return jax.nn.softmax(x, axis=axis)

def _gelu(x):
    return jax.nn.gelu(x, approximate=True)

def _silu(x):
    return jax.nn.silu(x)

def _sigmoid(x):
    return jax.nn.sigmoid(x)

def _layernorm(x, axis=-1, eps=1e-05):
    m = jnp.mean(x, axis=axis, keepdims=True)
    v = jnp.var(x, axis=axis, keepdims=True)
    return (x - m) / jnp.sqrt(v + eps)

def _scatter_add(tgt, idx, src, axis=0):
    return tgt.at[idx].add(src)

def _segment_sum(src, seg, n):
    return jax.ops.segment_sum(src, seg, n)
kernel_name = 'mk_metaformer_d2_conv_nchw256_r4_a02302'

def setup_inputs(seed: int=0):
    np.random.seed(seed)
    _w = jnp.asarray

    def _rec_inputs():
        import jax
        import jax.numpy as jnp
        _gk = jax.random.key(seed)
        x = -0.0003929 + 0.9999 * jax.random.normal(jax.random.fold_in(_gk, 1), (16, 64, 16, 16), jnp.float32)
        return x
    x = _rec_inputs()

    def _L0_conv_setup():
        import jax, jax.numpy as jnp
        import numpy as np
        C = 64
        R = 16
        CR = C // R
        key = jax.random.key(seed)
        ks = jax.random.split(key, 12)
        s = lambda *sh: 1.0 / np.sqrt(np.prod(sh[1:]) if len(sh) > 1 else 1.0)
        return {'x': jax.random.normal(ks[0], (16, C, 16, 16), dtype=jnp.float32), 'ca_w1': jax.random.normal(ks[1], (CR, C), dtype=jnp.float32) * s(CR, C), 'ca_b1': jnp.zeros((CR,), dtype=jnp.float32), 'ca_w2': jax.random.normal(ks[2], (C, CR), dtype=jnp.float32) * s(C, CR), 'ca_b2': jnp.zeros((C,), dtype=jnp.float32), 'sa_w': jax.random.normal(ks[3], (1, C, 3, 3), dtype=jnp.float32) * s(1, C, 3, 3), 'sa_b': jnp.zeros((1,), dtype=jnp.float32), 'tp_w1': jax.random.normal(ks[4], (CR, C), dtype=jnp.float32) * s(CR, C), 'tp_b1': jnp.zeros((CR,), dtype=jnp.float32), 'tp_w2': jax.random.normal(ks[5], (1, CR), dtype=jnp.float32) * s(1, CR), 'tp_b2': jnp.zeros((1,), dtype=jnp.float32)}
    _L0_conv_all = _L0_conv_setup()
    _L0_conv_in = {k: v for k, v in _L0_conv_all.items() if k in ('ca_w1', 'ca_b1', 'ca_w2', 'ca_b2', 'sa_w', 'sa_b', 'tp_w1', 'tp_b1', 'tp_w2', 'tp_b2')}
    del _L0_conv_all

    def _L0_ffn_setup():
        import jax, jax.numpy as jnp
        import numpy as np
        NUM_EXPERTS = 8
        TOP_K = 2
        B, S, D = (8, 2048, 64)

        def _moe(tokens, router_w, w1, b1, w2, b2):
            N = tokens.shape[0]
            E = router_w.shape[0]
            logits = tokens.astype(jnp.float32) @ router_w.astype(jnp.float32).T
            probs = jax.nn.softmax(logits, axis=-1)
            rw, re = jax.lax.top_k(probs, TOP_K)
            if TOP_K > 1:
                rw = rw / jnp.maximum(rw.sum(-1, keepdims=True), 1e-12)
            rw = rw.astype(tokens.dtype)
            combine = jnp.zeros((N, E), tokens.dtype).at[jnp.arange(N)[:, None], re].set(rw)
            out = tokens
            for e in range(E):
                h = jax.nn.gelu(tokens @ w1[e] + b1[e], approximate=False)
                y = h @ w2[e] + b2[e]
                out = out + combine[:, e:e + 1] * y
            return out
        key = jax.random.key(seed)
        ks = jax.random.split(key, 4)
        scale = 1.0 / np.sqrt(D).astype(np.float32)
        return {'input_embeddings': jax.random.normal(ks[0], (B, S, D), jnp.float32), 'router_w': jax.random.normal(ks[1], (NUM_EXPERTS, D), jnp.float32) * scale, 'w1': jax.random.normal(ks[2], (NUM_EXPERTS, D, D), jnp.float32) * scale, 'b1': jnp.zeros((NUM_EXPERTS, D), jnp.float32), 'w2': jax.random.normal(ks[3], (NUM_EXPERTS, D, D), jnp.float32) * scale, 'b2': jnp.zeros((NUM_EXPERTS, D), jnp.float32)}
    _L0_ffn_all = _L0_ffn_setup()
    _L0_ffn_in = {k: v for k, v in _L0_ffn_all.items() if k in ('router_w', 'w1', 'b1', 'w2', 'b2')}
    del _L0_ffn_all

    def _L1_conv_setup():
        import jax, jax.numpy as jnp
        import numpy as np
        CHAN = 64
        KEY_DIM = 16
        VALUE_DIM = 16
        HEADS = 8

        def _conv1x1(x, W, b):
            return jnp.einsum('oc,bchw->bohw', W, x) + b[None, :, None, None]
        key = jax.random.key(seed)
        ks = jax.random.split(key, 9)
        scale = 1.0 / np.sqrt(CHAN)
        x = jax.random.normal(ks[0], (16, CHAN, 16, 16), dtype=jnp.float32)
        Wq = jax.random.normal(ks[1], (KEY_DIM * HEADS, CHAN), dtype=jnp.float32) * scale
        bq = jax.random.normal(ks[2], (KEY_DIM * HEADS,), dtype=jnp.float32) * 0.01
        Wk = jax.random.normal(ks[3], (KEY_DIM, CHAN), dtype=jnp.float32) * scale
        bk = jax.random.normal(ks[4], (KEY_DIM,), dtype=jnp.float32) * 0.01
        Wv = jax.random.normal(ks[5], (VALUE_DIM, CHAN), dtype=jnp.float32) * scale
        bv = jax.random.normal(ks[6], (VALUE_DIM,), dtype=jnp.float32) * 0.01
        Wo = jax.random.normal(ks[7], (CHAN, VALUE_DIM * HEADS), dtype=jnp.float32) * (1.0 / np.sqrt(VALUE_DIM * HEADS))
        bo = jax.random.normal(ks[8], (CHAN,), dtype=jnp.float32) * 0.01
        return {'x': x, 'Wq': Wq, 'bq': bq, 'Wk': Wk, 'bk': bk, 'Wv': Wv, 'bv': bv, 'Wo': Wo, 'bo': bo}
    _L1_conv_all = _L1_conv_setup()
    _L1_conv_in = {k: v for k, v in _L1_conv_all.items() if k in ('Wq', 'bq', 'Wk', 'bk', 'Wv', 'bv', 'Wo', 'bo')}
    del _L1_conv_all

    def _L1_ffn_setup():
        import jax, jax.numpy as jnp
        import numpy as np
        BN_EPS = 0.001

        def _bn(h, g, b, m, v):
            return g * (h - m) * jax.lax.rsqrt(v + BN_EPS) + b
        key = jax.random.key(seed)
        ks = jax.random.split(key, 8)
        B, F, Df = (64, 16, 64)
        E, H, D = (8, 64, 64)
        s1 = 1.0 / np.sqrt(Df)
        s2 = 1.0 / np.sqrt(H)
        return {'x': jax.random.normal(ks[0], (B, F, Df), jnp.float32), 'Wr': jax.random.normal(ks[1], (Df, E), jnp.float32) * s1, 'br': jnp.zeros((E,), jnp.float32), 'W1': jax.random.normal(ks[2], (E, Df, H), jnp.float32) * s1, 'b1': jnp.zeros((E, H), jnp.float32), 'g1': jnp.ones((E, H), jnp.float32), 'be1': jnp.zeros((E, H), jnp.float32), 'm1': jnp.zeros((E, H), jnp.float32), 'v1': jnp.ones((E, H), jnp.float32), 'W2': jax.random.normal(ks[3], (E, H, H), jnp.float32) * s2, 'b2': jnp.zeros((E, H), jnp.float32), 'g2': jnp.ones((E, H), jnp.float32), 'be2': jnp.zeros((E, H), jnp.float32), 'm2': jnp.zeros((E, H), jnp.float32), 'v2': jnp.ones((E, H), jnp.float32), 'Wo': jax.random.normal(ks[4], (E, H, D), jnp.float32) * s2, 'bo': jnp.zeros((E, D), jnp.float32)}
    _L1_ffn_all = _L1_ffn_setup()
    _L1_ffn_in = {k: v for k, v in _L1_ffn_all.items() if k in ('Wr', 'br', 'W1', 'b1', 'g1', 'be1', 'm1', 'v1', 'W2', 'b2', 'g2', 'be2', 'm2', 'v2', 'Wo', 'bo')}
    del _L1_ffn_all
    return {'x': x, 'L0_conv_ca_w1': _L0_conv_in['ca_w1'], 'L0_conv_ca_b1': _L0_conv_in['ca_b1'], 'L0_conv_ca_w2': _L0_conv_in['ca_w2'], 'L0_conv_ca_b2': _L0_conv_in['ca_b2'], 'L0_conv_sa_w': _L0_conv_in['sa_w'], 'L0_conv_sa_b': _L0_conv_in['sa_b'], 'L0_conv_tp_w1': _L0_conv_in['tp_w1'], 'L0_conv_tp_b1': _L0_conv_in['tp_b1'], 'L0_conv_tp_w2': _L0_conv_in['tp_w2'], 'L0_conv_tp_b2': _L0_conv_in['tp_b2'], 'L0_ffn_router_w': _L0_ffn_in['router_w'], 'L0_ffn_w1': _L0_ffn_in['w1'], 'L0_ffn_b1': _L0_ffn_in['b1'], 'L0_ffn_w2': _L0_ffn_in['w2'], 'L0_ffn_b2': _L0_ffn_in['b2'], 'L1_conv_Wq': _L1_conv_in['Wq'], 'L1_conv_bq': _L1_conv_in['bq'], 'L1_conv_Wk': _L1_conv_in['Wk'], 'L1_conv_bk': _L1_conv_in['bk'], 'L1_conv_Wv': _L1_conv_in['Wv'], 'L1_conv_bv': _L1_conv_in['bv'], 'L1_conv_Wo': _L1_conv_in['Wo'], 'L1_conv_bo': _L1_conv_in['bo'], 'L1_ffn_Wr': _L1_ffn_in['Wr'], 'L1_ffn_br': _L1_ffn_in['br'], 'L1_ffn_W1': _L1_ffn_in['W1'], 'L1_ffn_b1': _L1_ffn_in['b1'], 'L1_ffn_g1': _L1_ffn_in['g1'], 'L1_ffn_be1': _L1_ffn_in['be1'], 'L1_ffn_m1': _L1_ffn_in['m1'], 'L1_ffn_v1': _L1_ffn_in['v1'], 'L1_ffn_W2': _L1_ffn_in['W2'], 'L1_ffn_b2': _L1_ffn_in['b2'], 'L1_ffn_g2': _L1_ffn_in['g2'], 'L1_ffn_be2': _L1_ffn_in['be2'], 'L1_ffn_m2': _L1_ffn_in['m2'], 'L1_ffn_v2': _L1_ffn_in['v2'], 'L1_ffn_Wo': _L1_ffn_in['Wo'], 'L1_ffn_bo': _L1_ffn_in['bo']}

def reference(x, L0_conv_ca_w1, L0_conv_ca_b1, L0_conv_ca_w2, L0_conv_ca_b2, L0_conv_sa_w, L0_conv_sa_b, L0_conv_tp_w1, L0_conv_tp_b1, L0_conv_tp_w2, L0_conv_tp_b2, L0_ffn_router_w, L0_ffn_w1, L0_ffn_b1, L0_ffn_w2, L0_ffn_b2, L1_conv_Wq, L1_conv_bq, L1_conv_Wk, L1_conv_bk, L1_conv_Wv, L1_conv_bv, L1_conv_Wo, L1_conv_bo, L1_ffn_Wr, L1_ffn_br, L1_ffn_W1, L1_ffn_b1, L1_ffn_g1, L1_ffn_be1, L1_ffn_m1, L1_ffn_v1, L1_ffn_W2, L1_ffn_b2, L1_ffn_g2, L1_ffn_be2, L1_ffn_m2, L1_ffn_v2, L1_ffn_Wo, L1_ffn_bo):
    import jax
    import jax.numpy as jnp

    def _L0_conv_ref(x, ca_w1, ca_b1, ca_w2, ca_b2, sa_w, sa_b, tp_w1, tp_b1, tp_w2, tp_b2):
        import jax, jax.numpy as jnp
        import numpy as np
        C = 64
        R = 16
        CR = C // R
        B = x.shape[0]
        pooled = x.mean(axis=(2, 3))
        h = jax.nn.relu(pooled @ ca_w1.T + ca_b1)
        channel_weights = jax.nn.sigmoid(h @ ca_w2.T + ca_b2)
        channel_weights = channel_weights[:, :, None, None]
        sp = jax.lax.conv_general_dilated(x, sa_w, window_strides=(1, 1), padding='SAME', dimension_numbers=('NCHW', 'OIHW', 'NCHW'))
        spatial_weights = jax.nn.sigmoid(sp + sa_b[None, :, None, None])
        th = jax.nn.relu(jnp.einsum('bchw,rc->brhw', x, tp_w1) + tp_b1[None, :, None, None])
        relative_threshold = jax.nn.sigmoid(jnp.einsum('brhw,or->bohw', th, tp_w2) + tp_b2[None, :, None, None])
        abs_x = jnp.abs(x)
        global_threshold = jnp.quantile(abs_x.reshape(B, -1), 0.85, axis=1)
        global_threshold = global_threshold.reshape(B, 1, 1, 1)
        threshold = global_threshold * relative_threshold
        mask = jax.nn.sigmoid((abs_x - threshold) * 10.0)
        return x * mask * channel_weights * spatial_weights

    def _L0_ffn_ref(input_embeddings, router_w, w1, b1, w2, b2):
        import jax, jax.numpy as jnp
        import numpy as np
        NUM_EXPERTS = 8
        TOP_K = 2
        B, S, D = (8, 2048, 64)

        def _moe(tokens, router_w, w1, b1, w2, b2):
            N = tokens.shape[0]
            E = router_w.shape[0]
            logits = tokens.astype(jnp.float32) @ router_w.astype(jnp.float32).T
            probs = jax.nn.softmax(logits, axis=-1)
            rw, re = jax.lax.top_k(probs, TOP_K)
            if TOP_K > 1:
                rw = rw / jnp.maximum(rw.sum(-1, keepdims=True), 1e-12)
            rw = rw.astype(tokens.dtype)
            combine = jnp.zeros((N, E), tokens.dtype).at[jnp.arange(N)[:, None], re].set(rw)
            out = tokens
            for e in range(E):
                h = jax.nn.gelu(tokens @ w1[e] + b1[e], approximate=False)
                y = h @ w2[e] + b2[e]
                out = out + combine[:, e:e + 1] * y
            return out
        b, s, d = input_embeddings.shape
        tokens = input_embeddings.reshape(b * s, d)
        return _moe(tokens, router_w, w1, b1, w2, b2).reshape(b, s, d)

    def _L1_conv_ref(x, Wq, bq, Wk, bk, Wv, bv, Wo, bo):
        import jax, jax.numpy as jnp
        import numpy as np
        CHAN = 64
        KEY_DIM = 16
        VALUE_DIM = 16
        HEADS = 8

        def _conv1x1(x, W, b):
            return jnp.einsum('oc,bchw->bohw', W, x) + b[None, :, None, None]
        b, _, h, w = x.shape
        n = h * w
        q = _conv1x1(x, Wq, bq).reshape(b, HEADS, KEY_DIM, n)
        k = _conv1x1(x, Wk, bk).reshape(b, KEY_DIM, n)
        v = _conv1x1(x, Wv, bv).reshape(b, VALUE_DIM, n)
        k = jax.nn.softmax(k, axis=2)
        q = jax.nn.softmax(q, axis=2)
        context = jnp.einsum('bdn,ben->bde', k, v)
        out = jnp.einsum('bhdn,bde->bhen', q, context)
        out = out.reshape(b, HEADS * VALUE_DIM, h, w)
        return _conv1x1(out, Wo, bo)

    def _L1_ffn_ref(x, Wr, br, W1, b1, g1, be1, m1, v1, W2, b2, g2, be2, m2, v2, Wo, bo):
        import jax, jax.numpy as jnp
        import numpy as np
        BN_EPS = 0.001

        def _bn(h, g, b, m, v):
            return g * (h - m) * jax.lax.rsqrt(v + BN_EPS) + b
        feat = jnp.mean(x, axis=0)
        w = jax.nn.softmax(feat @ Wr + br, axis=-1)
        h = jnp.einsum('bfd,edh->bfeh', x, W1) + b1
        h = jax.nn.relu(_bn(h, g1, be1, m1, v1))
        h = jnp.einsum('bfeh,ehk->bfek', h, W2) + b2
        h = jax.nn.relu(_bn(h, g2, be2, m2, v2))
        y = jnp.einsum('bfeh,ehd->bfed', h, Wo) + bo
        return jnp.einsum('bfed,fe->bfd', y, w)

    def _gn(v, G=32, eps=1e-05):
        B_, C_, H_, W_ = v.shape
        g = v.reshape(B_, G, C_ // G, H_, W_)
        m = jnp.mean(g, axis=(2, 3, 4), keepdims=True)
        s = jnp.var(g, axis=(2, 3, 4), keepdims=True)
        return ((g - m) / jnp.sqrt(s + eps)).reshape(v.shape)

    def _ln_c(v, eps=1e-06):
        m = jnp.mean(v, axis=1, keepdims=True)
        s = jnp.var(v, axis=1, keepdims=True)
        return (v - m) / jnp.sqrt(s + eps)

    def _ln_t(v, eps=1e-05):
        m = jnp.mean(v, axis=-1, keepdims=True)
        s = jnp.var(v, axis=-1, keepdims=True)
        return (v - m) / jnp.sqrt(s + eps)

    def _to_tokens(v):
        B_, C_, H_, W_ = v.shape
        return v.reshape(B_, C_, H_ * W_).transpose(0, 2, 1)

    def _from_tokens(t, like):
        B_, C_, H_, W_ = like.shape
        return t.transpose(0, 2, 1).reshape(B_, C_, H_, W_)
    x = x + _L0_conv_ref(_ln_c(x), L0_conv_ca_w1, L0_conv_ca_b1, L0_conv_ca_w2, L0_conv_ca_b2, L0_conv_sa_w, L0_conv_sa_b, L0_conv_tp_w1, L0_conv_tp_b1, L0_conv_tp_w2, L0_conv_tp_b2)
    t = _to_tokens(x)
    t = t + _L0_ffn_ref(_ln_t(t), L0_ffn_router_w, L0_ffn_w1, L0_ffn_b1, L0_ffn_w2, L0_ffn_b2)
    x = _from_tokens(t, x)
    x = x + _L1_conv_ref(_ln_c(x), L1_conv_Wq, L1_conv_bq, L1_conv_Wk, L1_conv_bk, L1_conv_Wv, L1_conv_bv, L1_conv_Wo, L1_conv_bo)
    t = _to_tokens(x)
    t = t + _L1_ffn_ref(_ln_t(t), L1_ffn_Wr, L1_ffn_br, L1_ffn_W1, L1_ffn_b1, L1_ffn_g1, L1_ffn_be1, L1_ffn_m1, L1_ffn_v1, L1_ffn_W2, L1_ffn_b2, L1_ffn_g2, L1_ffn_be2, L1_ffn_m2, L1_ffn_v2, L1_ffn_Wo, L1_ffn_bo)
    x = _from_tokens(t, x)
    return x

_drawn_inputs = setup_inputs


def setup_inputs(seed=0):
    import zlib

    import numpy as np

    out = dict(_drawn_inputs(seed))
    spreads = {'L0_conv_ca_b1': (0.0, 0.8),
     'L0_conv_ca_b2': (0.0, 0.458),
     'L0_conv_tp_b1': (0.0, 2.0),
     'L0_ffn_b1': (0.0, 0.357),
     'L0_ffn_b2': (0.0, 0.1),
     'L1_ffn_br': (0.0, 0.8),
     'L1_ffn_b1': (0.0, 0.8),
     'L1_ffn_g1': (1.0, 0.6),
     'L1_ffn_be1': (0.0, 0.8),
     'L1_ffn_m1': (0.0, 0.8),
     'L1_ffn_v1': (1.0, 0.6),
     'L1_ffn_b2': (0.0, 0.615),
     'L1_ffn_g2': (1.0, 0.6),
     'L1_ffn_be2': (0.0, 0.727),
     'L1_ffn_m2': (0.0, 0.648),
     'L1_ffn_v2': (1.0, 0.6),
     'L1_ffn_bo': (0.0, 0.451)}
    factors = {'L0_conv_ca_w1': 6.974,
     'L0_conv_ca_w2': 4.901,
     'L1_conv_Wq': 3.173,
     'L1_conv_bq': 64.0,
     'L1_conv_Wk': 2.765,
     'L1_conv_bk': 64.0,
     'L1_conv_bv': 8.0,
     'L1_conv_bo': 8.0,
     'L1_ffn_Wr': 2.69}
    for name, (base, spread) in spreads.items():
        noise = np.random.default_rng([zlib.crc32(name.encode()), seed]).standard_normal(out[name].shape)
        drawn = base * np.exp(spread * noise) if base else spread * noise
        out[name] = jnp.asarray(drawn.astype(out[name].dtype))
    for name, factor in factors.items():
        out[name] = (out[name] * factor).astype(out[name].dtype)
    return out
```

```python
from contextlib import ExitStack

import numpy as np

import concourse.bass as bass
from concourse import mybir

F32 = mybir.dt.float32
F32R = mybir.dt.float32r
F16 = mybir.dt.float16
ALU = mybir.AluOpType
ACT = mybir.ActivationFunctionType
AX_X = mybir.AxisListType.X

P = 128
C = 64
B, H, W = 16, 16, 16
N = H * W
HALVES = 2
BH = B // HALVES
COLS = BH * N
Q = 512
NQ = COLS // Q
CR = 4
TAPS = 9
E = 8
PAIRS = E // 2
HEADS, KD = 8, 16

PITCH = W + 1
MAP = PITCH * (H + 1)
LEAD = PITCH + 1
FLAT = BH * MAP

VALUE_BITS = 23
STEP = 256.0
SCALE = STEP * 2 ** 20
TOP = STEP * 2 ** VALUE_BITS
QUANT = 0.85
POS = np.float32(QUANT) * np.float32(C * N - 1)
LOW = int(np.floor(POS))
W_HIGH = float(np.float32(POS - np.floor(POS)))
W_LOW = float(np.float32(1) - np.float32(W_HIGH))
RANK = C * N - LOW
GROUP = 8
ACT_COLS = 1024
DVE_COLS = COLS - ACT_COLS


def weight_columns():
    return [
        ("center", P), ("mean", P), ("eps", 4), ("tap_th", 40), ("tp_b1", 1), ("tp_w2", P), ("tp_b2", 1),
        ("sa_b", 1), ("tap_sum", P), ("ca_w1", 8), ("ca_b1", 1), ("ca_w2", P), ("ca_b2", 1),
        ("mask8", 8), ("gt_sel", 8), ("ident", P), ("group", P),
        ("router", E), ("f_wr", E), ("ident2", P), ("sel", HALVES * PAIRS * P), ("w1", PAIRS * P), ("b2", P),
        ("wq", P), ("wv", P), ("bq", Q), ("ones_row", P), ("f_w1", PAIRS * P),
        ("b1", PAIRS), ("expert_rank", E), ("w2", PAIRS * C),
        ("wk", 32), ("bk", 1), ("bv", 1), ("wo", C), ("bo", 1), ("head_mask", P),
        ("bn_g", 2 * PAIRS), ("bn_b", 2 * PAIRS), ("bn_be", 2 * PAIRS), ("bn_m", 2 * PAIRS), ("bn_v", 2 * PAIRS),
        ("f_w2", PAIRS * P), ("f_wo", PAIRS * C), ("f_bo", P), ("f_br", E),
    ]


AT = {}
NCOL = 0
for _name, _n in weight_columns():
    AT[_name] = (NCOL, NCOL + _n)
    NCOL += _n
SPLIT0, SPLIT1 = AT["router"][0], AT["f_w1"][1]
EARLY = SPLIT0


def metaformer_kernel(nc, x_dram, weights_dram, out_dram):
    ctx = ExitStack()
    with ctx:
        def sb(name, shape, dt=F32):
            return ctx.enter_context(nc.sbuf_tensor(name, shape, dt))

        def sem(name):
            return ctx.enter_context(nc.semaphore(name))

        WT = sb("weights", [P, NCOL])

        def w(name, rows=slice(0, P), cols=None):
            a, b = AT[name]
            if cols is not None:
                a, b = a + cols.start, a + cols.stop
            return WT[rows, a:b]

        X = sb("x_resid", [P, COLS])
        XC = sb("x_centered", [P, COLS])
        SQ = sb("x_squared", [P, COLS])
        RS = sb("rstd", [P, COLS])
        T = sb("x_normed", [P, COLS])
        S = sb("x_split", [P, HALVES, COLS], F32R)
        ident_r = sb("ident_r", [P, P], F32R)

        AB = sb("abs_x", [P, COLS])
        QT = sb("abs_by_batch", [P, COLS])
        QX = sb("abs_complement", [P, COLS])
        PADDED = sb("taps_padded", [18, FLAT + 2 * LEAD])
        SHIFTED = sb("taps_shifted", [18, FLAT])
        TH = sb("threshold_hidden", [40, COLS])
        REL = sb("relative_threshold", [P, COLS])
        SW = sb("spatial_weights", [P, COLS])
        U = sb("gated_x", [P, COLS])
        pooled = sb("pooled", [P, BH])
        ca_h = sb("channel_hidden", [8, BH])
        CW = sb("channel_weights", [P, BH])
        thr = sb("threshold", [P, 1])
        thr_half = sb("threshold_less_half_step", [P, 1])
        thr_top = sb("threshold_above", [P, 1])
        step = sb("bit_step", [P, 1])
        bit = sb("bit_stays", [P, 1])
        counts = sb("partial_counts", [P, 2], F16)
        group16 = sb("group_f16", [P, P], F16)
        above = sb("above_max", [P, 1])
        above8 = sb("above_max_spread", [P, 8])
        upper = sb("upper_value", [P, 1])
        flag = sb("upper_is_next", [P, 1])
        gt = sb("quantile", [P, 1])
        gt8 = sb("quantile_spread", [P, BH])
        neg_gt = sb("neg_quantile", [P, BH])

        WH = sb("weights_high", [P, SPLIT1 - SPLIT0], F32R)
        WL = sb("weights_low", [P, SPLIT1 - SPLIT0], F32R)
        router2 = sb("router_parts", [P, 2 * E], F32R)
        f_wr2 = sb("f_router_parts", [P, 2 * E], F32R)

        def part(tile, name, rows=slice(0, P), cols=None):
            a, b = (n - SPLIT0 for n in AT[name])
            if cols is not None:
                a, b = a + cols.start, a + cols.stop
            return tile[rows, a:b]

        TILES = B * N // P
        logits = sb("logits", [P, TILES, E])
        best = sb("best_logit", [P, TILES])
        second = sb("second_logit", [P, TILES])
        is_best = sb("is_best", [P, TILES, E])
        is_second = sb("is_second", [P, TILES, E])
        key = sb("tie_key", [P, TILES, E])
        key_max = sb("tie_key_max", [P, TILES])
        share1 = sb("best_share", [P, TILES])
        share2 = sb("second_share", [P, TILES])
        combine = sb("combine", [P, TILES, E])
        combine2 = sb("combine_parts", [P, TILES, 2, E], F32R)
        CT = sb("combine_rows", [HALVES * 2 * E, COLS], F32R)
        G, HS, H2 = (t[:, :].rearrange("p (g q) -> p g q", g=PAIRS) for t in (QT, U, QX))

        kmax = sb("key_max", [32, BH])
        kbias = sb("key_bias", [32, BH])
        ksum = sb("key_sum", [32, BH])
        krec = sb("key_reciprocal", [32, BH])
        EK = REL[0:32, :]
        QE = sb("queries", [P, 2, Q])
        qmax = sb("query_max", [P, 32])
        qsum = sb("query_sum", [P, 32])
        qrec = sb("query_reciprocal", [P, 32])
        VR = sb("values_by_token", [P, Q])
        EKT = sb("keys_by_token", [P, 64])
        BD = sb("context_blocks", [P, HALVES, P])
        MB = sb("context_out", [P, HALVES, C])
        QS = sb("queries_by_channel", [P, Q])

        bn_a = sb("bn_scale", [P, 2 * PAIRS])
        bn_c = sb("bn_shift", [P, 2 * PAIRS])
        f_logits = sb("f_logits", [P, 2, E])
        f_max = sb("f_max", [P, 2])
        f_sum = sb("f_sum", [P, 2])
        fT = sb("f_weights_rows", [E, N])
        FW = SW[:, 0:PAIRS * N].rearrange("p (g n) -> p g n", g=PAIRS)
        FB = SW[:, PAIRS * N:(PAIRS + 1) * N]
        H1 = G
        HW = HS

        PS = ctx.enter_context(nc.psum_tensor("ps", [P, 8, Q], F32))

        w_in, x_in, late_in = sem("weights_in"), sem("x_in"), sem("late_weights_in")
        xc_ready, xc_copied, sq_ready, var_ready = sem("xc_ready"), sem("xc_copied"), sem("sq_ready"), sem("var_ready")
        ln_taken, rs_ready, t_ready = sem("ln_taken"), sem("rs_ready"), sem("t_ready")
        abs_ready, q_in, rounded_ready = sem("abs_ready"), sem("quantile_in"), sem("rounded_ready")
        half_ready, bit_ready = sem("half_ready"), sem("bit_ready")
        step_ready, group_ready = sem("step_ready"), sem("group_ready")
        padded_zero, taps_ready, taps_out, th_out, shifted_in = sem("padded_zero"), sem("taps_ready"), sem("taps_out"), sem("th_out"), sem("shifted_in")
        rel_ready, rel_out, sw_ready, sw_out = sem("rel_ready"), sem("rel_out"), sem("sw_ready"), sem("sw_out")
        pooled_ready, ca1_ready, ca1_out, ca2_ready, cw_ready = sem("pooled_ready"), sem("ca1_ready"), sem("ca1_out"), sem("ca2_ready"), sem("cw_ready")
        u_ready, comp_ready = sem("u_ready"), sem("complement_ready")
        thr_ready, dve_counted, act_counted, counted = sem("thr_ready"), sem("dve_counted"), sem("act_counted"), sem("counted")
        chain_v, chain_a, chain_g = sem("vector_chain"), sem("scalar_chain"), sem("gpsimd_chain")
        top_ready, top_counted, above_ready, above_spread = sem("top_ready"), sem("top_counted"), sem("above_ready"), sem("above_spread")
        top_summed, gt_ready, gt_spread = sem("top_summed"), sem("gt_ready"), sem("gt_spread")
        split_high, split_low = sem("split_high"), sem("split_low")
        hi_ready, s_ready = sem("hi_ready"), sem("s_ready")
        logits_ready, top_v, exp_ready, combine_ready = sem("logits_ready"), sem("top_chain"), sem("exp_ready"), sem("combine_ready")
        ct_ready, ct_out, x_added = sem("ct_ready"), sem("ct_out"), sem("x_added")
        z_ready, gelu_done, cb_ready = ([sem(f"{n}{p}") for p in range(PAIRS)] for n in ("z_ready", "gelu_done", "cb_ready"))
        hs_ready, w2_done = ([sem(f"{n}{p}") for p in range(PAIRS)] for n in ("hs_ready", "w2_done"))
        y_taken, top_used = sem("y_taken"), sem("top_used")
        kp_ready, kmax_ready, kb_chain, ek_exp, ek_ready = sem("kp_ready"), sem("kmax_ready"), sem("kb_chain"), sem("ek_exp"), sem("ek_ready")
        ekt_ready, ekt_out, q_ready, v_ready, v_out = sem("ekt_ready"), sem("ekt_out"), sem("q_ready"), sem("v_ready"), sem("v_out")
        qmax_ready, qsub_ready, qexp_ready, qsum_ready = sem("qmax_ready"), sem("qsub_ready"), sem("qexp_ready"), sem("qsum_ready")
        qrec_ready, qn_ready, qt_ready, qt_out = sem("qrec_ready"), sem("qn_ready"), sem("qt_ready"), sem("qt_out")
        cx_ready, bd_ready, mb_ready, mb_out, a_ready, x3_ready = (sem(n) for n in ("cx_ready", "bd_ready", "mb_ready", "mb_out", "a_ready", "x3_ready"))
        bn_chain, bn_chain2, bn_rs, fl_ready, fl_chain, fe_ready, fw_ready = (sem(n) for n in ("bn_chain", "bn_chain2", "bn_rs", "fl_ready", "fl_chain", "fe_ready", "fw_ready"))
        ft_ready, ft_out, fb_ready, fb_out, bias_added = (sem(n) for n in ("ft_ready", "ft_out", "fb_ready", "fb_out", "bias_added"))
        z1_ready, h1_ready, z2_ready = ([sem(f"{n}{p}") for p in range(PAIRS)] for n in ("z1_ready", "h1_ready", "z2_ready"))
        h2_ready, hw_ready, wo_done = ([sem(f"{n}{p}") for p in range(PAIRS)] for n in ("h2_ready", "hw_ready", "wo_done"))
        x4_ready = sem("x4_ready")
        diff_ready, mask_ready, gated_ready, x1_ready = sem("diff_ready"), sem("mask_ready"), sem("gated_ready"), sem("x1_ready")
        out_done = sem("out_done")

        def cols(q, n=Q):
            return slice(q * n, (q + 1) * n)

        def maps(ap):
            return ap.rearrange("p (b y x) -> p b y x", b=2, y=H)

        def padded_maps(ap, q):
            return ap[:, 2 * q * MAP:2 * (q + 1) * MAP].rearrange("p (b y x) -> p b y x", b=2, x=PITCH)[:, :, 0:H, 0:W]

        class Chain:

            def __init__(self, eng, s):
                self.eng, self.s, self.n = eng, s, 0

            def __call__(self, ins):
                self.n += 1
                ins.then_inc(self.s, 1)

            def wait(self):
                self.eng.wait_ge(self.s, self.n)

        block = ctx.enter_context(nc.Block())

        def ln_pe_center(pe, n, q, x_wait):
            x_wait(q)
            if 4 * n + q >= 2:
                pe.wait_ge(xc_copied, 4 * n + q - 1)
            pe.matmul(PS[:, q % 2], w("center"), X[:, cols(q)], start=True, stop=True).then_inc(xc_ready, 1)

        def ln_pe_var(pe, n, q):
            pe.wait_ge(sq_ready, 4 * n + q + 1)
            if 4 * n + q >= 2:
                pe.wait_ge(ln_taken, 4 * n + q - 1)
            pe.matmul(PS[:, 2 + q % 2], w("mean"), SQ[:, cols(q)], start=True, stop=True).then_inc(var_ready, 1)

        def ln_pe(pe, n, x_wait):
            for q in range(NQ + 1):
                if q < NQ:
                    ln_pe_center(pe, n, q, x_wait)
                if q >= 1:
                    ln_pe_var(pe, n, q - 1)

        def ln_act_square(act, n, q):
            act.wait_ge(xc_copied, 4 * n + q + 1)
            act.activation(SQ[:, cols(q)], XC[:, cols(q)], ACT.Square).then_inc(sq_ready, 1)

        def ln_act_rstd(act, n, q, eps_col):
            act.wait_ge(var_ready, 4 * n + q + 1)
            if n:
                act.wait_ge(t_ready, 4 * n)
            act.activation(RS[:, cols(q)], PS[:, 2 + q % 2], ACT.Ln, bias=w("eps", cols=slice(eps_col, eps_col + 1))).then_inc(ln_taken, 1)
            act.wait_ge(ln_taken, 4 * n + q + 1)
            act.activation(RS[:, cols(q)], RS[:, cols(q)], ACT.Exp, scale=-0.5).then_inc(rs_ready, 1)

        def ln_act(act, n, eps_col):
            for q in range(NQ + 1):
                if q < NQ:
                    ln_act_square(act, n, q)
                if q >= 1:
                    ln_act_rstd(act, n, q - 1, eps_col)

        def ln_dve_copy(dve, n, q):
            dve.wait_ge(xc_ready, 4 * n + q + 1)
            if n:
                dve.wait_ge(t_ready, 4 * n)
            dve.tensor_copy(XC[:, cols(q)], PS[:, q % 2]).then_inc(xc_copied, 1)

        def ln_dve_scale(dve, n, q, t_free=None):
            dve.wait_ge(rs_ready, 4 * n + q + 1)
            dve.wait_ge(xc_copied, 4 * n + q + 1)
            if t_free:
                t_free(q)
            dve.tensor_tensor(T[:, cols(q)], XC[:, cols(q)], RS[:, cols(q)], ALU.mult).then_inc(t_ready, 1)

        def ln_dve(dve, n, t_free=None):
            for q in range(NQ + 2):
                if q < NQ:
                    ln_dve_copy(dve, n, q)
                if q >= 2:
                    ln_dve_scale(dve, n, q - 2, t_free)

        def split_act(act, n, q, s_free=None):
            act.wait_ge(t_ready, 4 * n + q + 1)
            if s_free:
                s_free()
            act.activation(S[0:C, 0, cols(q)], T[0:C, cols(q)], ACT.Copy).then_inc(hi_ready, 1)
            act.activation(S[C:P, 1, cols(q)], T[C:P, cols(q)], ACT.Copy).then_inc(hi_ready, 1)

        def split_dve(dve, n, q):
            for h, (own, other) in enumerate(((slice(0, C), slice(C, P)), (slice(C, P), slice(0, C)))):
                dve.wait_ge(hi_ready, 8 * (n - 1) + 2 * q + h + 1)
                dve.tensor_tensor(S[other, h, cols(q)], T[own, cols(q)], S[own, h, cols(q)].bitcast(F32),
                                  ALU.subtract).then_inc(s_ready, 1)

        def ln_split_act(act, n, eps_col, s_free=None):
            for q in range(NQ + 2):
                if q < NQ:
                    ln_act_square(act, n, q)
                if 1 <= q <= NQ:
                    ln_act_rstd(act, n, q - 1, eps_col)
                if q >= 2:
                    split_act(act, n, q - 2, s_free)

        def ln_split_dve(dve, n, t_free=None):
            for q in range(NQ + 3):
                if q < NQ:
                    ln_dve_copy(dve, n, q)
                if 2 <= q < NQ + 2:
                    ln_dve_scale(dve, n, q - 2, t_free)
                if q >= 3:
                    split_dve(dve, n, q - 3)

        def pair(name, p, tile=None, n=P):
            c = slice(p * n, (p + 1) * n)
            return w(name, cols=c) if tile is None else part(tile, name, cols=c)

        def two_pass(pe, out, name, p, rhs, start=True, stop=True):
            pe.matmul(out, pair(name, p, WH), rhs, start=start, stop=False)
            return pe.matmul(out, pair(name, p, WL), rhs, start=False, stop=stop)

        def after(eng, i):
            return i + 1 if isinstance(i, int) else eng.snap(i + 1)

        def it_values(eng, i):
            i = i if isinstance(i, int) else eng.snap(i)
            return i, after(eng, i)

        def wait_last(eng, s, n):
            if not (isinstance(n, int) and n == 0):
                eng.wait_ge(s, n)

        @block.sync
        def _(sp):
            x_v = x_dram.rearrange("(h b) c y x -> h c b (y x)", h=HALVES)
            for h in range(HALVES):
                sp.dma_start(X[h * C:(h + 1) * C, :].rearrange("c (b n) -> c b n", b=BH), x_v[h]).then_inc(x_in, 16)
            sp.dma_start(WT[:, 0:EARLY], weights_dram[:, 0:EARLY]).then_inc(w_in, 16)
            sp.dma_start(WT[:, EARLY:NCOL], weights_dram[:, EARLY:NCOL]).then_inc(late_in, 16)
            sp.wait_ge(abs_ready, NQ)
            for h in range(HALVES):
                for b in range(BH):
                    g = h * C + b * GROUP
                    sp.dma_start(QT[g:g + GROUP, :].rearrange("j (c n) -> j c n", c=C // GROUP),
                                 AB[h * C:(h + 1) * C, b * N:(b + 1) * N]
                                 ).then_inc(q_in, 16)
            sp.wait_ge(taps_out, NQ)
            for dy in range(3):
                for dx in range(3):
                    tap = 3 * dy + dx
                    off = LEAD + (dy - 1) * PITCH + dx - 1
                    sp.dma_start(SHIFTED[tap:18:TAPS, :], PADDED[tap:18:TAPS, off:off + FLAT]).then_inc(shifted_in, 16)
            o_v = out_dram.rearrange("(h b) c y x -> h b c (y x)", h=HALVES)
            with sp.Fori(0, BH) as b0:
                b = sp.snap(b0)
                sp.wait_ge(x4_ready, b + 1)
                for h in range(HALVES):
                    sp.dma_start(o_v[h, bass.ds(b, 1)].rearrange("b c n -> (b c) n"), X[h * C:(h + 1) * C, bass.ds(b * N, N)]).then_inc(out_done, 16)
            sp.wait_ge(out_done, 16 * B)

        @block.tensor
        def _(pe):
            pe.wait_ge(w_in, 16)
            ln_pe(pe, 0, lambda q: pe.wait_ge(x_in, 32))
            for q in range(NQ):
                pe.wait_ge(t_ready, q + 1)
                if q >= 2:
                    pe.wait_ge(th_out, q - 1)
                    pe.wait_ge(taps_out, q - 1)
                pe.matmul(PS[0:40, 4 + q % 2], w("tap_th"), T[:, cols(q)], start=True, stop=True).then_inc(taps_ready, 1)
                pe.wait_ge(th_out, q + 1)
                if q >= 2:
                    pe.wait_ge(rel_out, q - 1)
                pe.matmul(PS[:, 6 + q % 2], w("tp_w2", slice(32, 40)), TH[32:40, cols(q)], start=True, stop=True).then_inc(rel_ready, 1)
            pe.wait_ge(pooled_ready, 1)
            pe.wait_ge(xc_copied, NQ)
            pe.matmul(PS[0:8, 0, 0:BH], w("ca_w1"), pooled[:, :], start=True, stop=True).then_inc(ca1_ready, 1)
            pe.wait_ge(ca1_out, 1)
            pe.matmul(PS[:, 1, 0:BH], w("ca_w2", slice(0, 8)), ca_h[:, :], start=True, stop=True).then_inc(ca2_ready, 1)
            for q in range(NQ):
                pe.wait_ge(shifted_in, 16 * TAPS)
                bank = 4 + q % 4
                if bank < 6:
                    pe.wait_ge(th_out, NQ)
                    pe.wait_ge(taps_out, NQ)
                else:
                    pe.wait_ge(rel_out, NQ)
                pe.matmul(maps(PS[:, bank]), w("tap_sum", slice(0, 18)), padded_maps(SHIFTED, q),
                          start=True, stop=True).then_inc(sw_ready, 1)
            def sum_counts(r):
                pe.wait_ge(dve_counted, r + 1)
                pe.wait_ge(act_counted, r + 1)
                pe.matmul(PS[:, 0, 0:2], group16[:, :], counts[:, :], start=True, stop=True).then_inc(counted, 1)

            pe.wait_ge(group_ready, 1)
            with pe.Fori(0, VALUE_BITS) as r:
                sum_counts(pe.snap(r))
            pe.wait_ge(above_ready, 1)
            pe.wait_ge(cw_ready, 1)
            pe.matmul(PS[:, 1, 0:8], w("group"), above8[:, :], start=True, stop=True).then_inc(above_spread, 1)
            pe.wait_ge(top_counted, 1)
            pe.wait_ge(thr_ready, VALUE_BITS + 1)
            pe.matmul(PS[:, 0, 0:2], group16[:, :], counts[:, :], start=True, stop=True).then_inc(top_summed, 1)
            pe.wait_ge(gt_ready, 1)
            pe.matmul(PS[:, 2, 0:BH], w("mean"), gt8[:, :], start=True, stop=True).then_inc(gt_spread, 1)

            pe.wait_ge(top_used, 1)
            ln_pe(pe, 1, lambda q: pe.wait_ge(x1_ready, q + 1))
            pe.wait_ge(split_low, 2)
            pe.wait_ge(sw_out, NQ)
            for j in range(TILES // 2):
                if j % 4 == 0:
                    pe.wait_ge(s_ready, 2 * (j // 4) + 2)
                for h in range(HALVES):
                    t = 2 * j + h
                    last = pe.matmul(PS[:, 4, 16 * t:16 * t + 16], S[:, h, cols(j, P)], router2[:, :], start=True, stop=True)
            last.then_inc(logits_ready, 1)
            pe.wait_ge(combine_ready, 2)
            for q in range(NQ):
                for j in range(4 * q, 4 * q + 4):
                    last = pe.transpose(PS[0:32, 4 + q, cols(j % 4, P)], combine2[:, 2 * j:2 * j + 2].rearrange("p t s e -> p (t s e)").bitcast(F32), w("ident"))
                last.then_inc(ct_ready, 1)

            def up(n_sem, it, n1, p, name, prior):
                wait_last(pe, prior[(p + 2) % PAIRS], it if p < 2 else n1)
                two_pass(pe, PS[:, p % 2], name, p, S[:, :, bass.ds(it * N, N)]).then_inc(n_sem[p], 1)

            def moe_up(it, n1, p):
                wait_last(pe, hs_ready[(p + 2) % PAIRS], it if p < 2 else n1)
                up(z_ready, it, n1, p, "w1", gelu_done)
                for h in range(HALVES):
                    last = pe.matmul(PS[:, 2 + p % 2, cols(h, N)], part(WH, "sel", slice(0, 32), cols(h * PAIRS + p, P)),
                                     CT[:, bass.ds(it * N, N)], start=True, stop=True)
                last.then_inc(cb_ready[p], 1)

            def moe_down(it, n1, p):
                if p == 0:
                    wait_last(pe, y_taken, it)
                pe.wait_ge(hs_ready[p], n1)
                for h in range(HALVES):
                    last = pe.matmul(PS[h * C:(h + 1) * C, 4, 0:N], pair("w2", p, n=C), HS[:, p, cols(h, N)], start=p == 0, stop=p == PAIRS - 1)
                if p == 0:
                    pe.matmul(PS[:, 4, 0:N], part(WH, "b2", slice(0, 32)), CT[:, bass.ds(it * N, N)], start=False, stop=False)
                    last = pe.matmul(PS[:, 4, 0:N], part(WL, "b2", slice(0, 32)), CT[:, bass.ds(it * N, N)], start=False, stop=False)
                last.then_inc(w2_done[p], 1)

            def moe_body(i, last=False):
                it, n1 = it_values(pe, i)
                n2 = None if last else after(pe, n1)
                moe_up(it, n1, 2)
                moe_down(it, n1, 0)
                moe_up(it, n1, 3)
                moe_down(it, n1, 1)
                if not last:
                    moe_up(n1, n2, 0)
                moe_down(it, n1, 2)
                if not last:
                    moe_up(n1, n2, 1)
                moe_down(it, n1, 3)

            pe.wait_ge(ct_out, NQ)
            pe.wait_ge(ln_taken, 2 * NQ)
            pe.wait_ge(xc_copied, 2 * NQ)
            moe_up(0, 1, 0)
            moe_up(0, 1, 1)
            moe_body(0)
            with pe.Fori(1, BH - 1) as i:
                moe_body(i)
            moe_body(BH - 1, last=True)

            for p in (2, 3):
                pe.wait_ge(gelu_done[p], BH)
                pe.wait_ge(hs_ready[p], BH)
            ln_pe(pe, 2, lambda q: pe.wait_ge(y_taken, 2 * q + 2))
            for q in range(NQ):
                pe.wait_ge(t_ready, 2 * NQ + q + 1)
                if q >= 2:
                    pe.wait_ge(ek_exp, 2 * (q - 1))
                pe.matmul(PS[0:32, 6 + q % 2], w("wk"), T[:, cols(q)], start=True, stop=True).then_inc(kp_ready, 1)

            SM = 4

            def attn_project(it):
                sm = SM + it % 2
                pe.wait_ge(ek_ready, 1)
                if it >= 2:
                    pe.wait_ge(mb_out, it - 1)
                for jj in range(2):
                    last = pe.transpose(PS[:, sm, 32 * jj:32 * jj + 32], EK[:, cols(2 * it + jj, P)], w("ident", slice(0, 32), slice(0, 32)))
                last.then_inc(ekt_ready, 1)
                pe.wait_ge(s_ready, 2 * NQ + 2 * (it // 2) + 2)
                if it >= 2:
                    pe.wait_ge(qsub_ready, it - 1)
                qb = it % 2
                pe.matmul(PS[:, qb], part(WH, "ones_row", slice(0, 1)), part(WH, "bq", slice(0, 1)), start=True, stop=False)
                pe.matmul(PS[:, qb], part(WH, "ones_row", slice(0, 1)), part(WL, "bq", slice(0, 1)), start=False, stop=False)
                for t in range(4):
                    s_t = S[:, t // 2, cols(2 * it + t % 2, P)]
                    pe.matmul(PS[:, qb, cols(t, P)], s_t, part(WH, "wq"), start=False, stop=False)
                    last = pe.matmul(PS[:, qb, cols(t, P)], s_t, part(WL, "wq"), start=False, stop=t == 3)
                last.then_inc(q_ready, 1)
                if it >= 1:
                    pe.wait_ge(v_out, it)
                for t in range(4):
                    s_t = S[:, t // 2, cols(2 * it + t % 2, P)]
                    pe.matmul(PS[:, 2, cols(t, P)], s_t, part(WH, "wv"), start=True, stop=False)
                    last = pe.matmul(PS[:, 2, cols(t, P)], s_t, part(WL, "wv"), start=False, stop=True)
                last.then_inc(v_ready, 1)

            def attn_context(it):
                sm = SM + it % 2
                pe.wait_ge(v_out, it + 1)
                pe.wait_ge(ekt_out, it + 1)
                for h in range(HALVES):
                    for jj in range(2):
                        last = pe.matmul(PS[:, sm, 64 + 16 * h:80 + 16 * h], VR[:, cols(2 * h + jj, P)], EKT[:, 32 * jj + 16 * h:32 * jj + 16 * h + 16],
                                         start=jj == 0, stop=jj == 1)
                last.then_inc(cx_ready, 1)

            def attn_out(it):
                sm = SM + it % 2
                pe.wait_ge(bd_ready, 2 * it + 2)
                for h in range(HALVES):
                    last = pe.matmul(PS[:, sm, 128 + C * h:128 + C * (h + 1)], BD[:, h], w("wo"), start=True, stop=True)
                last.then_inc(mb_ready, 1)
                pe.wait_ge(qn_ready, it + 1)
                if it >= 1:
                    pe.wait_ge(qt_out, it)
                for t in range(4):
                    last = pe.transpose(PS[:, 3, cols(t, P)], QE[:, it % 2, cols(t, P)], w("ident"))
                last.then_inc(qt_ready, 1)
                pe.wait_ge(qt_out, it + 1)
                pe.wait_ge(mb_out, it + 1)
                if it >= 1:
                    pe.wait_ge(x3_ready, it)
                for h in range(HALVES):
                    last = pe.matmul(PS[h * C:(h + 1) * C, 6, 0:N], MB[:, h], QS[:, cols(h, N)], start=True, stop=True)
                last.then_inc(a_ready, 1)

            pe.wait_ge(ln_taken, 3 * NQ)
            pe.wait_ge(xc_copied, 3 * NQ)
            pe.wait_ge(ek_exp, BH)
            attn_project(0)
            for it in range(BH):
                if it + 1 < BH:
                    attn_project(it + 1)
                attn_context(it)
                attn_out(it)

            pe.wait_ge(qsub_ready, BH)
            pe.wait_ge(v_out, BH)
            pe.wait_ge(qt_out, BH)
            ln_pe(pe, 3, lambda q: pe.wait_ge(x3_ready, 2 * q + 2))
            pe.wait_ge(mb_out, BH)
            for jj in range(2):
                for b in range(BH):
                    pe.wait_ge(s_ready, 4 * NQ + 2 * (b // 2) + 2)
                    for h in range(HALVES):
                        last = pe.matmul(PS[:, 4, 16 * jj:16 * jj + 16], S[:, h, cols(2 * b + jj, P)], f_wr2[:, :],
                                         start=b == 0 and h == 0, stop=b == BH - 1 and h == 1)
            last.then_inc(fl_ready, 1)
            pe.wait_ge(fw_ready, 1)
            for jj in range(2):
                last = pe.transpose(PS[0:E, 5, cols(jj, P)], f_logits[:, jj], w("ident"))
            last.then_inc(ft_ready, 1)
            pe.wait_ge(ft_out, 1)
            for p in range(PAIRS):
                pe.matmul(PS[:, 6 + p // 2, cols(p % 2, N)], w("sel", slice(0, E), cols(p, P)), fT[:, :], start=True, stop=True).then_inc(fb_ready, 1)
            pe.wait_ge(fl_chain, 1)
            pe.matmul(PS[:, 4, 0:N], w("f_bo", slice(0, E)), fT[:, :], start=True, stop=True).then_inc(fb_ready, 1)

            def f_up(it, n1, p):
                up(z1_ready, it, n1, p, "f_w1", h1_ready)

            def f_mid(it, n1, p):
                pe.wait_ge(h1_ready[p], n1)
                wait_last(pe, h2_ready[(p + 2) % PAIRS], it if p < 2 else n1)
                pe.matmul(PS[:, 2 + p % 2], pair("f_w2", p), H1[:, p], start=True, stop=True).then_inc(z2_ready[p], 1)

            def f_down(it, n1, p):
                if p == 0:
                    wait_last(pe, x4_ready, it)
                pe.wait_ge(hw_ready[p], n1)
                for h in range(HALVES):
                    last = pe.matmul(PS[h * C:(h + 1) * C, 4, 0:N], pair("f_wo", p, n=C), HW[:, p, cols(h, N)], start=p == 0, stop=p == PAIRS - 1)
                last.then_inc(wo_done[p], 1)

            def f_body(i, last=False):
                it, n1 = it_values(pe, i)
                n2 = None if last else after(pe, n1)
                f_up(it, n1, 2)
                f_mid(it, n1, 1)
                f_down(it, n1, 0)
                f_up(it, n1, 3)
                f_mid(it, n1, 2)
                f_down(it, n1, 1)
                if not last:
                    f_up(n1, n2, 0)
                f_mid(it, n1, 3)
                f_down(it, n1, 2)
                if not last:
                    f_up(n1, n2, 1)
                    f_mid(n1, n2, 0)
                f_down(it, n1, 3)

            pe.wait_ge(ln_taken, 4 * NQ)
            pe.wait_ge(xc_copied, 4 * NQ)
            pe.wait_ge(fb_out, PAIRS + 1)
            f_up(0, 1, 0)
            f_up(0, 1, 1)
            f_mid(0, 1, 0)
            f_body(0)
            with pe.Fori(1, BH - 1) as i:
                f_body(i)
            f_body(BH - 1, last=True)

        @block.scalar
        def _(act):
            act.preload_act_table_set("natural_log_exp_and_others")
            act.wait_ge(w_in, 16)
            ln_act(act, 0, 0)
            for q in range(NQ):
                act.wait_ge(t_ready, q + 1)
                act.activation(AB[:, cols(q)], T[:, cols(q)], ACT.Abs, scale=SCALE).then_inc(abs_ready, 1)
            act.wait_ge(padded_zero, 1)
            for q in range(NQ):
                act.wait_ge(taps_ready, q + 1)
                act.activation(TH[32:40, cols(q)], PS[32:40, 4 + q % 2], ACT.Relu, bias=w("tp_b1", slice(32, 40))).then_inc(th_out, 1)
                act.activation(padded_maps(PADDED[:, LEAD:LEAD + FLAT], q), maps(PS[0:18, 4 + q % 2]), ACT.Copy).then_inc(taps_out, 1)
                act.wait_ge(rel_ready, q + 1)
                act.activation(REL[:, cols(q)], PS[:, 6 + q % 2], ACT.Sigmoid, bias=w("tp_b2")).then_inc(rel_out, 1)
            act.wait_ge(ca1_ready, 1)
            act.activation(ca_h[:, :], PS[0:8, 0, 0:BH], ACT.Relu, bias=w("ca_b1", slice(0, 8)), scale=1.0 / N).then_inc(ca1_out, 1)
            act.wait_ge(ca2_ready, 1)
            act.activation(CW[:, :], PS[:, 1, 0:BH], ACT.Sigmoid, bias=w("ca_b2")).then_inc(cw_ready, 1)
            for q in range(NQ):
                act.wait_ge(sw_ready, q + 1)
                act.activation(SW[:, cols(q)], PS[:, 4 + q % 4], ACT.Sigmoid, bias=w("sa_b")).then_inc(sw_out, 1)
            act.wait_ge(rounded_ready, 1)
            act.wait_ge(var_ready, NQ)
            with act.Fori(0, VALUE_BITS) as r0:
                r = act.snap(r0)
                act.wait_ge(thr_ready, r + 1)
                with nc.allow_low_precision(reason="whole numbers up to 2048"):
                    act.activation(SQ[:, 0:ACT_COLS], QT[:, DVE_COLS:COLS], ACT.Sigmoid, bias=thr[:, 0:1], scale=-1.0,
                                   accum_out=counts[:, 1:2]).then_inc(act_counted, 1)
            act.wait_ge(top_ready, 1)
            with nc.allow_low_precision(reason="whole numbers up to 2048"):
                act.activation(SQ[:, :], QT[:, :], ACT.Sigmoid, bias=thr_top[:, 0:1], scale=-1.0,
                               accum_out=counts[:, 1:2]).then_inc(top_counted, 1)
            for q in range(NQ):
                act.wait_ge(diff_ready, 2 * q + 2)
                act.activation(AB[:, cols(q)], AB[:, cols(q)], ACT.Sigmoid, scale=10.0 / SCALE).then_inc(mask_ready, 1)

            act.preload_act_table_set("natural_log_exp_and_others")
            act.wait_ge(top_counted, 1)
            ln_split_act(act, 1, 1)
            act.wait_ge(top_v, 13)
            act.activation(share2[:, :], second[:, :], ACT.Exp).then_inc(exp_ready, 1)
            for q in range(1, NQ, 2):
                act.wait_ge(ct_ready, q + 1)
                act.activation(CT[:, cols(q)], PS[0:32, 4 + q], ACT.Copy).then_inc(ct_out, 1)
            act.preload_act_table(ACT.Gelu)

            def moe_gelu(i):
                it, n1 = it_values(act, i)
                for p in range(PAIRS):
                    act.wait_ge(z_ready[p], n1)
                    wait_last(act, hs_ready[p], it)
                    act.activation(G[:, p], PS[:, p % 2], ACT.Gelu, bias=w("b1", cols=slice(p, p + 1))).then_inc(gelu_done[p], 1)

            moe_gelu(0)
            with act.Fori(1, BH) as i:
                moe_gelu(i)

            act.preload_act_table_set("natural_log_exp_and_others")
            for p in range(PAIRS):
                act.wait_ge(z_ready[p], BH)
            for q in range(NQ + 3):
                if q < NQ:
                    ln_act_square(act, 2, q)
                if 1 <= q <= NQ:
                    ln_act_rstd(act, 2, q - 1, 0)
                if 2 <= q < NQ + 2:
                    split_act(act, 2, q - 2)
                if q >= 3:
                    for b in (2 * (q - 3), 2 * (q - 3) + 1):
                        act.wait_ge(kb_chain, 2 * (q - 3) + 2)
                        act.activation(EK[:, cols(b, N)], PS[0:32, 6 + (q - 3) % 2, cols(b % 2, N)], ACT.Exp, bias=kbias[:, b:b + 1],
                                       accum_out=ksum[:, b:b + 1]).then_inc(ek_exp, 1)
            def values_out(it):
                act.wait_ge(v_ready, it + 1)
                if it >= 1:
                    act.wait_ge(cx_ready, it)
                act.activation(VR[:, :], PS[:, 2], ACT.Copy).then_inc(v_out, 1)

            values_out(0)
            for it in range(BH):
                act.wait_ge(qsub_ready, it + 1)
                act.activation(QE[:, it % 2], QE[:, it % 2], ACT.Exp).then_inc(qexp_ready, 1)
                act.wait_ge(mb_ready, it + 1)
                if it >= 1:
                    act.wait_ge(a_ready, it)
                act.activation(MB[:, :], PS[:, 4 + it % 2, 128:128 + HALVES * C].rearrange("p (h c) -> p h c", h=HALVES), ACT.Copy).then_inc(mb_out, 1)
                if it + 1 < BH:
                    values_out(it + 1)
                act.wait_ge(qt_ready, it + 1)
                act.activation(QS[:, :], PS[:, 3], ACT.Copy).then_inc(qt_out, 1)

            act.wait_ge(late_in, 16)
            act.activation(bn_a[:, :], w("bn_v"), ACT.Ln, bias=w("eps", cols=slice(2, 3))).then_inc(bn_rs, 1)
            act.wait_ge(bn_rs, 1)
            act.activation(bn_a[:, :], bn_a[:, :], ACT.Exp, scale=-0.5).then_inc(bn_rs, 1)
            ln_split_act(act, 3, 1, lambda: act.wait_ge(v_ready, BH))
            act.wait_ge(fl_chain, 5)
            act.activation(f_logits[:, :], f_logits[:, :], ACT.Exp).then_inc(fe_ready, 1)
            act.wait_ge(ft_ready, 1)
            act.activation(fT[:, :], PS[0:E, 5, 0:N], ACT.Copy).then_inc(ft_out, 1)
            for p in range(PAIRS):
                act.wait_ge(fb_ready, p + 1)
                if p % 2 == 0:
                    act.wait_ge(fb_ready, p + 2)
                act.activation(FW[:, p], PS[:, 6 + p // 2, cols(p % 2, N)], ACT.Copy).then_inc(fb_out, 1)
            act.wait_ge(fb_ready, PAIRS + 1)
            act.activation(FB[:, :], PS[:, 4, 0:N], ACT.Copy).then_inc(fb_out, 1)

            def bn_relu(out, bank, p, layer):
                n = layer * PAIRS + p
                return act.activation(out, PS[:, bank + p % 2], ACT.Relu, bias=bn_c[:, n:n + 1], scale=bn_a[:, n:n + 1])

            def f_h1(it, n1, p):
                act.wait_ge(z1_ready[p], n1)
                wait_last(act, z2_ready[p], it)
                bn_relu(H1[:, p], 0, p, 0).then_inc(h1_ready[p], 1)

            def f_h2(it, n1, p):
                act.wait_ge(z2_ready[p], n1)
                wait_last(act, hw_ready[p], it)
                bn_relu(H2[:, p], 2, p, 1).then_inc(h2_ready[p], 1)

            def f_act_body(i, last=False):
                it, n1 = it_values(act, i)
                f_h1(it, n1, 2)
                f_h2(it, n1, 1)
                f_h1(it, n1, 3)
                f_h2(it, n1, 2)
                n2 = None if last else after(act, n1)
                if not last:
                    f_h1(n1, n2, 0)
                f_h2(it, n1, 3)
                if not last:
                    f_h1(n1, n2, 1)
                    f_h2(n1, n2, 0)

            act.wait_ge(bn_chain, 3)
            act.wait_ge(hs_ready[3], BH)
            f_h1(0, 1, 0)
            f_h1(0, 1, 1)
            f_h2(0, 1, 0)
            f_act_body(0)
            with act.Fori(1, BH - 1) as i:
                f_act_body(i)
            f_act_body(BH - 1, last=True)

        @block.vector
        def _(dve):
            chain = Chain(dve, chain_v)
            dve.wait_ge(w_in, 16)
            ln_dve(dve, 0)
            dve.wait_ge(t_ready, NQ)
            dve.tensor_reduce(pooled[:, :], T[:, :].rearrange("p (b n) -> p b n", b=BH), AX_X, ALU.add).then_inc(pooled_ready, 1)
            dve.wait_ge(q_in, 16 * B)
            dve.tensor_scalar(QT[:, :], QT[:, :], TOP, TOP, ALU.add, ALU.subtract).then_inc(rounded_ready, 1)
            dve.memset(step[:, :], TOP).then_inc(chain_v, 1)
            dve.wait_ge(chain_v, 1)
            dve.memset(thr[:, :], TOP / 2 - STEP / 2).then_inc(thr_ready, 1)
            dve.tensor_copy(group16[:, :], w("group")).then_inc(group_ready, 1)
            dve.wait_ge(rounded_ready, 1)
            dve.wait_ge(xc_copied, NQ)

            def count_below(n):
                dve.wait_ge(thr_ready, n)
                with nc.allow_low_precision(reason="whole numbers up to 2048"):
                    dve.tensor_scalar(XC[:, 0:DVE_COLS], QT[:, 0:DVE_COLS], thr[:, 0:1], None, ALU.is_lt, ALU.add,
                                      accum_out=counts[:, 0:1]).then_inc(dve_counted, 1)
                dve.tensor_scalar(step[:, :], step[:, :], 0.5, None, ALU.mult).then_inc(step_ready, 1)
                dve.wait_ge(step_ready, n)
                dve.scalar_tensor_tensor(thr_half[:, :], step[:, :], -0.5, thr[:, :], ALU.mult, ALU.add).then_inc(half_ready, 1)

            def set_bit(n):
                dve.wait_ge(counted, n)
                dve.tensor_scalar(bit[:, :], PS[:, 0, 0:1], PS[:, 0, 1:2], C * N - RANK + 0.5, ALU.add, ALU.is_lt).then_inc(bit_ready, 1)
                dve.wait_ge(bit_ready, n)
                dve.wait_ge(half_ready, n)
                dve.scalar_tensor_tensor(thr[:, :], bit[:, :], step[:, 0:1], thr_half[:, :], ALU.mult, ALU.add).then_inc(thr_ready, 1)

            count_below(1)
            with dve.Fori(1, VALUE_BITS) as r0:
                r = dve.snap(r0)
                set_bit(r)
                count_below(dve.snap(r + 1))
            set_bit(VALUE_BITS)
            dve.wait_ge(thr_ready, VALUE_BITS + 1)
            dve.tensor_scalar(thr_top[:, :], thr[:, :], STEP / 2, None, ALU.add).then_inc(top_ready, 1)
            dve.tensor_scalar(XC[:, :], QT[:, :], thr[:, 0:1], None, ALU.is_gt).then_inc(chain_v, 1)
            dve.wait_ge(chain_v, 2)
            dve.wait_ge(comp_ready, 1)
            dve.tensor_tensor_reduce(out=XC[:, :], in0=XC[:, :], in1=QX[:, :], scale=1.0, scalar=0.0, op0=ALU.mult, op1=ALU.max,
                                     accum_out=above[:, :]).then_inc(chain_v, 1)
            dve.wait_ge(chain_v, 3)
            dve.tensor_scalar(above8[:, :], w("mask8"), above[:, 0:1], None, ALU.mult).then_inc(above_ready, 1)
            dve.wait_ge(above_spread, 1)
            dve.reduce_max(above[:, :], PS[:, 1, 0:8], AX_X).then_inc(chain_v, 1)
            dve.wait_ge(chain_v, 4)
            dve.tensor_scalar(upper[:, :], above[:, :], -1.0, TOP, ALU.mult, ALU.add).then_inc(chain_v, 1)
            dve.wait_ge(top_summed, 1)
            dve.tensor_scalar(flag[:, :], PS[:, 0, 1:2], C * N - RANK + 1.5, None, ALU.is_lt).then_inc(chain_v, 1)
            dve.wait_ge(chain_v, 6)
            dve.tensor_tensor(upper[:, :], upper[:, :], thr[:, :], ALU.subtract).then_inc(chain_v, 1)
            dve.wait_ge(chain_v, 7)
            dve.scalar_tensor_tensor(upper[:, :], upper[:, :], flag[:, 0:1], thr[:, :], ALU.mult, ALU.add).then_inc(chain_v, 1)
            dve.tensor_scalar(gt[:, :], thr[:, :], W_LOW, None, ALU.mult).then_inc(chain_v, 1)
            dve.wait_ge(chain_v, 9)
            dve.scalar_tensor_tensor(gt[:, :], upper[:, :], W_HIGH, gt[:, :], ALU.mult, ALU.add).then_inc(chain_v, 1)
            dve.wait_ge(chain_v, 10)
            dve.tensor_scalar(gt8[:, :], w("gt_sel"), gt[:, 0:1], None, ALU.mult).then_inc(gt_ready, 1)
            dve.wait_ge(gt_spread, 1)
            dve.tensor_scalar(neg_gt[:, :], PS[:, 2, 0:BH], -1.0, None, ALU.mult).then_inc(top_used, 1)
            dve.wait_ge(top_used, 1)
            dve.wait_ge(rel_out, NQ)
            dve.wait_ge(q_in, 16 * B)
            for b in range(BH):
                c = cols(b, N)
                dve.scalar_tensor_tensor(AB[:, c], REL[:, c], neg_gt[:, b:b + 1], AB[:, c], ALU.mult, ALU.add).then_inc(diff_ready, 1)
            dve.wait_ge(u_ready, NQ)
            for q in range(NQ):
                dve.wait_ge(mask_ready, q + 1)
                dve.tensor_tensor(U[:, cols(q)], U[:, cols(q)], AB[:, cols(q)], ALU.mult).then_inc(gated_ready, 1)

            ln_split_dve(dve, 1)
            dve.wait_ge(logits_ready, 1)
            top = Chain(dve, top_v)

            def by_token(ap, n=E):
                return ap[:, :].unsqueeze(2).to_broadcast([P, TILES, n])

            rank = w("expert_rank").unsqueeze(1).to_broadcast([P, TILES, E])
            top(dve.tensor_reduce(logits[:, :, :], PS[:, 4].rearrange("p (t s e) -> p t e s", s=2, e=E), AX_X, ALU.add))
            for n, (m, chosen) in enumerate(((best, is_best), (second, is_second))):
                top.wait()
                top(dve.reduce_max(m[:, :], logits[:, :, :], AX_X))
                top.wait()
                top(dve.tensor_tensor(key[:, :, :], logits[:, :, :], by_token(m), ALU.is_equal))
                top.wait()
                top(dve.tensor_tensor(key[:, :, :], key[:, :, :], rank, ALU.mult))
                top.wait()
                top(dve.reduce_max(key_max[:, :], key[:, :, :], AX_X))
                top.wait()
                top(dve.tensor_tensor(chosen[:, :, :], by_token(key_max), rank, ALU.is_equal))
                top.wait()
                if n == 0:
                    top(dve.scalar_tensor_tensor(logits[:, :, :], chosen[:, :, :], -1e30, logits[:, :, :], ALU.mult, ALU.add))
            top(dve.tensor_tensor(second[:, :], second[:, :], best[:, :], ALU.subtract))
            assert top.n == 13
            dve.wait_ge(exp_ready, 1)
            top(dve.tensor_scalar(share1[:, :], share2[:, :], 1.0, None, ALU.add))
            top.wait()
            top(dve.reciprocal(share1[:, :], share1[:, :]))
            top.wait()
            top(dve.tensor_tensor(share2[:, :], share2[:, :], share1[:, :], ALU.mult))
            top(dve.tensor_tensor(combine[:, :, :], is_best[:, :, :], by_token(share1), ALU.mult))
            top.wait()
            top(dve.tensor_tensor(is_second[:, :, :], is_second[:, :, :], by_token(share2), ALU.mult))
            top.wait()
            top(dve.tensor_tensor(combine[:, :, :], combine[:, :, :], is_second[:, :, :], ALU.add))
            top.wait()
            dve.tensor_copy(combine2[:, :, 0], combine[:, :, :]).then_inc(combine_ready, 1)
            dve.wait_ge(combine_ready, 1)
            dve.tensor_tensor(combine2[:, :, 1], combine[:, :, :], combine2[:, :, 0].bitcast(F32), ALU.subtract).then_inc(combine_ready, 1)
            for q in range(0, NQ, 2):
                dve.wait_ge(ct_ready, q + 1)
                dve.tensor_copy(CT[:, cols(q)], PS[0:32, 4 + q]).then_inc(ct_out, 1)

            def moe_scale(it, n1, p):
                dve.wait_ge(gelu_done[p], n1)
                dve.wait_ge(cb_ready[p], n1)
                wait_last(dve, w2_done[p], it)
                dve.tensor_tensor(HS[:, p], G[:, p], PS[:, 2 + p % 2], ALU.mult).then_inc(hs_ready[p], 1)

            def moe_add(it, n1):
                dve.wait_ge(w2_done[PAIRS - 1], n1)
                x_it = X[:, bass.ds(it * N, N)]
                dve.tensor_tensor(x_it, PS[:, 4, 0:N], x_it, ALU.add).then_inc(y_taken, 1)

            dve.wait_ge(x_added, NQ)
            for p in range(PAIRS):
                moe_scale(0, 1, p)
            with dve.Fori(1, BH) as i:
                it, n1 = it_values(dve, i)
                moe_scale(it, n1, 0)
                moe_scale(it, n1, 1)
                moe_add(dve.snap(it - 1), it)
                moe_scale(it, n1, 2)
                moe_scale(it, n1, 3)
            moe_add(BH - 1, BH)

            for q in range(NQ + 4):
                if q < NQ:
                    ln_dve_copy(dve, 2, q)
                if 2 <= q < NQ + 2:
                    ln_dve_scale(dve, 2, q - 2, lambda _: dve.wait_ge(x_added, NQ))
                if 3 <= q < NQ + 3:
                    split_dve(dve, 2, q - 3)
                if q >= 3 and q - 3 < NQ:
                    r = q - 3
                    dve.wait_ge(kp_ready, r + 1)
                    dve.reduce_max(kmax[:, 2 * r:2 * r + 2], PS[0:32, 6 + r % 2].rearrange("p (b n) -> p b n", b=2), AX_X).then_inc(kmax_ready, 1)
                    dve.wait_ge(kmax_ready, r + 1)
                    dve.tensor_scalar(kmax[:, 2 * r:2 * r + 2], kmax[:, 2 * r:2 * r + 2], w("bk", slice(0, 32)), None, ALU.add).then_inc(kb_chain, 1)
                    dve.wait_ge(kb_chain, 2 * r + 1)
                    dve.tensor_scalar(kbias[:, 2 * r:2 * r + 2], kmax[:, 2 * r:2 * r + 2], -1.0, w("bk", slice(0, 32)), ALU.mult, ALU.add).then_inc(kb_chain, 1)
            dve.wait_ge(ek_exp, BH)
            dve.reciprocal(krec[:, :], ksum[:, :]).then_inc(kmax_ready, 1)
            dve.wait_ge(kmax_ready, NQ + 1)
            ek = EK[:, :].rearrange("p (b n) -> p b n", b=BH)
            dve.tensor_tensor(ek, ek, krec[:, :].unsqueeze(2).to_broadcast([32, BH, N]), ALU.mult).then_inc(ek_ready, 1)

            def heads(ap):
                return ap.rearrange("p (g d) -> p g d", d=KD)

            def by_head(ap):
                return ap[:, :].unsqueeze(2).to_broadcast([P, 32, KD])

            def queries_shift(it):
                dve.wait_ge(q_ready, it + 1)
                if it >= 1:
                    dve.wait_ge(qsub_ready, it)
                dve.reduce_max(qmax[:, :], heads(PS[:, it % 2]), AX_X).then_inc(qmax_ready, 1)
                dve.wait_ge(qmax_ready, it + 1)
                if it >= 2:
                    dve.wait_ge(qt_ready, it - 1)
                dve.tensor_tensor(heads(QE[:, it % 2]), heads(PS[:, it % 2]), by_head(qmax), ALU.subtract).then_inc(qsub_ready, 1)

            def attn_add(it):
                dve.wait_ge(a_ready, it + 1)
                dve.scalar_tensor_tensor(X[:, cols(it, N)], PS[:, 6, 0:N], w("bo"), X[:, cols(it, N)], ALU.add, ALU.add).then_inc(x3_ready, 1)

            queries_shift(0)
            for it in range(BH):
                dve.wait_ge(ekt_ready, it + 1)
                if it >= 1:
                    dve.wait_ge(cx_ready, it)
                dve.tensor_copy(EKT[:, :], PS[:, 4 + it % 2, 0:64]).then_inc(ekt_out, 1)
                if it + 1 < BH:
                    queries_shift(it + 1)
                dve.wait_ge(cx_ready, it + 1)
                for h in range(HALVES):
                    if it >= 1:
                        dve.wait_ge(mb_ready, it)
                    dve.scalar_tensor_tensor(BD[:, h].rearrange("p (g d) -> p g d", d=KD),
                                             PS[:, 4 + it % 2, 64 + 16 * h:80 + 16 * h].unsqueeze(1).to_broadcast([P, HEADS, KD]),
                                             w("bv"), w("head_mask").rearrange("p (g d) -> p g d", d=KD), ALU.add, ALU.mult).then_inc(bd_ready, 1)
                dve.wait_ge(qexp_ready, it + 1)
                if it >= 1:
                    dve.wait_ge(qn_ready, it)
                dve.tensor_reduce(qsum[:, :], heads(QE[:, it % 2]), AX_X, ALU.add).then_inc(qsum_ready, 1)
                dve.wait_ge(qsum_ready, it + 1)
                dve.reciprocal(qrec[:, :], qsum[:, :]).then_inc(qrec_ready, 1)
                if it >= 1:
                    attn_add(it - 1)
            attn_add(BH - 1)

            dve.wait_ge(bn_rs, 2)
            dve.tensor_tensor(bn_a[:, :], bn_a[:, :], w("bn_g"), ALU.mult).then_inc(bn_chain, 1)
            dve.tensor_tensor(bn_c[:, :], w("bn_b"), w("bn_m"), ALU.subtract).then_inc(bn_chain, 1)
            dve.wait_ge(bn_chain, 2)
            dve.tensor_tensor(bn_c[:, :], bn_c[:, :], bn_a[:, :], ALU.mult).then_inc(bn_chain2, 1)
            dve.wait_ge(bn_chain2, 1)
            dve.tensor_tensor(bn_c[:, :], bn_c[:, :], w("bn_be"), ALU.add).then_inc(bn_chain, 1)
            ln_split_dve(dve, 3, lambda _: dve.wait_ge(kp_ready, NQ))
            f = Chain(dve, fl_chain)
            dve.wait_ge(fl_ready, 1)
            f(dve.tensor_reduce(f_logits[:, :, :], PS[:, 4, 0:32].rearrange("p (t s e) -> p t e s", s=2, e=E), AX_X, ALU.add))
            f.wait()
            br = w("f_br").unsqueeze(1).to_broadcast([P, 2, E])
            f(dve.tensor_scalar(f_logits[:, :, :], f_logits[:, :, :], 1.0 / B, None, ALU.mult))
            f.wait()
            f(dve.tensor_tensor(f_logits[:, :, :], f_logits[:, :, :], br, ALU.add))
            f.wait()
            f(dve.reduce_max(f_max[:, :], f_logits[:, :, :], AX_X))
            f.wait()
            f(dve.tensor_tensor(f_logits[:, :, :], f_logits[:, :, :], f_max[:, :].unsqueeze(2).to_broadcast([P, 2, E]), ALU.subtract))
            dve.wait_ge(fe_ready, 1)
            f(dve.reduce_sum(f_sum[:, :], f_logits[:, :, :], AX_X))
            f.wait()
            f(dve.reciprocal(f_sum[:, :], f_sum[:, :]))
            f.wait()
            dve.tensor_tensor(f_logits[:, :, :], f_logits[:, :, :], f_sum[:, :].unsqueeze(2).to_broadcast([P, 2, E]), ALU.mult).then_inc(fw_ready, 1)

            def f_scale(it, n1, p):
                dve.wait_ge(h2_ready[p], n1)
                wait_last(dve, wo_done[p], it)
                dve.tensor_tensor(HW[:, p].rearrange("p (h n) -> p h n", h=HALVES), H2[:, p].rearrange("p (h n) -> p h n", h=HALVES),
                                  FW[:, p].unsqueeze(1).to_broadcast([P, HALVES, N]), ALU.mult).then_inc(hw_ready[p], 1)

            def f_add(it, n1):
                dve.wait_ge(wo_done[PAIRS - 1], n1)
                x_it = X[:, bass.ds(it * N, N)]
                dve.tensor_tensor(x_it, PS[:, 4, 0:N], x_it, ALU.add).then_inc(x4_ready, 1)

            dve.wait_ge(fb_out, PAIRS + 1)
            dve.wait_ge(bias_added, NQ)
            for p in range(PAIRS):
                dve.wait_ge(w2_done[p], BH)
            for p in range(PAIRS):
                f_scale(0, 1, p)
            with dve.Fori(1, BH) as i:
                it, n1 = it_values(dve, i)
                f_scale(it, n1, 0)
                f_scale(it, n1, 1)
                f_add(dve.snap(it - 1), it)
                f_scale(it, n1, 2)
                f_scale(it, n1, 3)
            f_add(BH - 1, BH)

        @block.gpsimd
        def _(pool):
            pool.memset(PADDED[:, :], 0.0).then_inc(padded_zero, 1)
            pool.wait_ge(rounded_ready, 1)
            pool.tensor_scalar(QX[:, :], QT[:, :], -1.0, TOP, ALU.mult, ALU.add).then_inc(comp_ready, 1)
            pool.wait_ge(late_in, 16)
            pool.tensor_copy(WH[:, :], WT[:, SPLIT0:SPLIT1]).then_inc(split_high, 1)
            pool.wait_ge(split_high, 1)
            pool.tensor_tensor(WL[:, :], WT[:, SPLIT0:SPLIT1], WH[:, :].bitcast(F32), ALU.subtract).then_inc(split_low, 1)
            pool.wait_ge(split_low, 1)
            for both, name in ((router2, "router"), (f_wr2, "f_wr")):
                pool.tensor_copy(both[:, 0:E], part(WH, name))
                last = pool.tensor_copy(both[:, E:2 * E], part(WL, name))
            last.then_inc(split_low, 1)
            pool.wait_ge(cw_ready, 1)
            pool.wait_ge(t_ready, NQ)
            pool.wait_ge(sw_out, NQ)
            for q in range(NQ):
                pool.tensor_tensor(U[:, cols(q)].rearrange("p (b n) -> p b n", n=N), T[:, cols(q)].rearrange("p (b n) -> p b n", n=N),
                                   CW[:, 2 * q:2 * q + 2].unsqueeze(2).to_broadcast([P, 2, N]), ALU.mult).then_inc(chain_g, 1)
                pool.wait_ge(chain_g, q + 1)
                pool.tensor_tensor(U[:, cols(q)], U[:, cols(q)], SW[:, cols(q)], ALU.mult).then_inc(u_ready, 1)
            for q in range(NQ):
                pool.wait_ge(gated_ready, q + 1)
                pool.tensor_tensor(X[:, cols(q)], X[:, cols(q)], U[:, cols(q)], ALU.add).then_inc(x1_ready, 1)
            for q in range(NQ):
                pool.wait_ge(t_ready, NQ + q + 1)
                pool.wait_ge(xc_ready, NQ + q + 1)
                pool.wait_ge(x1_ready, q + 1)
                pool.tensor_tensor(X[:, cols(q)], X[:, cols(q)], T[:, cols(q)], ALU.add).then_inc(x_added, 1)
            for it in range(BH):
                pool.wait_ge(qrec_ready, it + 1)
                q3 = QE[:, it % 2].rearrange("p (g d) -> p g d", d=KD)
                pool.tensor_tensor(q3, q3, qrec[:, :].unsqueeze(2).to_broadcast([P, 32, KD]), ALU.mult).then_inc(qn_ready, 1)
            pool.wait_ge(fb_out, PAIRS + 1)
            for q in range(NQ):
                pool.wait_ge(xc_ready, 3 * NQ + q + 1)
                pool.wait_ge(x3_ready, BH)
                x_q = X[:, cols(q)].rearrange("p (b n) -> p b n", n=N)
                pool.tensor_tensor(x_q, x_q, FB[:, :].unsqueeze(1).to_broadcast([P, 2, N]), ALU.add).then_inc(bias_added, 1)


def pack_weights(v):
    a = np.zeros((P, NCOL), np.float32)

    def put(name, rows, value, cols=slice(None)):
        lo, hi = AT[name]
        a[rows, lo:hi][:, cols] = value

    half = [slice(0, C), slice(C, P)]
    eye = np.eye(C, dtype=np.float32)
    put("eps", slice(None), np.array([1e-6, 1e-5, 1e-3, 0], np.float32))
    put("ident", slice(None), np.eye(P, dtype=np.float32))
    group = np.kron(np.eye(P // GROUP), np.ones((GROUP, GROUP))).astype(np.float32)
    put("group", slice(None), group)
    put("mask8", slice(None), np.tile(np.eye(8), (P // 8, 1)))
    put("gt_sel", slice(None), np.tile(np.kron(np.eye(BH), np.full((GROUP, 1), 8.0)), (HALVES, 1)))
    for h, rows in enumerate(half):
        put("center", rows, eye - 1 / C, slice(h * C, (h + 1) * C))
        put("mean", rows, 1 / C, slice(h * C, (h + 1) * C))
        put("tap_th", rows, v["L0_conv_sa_w"].reshape(C, TAPS), slice(h * TAPS, (h + 1) * TAPS))
        put("tap_th", rows, v["L0_conv_tp_w1"].T, slice(32 + h * CR, 32 + (h + 1) * CR))
        put("tp_b1", slice(32 + h * CR, 32 + (h + 1) * CR), v["L0_conv_tp_b1"][:, None])
        put("tp_w2", slice(32 + h * CR, 32 + (h + 1) * CR), v["L0_conv_tp_w2"].T, slice(h * C, (h + 1) * C))
        put("tap_sum", slice(h * TAPS, (h + 1) * TAPS), 1.0, slice(h * C, (h + 1) * C))
        put("ca_w1", rows, v["L0_conv_ca_w1"].T, slice(h * CR, (h + 1) * CR))
        put("ca_b1", slice(h * CR, (h + 1) * CR), v["L0_conv_ca_b1"][:, None])
        put("ca_w2", slice(h * CR, (h + 1) * CR), v["L0_conv_ca_w2"].T, slice(h * C, (h + 1) * C))
        put("ca_b2", rows, v["L0_conv_ca_b2"][:, None])
        put("router", rows, v["L0_ffn_router_w"].T)
        put("f_wr", rows, v["L1_ffn_Wr"])
        put("w1", rows, v["L0_ffn_w1"].transpose(1, 0, 2).reshape(C, E * C))
        put("f_w1", rows, v["L1_ffn_W1"].transpose(1, 0, 2).reshape(C, E * C))
        for part in range(2):
            for e in range(E):
                row = slice(16 * h + E * part + e, 16 * h + E * part + e + 1)
                put("sel", row, 1.0, slice((h * PAIRS + e // 2) * P + e % 2 * C, (h * PAIRS + e // 2) * P + e % 2 * C + C))
                put("b2", row, v["L0_ffn_b2"][e], slice(h * C, (h + 1) * C))
        put("wq", rows, v["L1_conv_Wq"].T)
        put("wv", rows, np.tile(v["L1_conv_Wv"].T, (1, HEADS)))
        put("wk", rows, v["L1_conv_Wk"].T, slice(h * KD, (h + 1) * KD))
        put("bk", slice(h * KD, (h + 1) * KD), v["L1_conv_bk"][:, None])
        put("bo", rows, v["L1_conv_bo"][:, None])
        put("f_bo", slice(0, E), v["L1_ffn_bo"], slice(h * C, (h + 1) * C))

    def pairs(x):
        return x.reshape(PAIRS, P).T

    put("tp_b2", slice(None), v["L0_conv_tp_b2"][0])
    put("sa_b", slice(None), v["L0_conv_sa_b"][0])
    put("ident2", slice(None), np.eye(P))
    put("bq", slice(0, 1), np.tile(v["L1_conv_bq"], 4)[None])
    put("ones_row", slice(0, 1), 1.0)
    put("b1", slice(None), pairs(v["L0_ffn_b1"]))
    put("expert_rank", slice(None), np.arange(E, 0, -1))
    put("w2", slice(None), v["L0_ffn_w2"].reshape(PAIRS, P, C).transpose(1, 0, 2).reshape(P, PAIRS * C))
    put("bv", slice(None), np.tile(v["L1_conv_bv"], HEADS)[:, None])
    put("wo", slice(None), v["L1_conv_Wo"].T)
    put("head_mask", slice(None), np.kron(np.eye(HEADS), np.ones((KD, KD))))
    for name, k in (("bn_g", "g"), ("bn_b", "b"), ("bn_be", "be"), ("bn_m", "m"), ("bn_v", "v")):
        for layer in range(2):
            put(name, slice(None), pairs(v[f"L1_ffn_{k}{layer + 1}"]), slice(layer * PAIRS, (layer + 1) * PAIRS))
    for e in range(E):
        rows = half[e % 2]
        put("f_w2", rows, v["L1_ffn_W2"][e], slice(e * C, (e + 1) * C))
    put("f_wo", slice(None), v["L1_ffn_Wo"].reshape(PAIRS, P, C).transpose(1, 0, 2).reshape(P, PAIRS * C))
    put("f_br", slice(None), v["L1_ffn_br"])
    return a


def kernel(**inputs):
    import concourse.bacc as bacc
    from concourse.bass_utils import run_bass_kernel_spmd

    v = {k: np.asarray(a) for k, a in inputs.items()}
    arrays = {"in_x": np.ascontiguousarray(v["x"]), "in_weights": pack_weights(v)}
    nc = bacc.Bacc("TRN2", target_bir_lowering=False, num_devices=1)
    aps = [nc.dram_tensor(n, a.shape, F32, kind="ExternalInput").ap() for n, a in arrays.items()]
    out = nc.dram_tensor("out_x", v["x"].shape, F32, kind="ExternalOutput").ap()
    metaformer_kernel(nc, *aps, out)
    return run_bass_kernel_spmd(nc, [arrays], core_ids=[0]).results[0]["out_x"]
```

```python
from contextlib import ExitStack

import numpy as np

import concourse.bass as bass
from concourse import mybir

F32 = mybir.dt.float32
F32R = mybir.dt.float32r
F16 = mybir.dt.float16
ALU = mybir.AluOpType
ACT = mybir.ActivationFunctionType
AX_X = mybir.AxisListType.X

P = 128
C = 64
B, H, W = 16, 16, 16
N = H * W
HALVES = 2
BH = B // HALVES
COLS = BH * N
Q = 512
NQ = COLS // Q
CR = 4
TAPS = 9
E = 8
PAIRS = E // 2
HEADS, KD = 8, 16

PITCH = W + 1
MAP = PITCH * (H + 1)
LEAD = PITCH + 1
FLAT = BH * MAP

VALUE_BITS = 23
STEP = 256.0
SCALE = STEP * 2 ** 20
TOP = STEP * 2 ** VALUE_BITS
QUANT = 0.85
POS = np.float32(QUANT) * np.float32(C * N - 1)
LOW = int(np.floor(POS))
W_HIGH = float(np.float32(POS - np.floor(POS)))
W_LOW = float(np.float32(1) - np.float32(W_HIGH))
RANK = C * N - LOW
GROUP = 8
ACT_COLS = 1024
DVE_COLS = COLS - ACT_COLS


def weight_columns():
    return [
        ("center", P), ("mean", P), ("eps", 4), ("tap_th", 40), ("tp_b1", 1), ("tp_w2", P), ("tp_b2", 1),
        ("sa_b", 1), ("tap_sum", P), ("ca_w1", 8), ("ca_b1", 1), ("ca_w2", P), ("ca_b2", 1),
        ("mask8", 8), ("gt_sel", 8), ("ident", P), ("group", P),
        ("router", E), ("f_wr", E), ("ident2", P), ("sel", HALVES * PAIRS * P), ("w1", PAIRS * P), ("b2", P),
        ("f_w1", PAIRS * P),
        ("b1", PAIRS), ("expert_rank", E), ("w2", PAIRS * C),
        ("wkv", 4 * KD), ("kv_bias", 1), ("wq", HALVES * P), ("bq", 1), ("to_heads", HALVES * P), ("wo", C), ("bo", 1),
        ("head_mask", P),
        ("bn_g", 2 * PAIRS), ("bn_b", 2 * PAIRS), ("bn_be", 2 * PAIRS), ("bn_m", 2 * PAIRS), ("bn_v", 2 * PAIRS),
        ("f_w2", PAIRS * P), ("f_wo", PAIRS * C), ("f_bo", P), ("f_br", E),
    ]


AT = {}
NCOL = 0
for _name, _n in weight_columns():
    AT[_name] = (NCOL, NCOL + _n)
    NCOL += _n
SPLIT0, SPLIT1 = AT["router"][0], AT["f_w1"][1]
EARLY = SPLIT0


def metaformer_kernel(nc, x_dram, weights_dram, out_dram):
    ctx = ExitStack()
    with ctx:
        def sb(name, shape, dt=F32):
            return ctx.enter_context(nc.sbuf_tensor(name, shape, dt))

        def sem(name):
            return ctx.enter_context(nc.semaphore(name))

        WT = sb("weights", [P, NCOL])

        def w(name, rows=slice(0, P), cols=None):
            a, b = AT[name]
            if cols is not None:
                a, b = a + cols.start, a + cols.stop
            return WT[rows, a:b]

        X = sb("x_resid", [P, COLS])
        HID = sb("hidden_of_all_tokens", [P, BH * COLS])
        QX, QT, SW, REL, AB, SQ, XC, RS = (HID[:, i * COLS:(i + 1) * COLS] for i in range(BH))
        T = sb("x_normed", [P, COLS])
        S = sb("x_split", [P, HALVES, COLS], F32R)
        ident_r = sb("ident_r", [P, P], F32R)

        PADDED = sb("taps_padded", [18, FLAT + 2 * LEAD])
        SHIFTED = sb("taps_shifted", [18, FLAT])
        TH = sb("threshold_hidden", [40, COLS])
        U = sb("gated_x", [P, COLS])
        pooled = sb("pooled", [P, BH])
        ca_h = sb("channel_hidden", [8, BH])
        CW = sb("channel_weights", [P, BH])
        thr = sb("threshold", [P, 1])
        thr_half = sb("threshold_less_half_step", [P, 1])
        thr_top = sb("threshold_above", [P, 1])
        step = sb("bit_step", [P, 1])
        bit = sb("bit_stays", [P, 1])
        counts = sb("partial_counts", [P, 2], F16)
        group16 = sb("group_f16", [P, P], F16)
        above = sb("above_max", [P, 1])
        above8 = sb("above_max_spread", [P, 8])
        upper = sb("upper_value", [P, 1])
        flag = sb("upper_is_next", [P, 1])
        gt = sb("quantile", [P, 1])
        gt8 = sb("quantile_spread", [P, BH])
        neg_gt = sb("neg_quantile", [P, BH])

        WH = sb("weights_high", [P, SPLIT1 - SPLIT0], F32R)
        WL = sb("weights_low", [P, SPLIT1 - SPLIT0], F32R)
        router2 = sb("router_parts", [P, 2 * E], F32R)
        f_wr2 = sb("f_router_parts", [P, 2 * E], F32R)

        def part(tile, name, rows=slice(0, P), cols=None):
            a, b = (n - SPLIT0 for n in AT[name])
            if cols is not None:
                a, b = a + cols.start, a + cols.stop
            return tile[rows, a:b]

        TILES = B * N // P
        logits = sb("logits", [P, TILES, E])
        best = sb("best_logit", [P, TILES])
        second = sb("second_logit", [P, TILES])
        is_best = sb("is_best", [P, TILES, E])
        is_second = sb("is_second", [P, TILES, E])
        key = sb("tie_key", [P, TILES, E])
        key_max = sb("tie_key_max", [P, TILES])
        lead = sb("share_lead", [P, TILES])
        share1 = sb("best_share", [P, TILES])
        share2 = sb("second_share", [P, TILES])
        combine = sb("combine", [P, TILES, E])
        combine2 = sb("combine_parts", [P, TILES, 2, E], F32R)
        CT = sb("combine_rows", [P, COLS], F32R)
        G, HS, H2 = (t[:, :].rearrange("p (g q) -> p g q", g=PAIRS) for t in (QT, U, QX))

        EKV = REL[0:4 * KD, :]
        EKVT = AB[:, 0:1024]
        MB = AB[:, 1024:2048].rearrange("p (h b c) -> p h b c", h=HALVES, b=BH)
        BD = H2.rearrange("p g (b n) -> p (g b) n", n=P)
        Q0 = G[:, 0:2]
        QB = HS
        QS = G[:, 2:4]
        kmax = sb("key_max", [32, BH])
        kbias = sb("key_bias", [32, BH])
        ksum = sb("key_sum", [32, BH])
        krec = sb("key_reciprocal", [32, BH])
        CTX = sb("contexts", [32, BH * 32])
        qmax = sb("query_max", [P, 2, 32])
        qsum = sb("query_sum", [P, 2, 32])
        qrec = sb("query_reciprocal", [P, 2, 32])

        bn_a = sb("bn_scale", [P, 2 * PAIRS])
        bn_c = sb("bn_shift", [P, 2 * PAIRS])
        f_logits = sb("f_logits", [P, 2, E])
        f_max = sb("f_max", [P, 2])
        f_sum = sb("f_sum", [P, 2])
        fT = sb("f_weights_rows", [E, N])
        FW = SW[:, 0:PAIRS * N].rearrange("p (g n) -> p g n", g=PAIRS)
        FB = SW[:, PAIRS * N:(PAIRS + 1) * N]
        H1 = G
        HW = HS

        PS = ctx.enter_context(nc.psum_tensor("ps", [P, 8, Q], F32))

        w_in, x_in, late_in = sem("weights_in"), sem("x_in"), sem("late_weights_in")
        xc_ready, xc_copied, sq_ready, var_ready = sem("xc_ready"), sem("xc_copied"), sem("sq_ready"), sem("var_ready")
        ln_taken, rs_ready, t_ready = sem("ln_taken"), sem("rs_ready"), sem("t_ready")
        abs_ready, q_in, rounded_ready = sem("abs_ready"), sem("quantile_in"), sem("rounded_ready")
        half_ready, bit_ready = sem("half_ready"), sem("bit_ready")
        step_ready, group_ready = sem("step_ready"), sem("group_ready")
        padded_zero, taps_ready, taps_out, th_out, shifted_in = sem("padded_zero"), sem("taps_ready"), sem("taps_out"), sem("th_out"), sem("shifted_in")
        rel_ready, rel_out, sw_ready, sw_out = sem("rel_ready"), sem("rel_out"), sem("sw_ready"), sem("sw_out")
        pooled_ready, ca1_ready, ca1_out, ca2_ready, cw_ready = sem("pooled_ready"), sem("ca1_ready"), sem("ca1_out"), sem("ca2_ready"), sem("cw_ready")
        u_ready, comp_ready = sem("u_ready"), sem("complement_ready")
        thr_ready, dve_counted, act_counted, counted = sem("thr_ready"), sem("dve_counted"), sem("act_counted"), sem("counted")
        chain_v, chain_a, chain_g = sem("vector_chain"), sem("scalar_chain"), sem("gpsimd_chain")
        top_ready, top_counted, above_ready, above_spread = sem("top_ready"), sem("top_counted"), sem("above_ready"), sem("above_spread")
        top_summed, gt_ready, gt_spread = sem("top_summed"), sem("gt_ready"), sem("gt_spread")
        split_high, split_low = sem("split_high"), sem("split_low")
        hi_ready, s_ready = sem("hi_ready"), sem("s_ready")
        logits_ready, top_v, lead_ready, tanh_ready, combine_ready = sem("logits_ready"), sem("top_chain"), sem("lead_ready"), sem("tanh_ready"), sem("combine_ready")
        ct_ready, ct_out, x_added = sem("ct_ready"), sem("ct_out"), sem("x_added")
        z_ready, gelu_done, cb_ready = ([sem(f"{n}{p}") for p in range(PAIRS)] for n in ("z_ready", "gelu_done", "cb_ready"))
        hs_ready, w2_done = ([sem(f"{n}{p}") for p in range(PAIRS)] for n in ("hs_ready", "w2_done"))
        y_taken, top_used = sem("y_taken"), sem("top_used")
        kv_ready, kmax_ready, kb_chain, ek_exp, ek_ready = (sem(n) for n in ("kv_ready", "kmax_ready", "kb_chain", "ek_exp", "ek_ready"))
        krec_ready, v_out, ekt_ready, ekt_out = (sem(n) for n in ("krec_ready", "v_out", "ekt_ready", "ekt_out"))
        q_ready, q_biased, qb_ready, qmax_ready, qsub_ready = (sem(n) for n in ("q_ready", "q_biased", "qb_ready", "qmax_ready", "qsub_ready"))
        qexp_ready, qsum_ready, qrec_ready, qn_ready, qs_ready = (sem(n) for n in ("qexp_ready", "qsum_ready", "qrec_ready", "qn_ready", "qs_ready"))
        cx_ready, cx_out, heads_ready, bd_ready, mb_ready, mb_out = (sem(n) for n in ("cx_ready", "cx_out", "heads_ready", "bd_ready", "mb_ready", "mb_out"))
        a_ready, x3_ready = sem("a_ready"), sem("x3_ready")
        bn_chain, bn_chain2, bn_rs, fl_ready, fl_chain, fe_ready, fw_ready = (sem(n) for n in ("bn_chain", "bn_chain2", "bn_rs", "fl_ready", "fl_chain", "fe_ready", "fw_ready"))
        ft_ready, ft_out, fb_ready, fb_out, bias_added = (sem(n) for n in ("ft_ready", "ft_out", "fb_ready", "fb_out", "bias_added"))
        z1_ready, h1_ready, z2_ready = ([sem(f"{n}{p}") for p in range(PAIRS)] for n in ("z1_ready", "h1_ready", "z2_ready"))
        h2_ready, hw_ready, wo_done = ([sem(f"{n}{p}") for p in range(PAIRS)] for n in ("h2_ready", "hw_ready", "wo_done"))
        x4_ready, rows_zero = sem("x4_ready"), sem("rows_zero")
        diff_ready, mask_ready, gated_ready, x1_ready = sem("diff_ready"), sem("mask_ready"), sem("gated_ready"), sem("x1_ready")
        out_done = sem("out_done")

        def cols(q, n=Q):
            return slice(q * n, (q + 1) * n)

        def maps(ap):
            return ap.rearrange("p (b y x) -> p b y x", b=2, y=H)

        def padded_maps(ap, q):
            return ap[:, 2 * q * MAP:2 * (q + 1) * MAP].rearrange("p (b y x) -> p b y x", b=2, x=PITCH)[:, :, 0:H, 0:W]

        class Chain:

            def __init__(self, eng, s):
                self.eng, self.s, self.n = eng, s, 0

            def __call__(self, ins):
                self.n += 1
                ins.then_inc(self.s, 1)

            def wait(self):
                self.eng.wait_ge(self.s, self.n)

        block = ctx.enter_context(nc.Block())

        def ln_pe_center(pe, n, q, x_wait):
            x_wait(q)
            if 4 * n + q >= 2:
                pe.wait_ge(xc_copied, 4 * n + q - 1)
            if n == 1:
                pe.matmul(PS[:, q % 2], w("center"), X[:, cols(q)], start=True, stop=False)
                pe.wait_ge(gated_ready, q + 1)
                pe.matmul(PS[:, q % 2], w("center"), U[:, cols(q)], start=False, stop=True).then_inc(xc_ready, 1)
            else:
                pe.matmul(PS[:, q % 2], w("center"), X[:, cols(q)], start=True, stop=True).then_inc(xc_ready, 1)

        def ln_pe_var(pe, n, q):
            pe.wait_ge(sq_ready, 4 * n + q + 1)
            if 4 * n + q >= 2:
                pe.wait_ge(ln_taken, 4 * n + q - 1)
            pe.matmul(PS[:, 2 + q % 2], w("mean"), SQ[:, cols(q)], start=True, stop=True).then_inc(var_ready, 1)

        def ln_pe(pe, n, x_wait):
            for q in range(NQ + 1):
                if q < NQ:
                    ln_pe_center(pe, n, q, x_wait)
                if q >= 1:
                    ln_pe_var(pe, n, q - 1)

        def ln_act_square(act, n, q):
            act.wait_ge(xc_copied, 4 * n + q + 1)
            act.activation(SQ[:, cols(q)], XC[:, cols(q)], ACT.Square).then_inc(sq_ready, 1)

        def ln_pool_square(pool, n, q):
            pool.wait_ge(xc_copied, 4 * n + q + 1)
            pool.tensor_tensor(SQ[:, cols(q)], XC[:, cols(q)], XC[:, cols(q)], ALU.mult).then_inc(sq_ready, 1)

        def ln_act_rstd(act, n, q, eps_col):
            act.wait_ge(var_ready, 4 * n + q + 1)
            if n:
                act.wait_ge(t_ready, 4 * n)
            act.activation(RS[:, cols(q)], PS[:, 2 + q % 2], ACT.Ln, bias=w("eps", cols=slice(eps_col, eps_col + 1))).then_inc(ln_taken, 1)
            act.wait_ge(ln_taken, 4 * n + q + 1)
            act.activation(RS[:, cols(q)], RS[:, cols(q)], ACT.Exp, scale=-0.5).then_inc(rs_ready, 1)

        def ln_act(act, n, eps_col):
            for q in range(NQ + 1):
                if q < NQ:
                    ln_act_square(act, n, q)
                if q >= 1:
                    ln_act_rstd(act, n, q - 1, eps_col)

        def ln_dve_copy(dve, n, q):
            dve.wait_ge(xc_ready, 4 * n + q + 1)
            if n:
                dve.wait_ge(t_ready, 4 * n)
            dve.tensor_copy(XC[:, cols(q)], PS[:, q % 2]).then_inc(xc_copied, 1)

        def ln_dve_scale(dve, n, q, t_free=None):
            dve.wait_ge(rs_ready, 4 * n + q + 1)
            dve.wait_ge(xc_copied, 4 * n + q + 1)
            if t_free:
                t_free(q)
            dve.tensor_tensor(T[:, cols(q)], XC[:, cols(q)], RS[:, cols(q)], ALU.mult).then_inc(t_ready, 1)

        def ln_dve(dve, n, t_free=None):
            for q in range(NQ + 2):
                if q < NQ:
                    ln_dve_copy(dve, n, q)
                if q >= 2:
                    ln_dve_scale(dve, n, q - 2, t_free)

        def split_act(act, n, q, s_free=None):
            act.wait_ge(t_ready, 4 * n + q + 1)
            if s_free:
                s_free()
            act.activation(S[0:C, 0, cols(q)], T[0:C, cols(q)], ACT.Copy).then_inc(hi_ready, 1)
            act.activation(S[C:P, 1, cols(q)], T[C:P, cols(q)], ACT.Copy).then_inc(hi_ready, 1)

        def split_dve(dve, n, q):
            for h, (own, other) in enumerate(((slice(0, C), slice(C, P)), (slice(C, P), slice(0, C)))):
                dve.wait_ge(hi_ready, 2 * NQ * (n // 2) + 2 * q + h + 1)
                dve.tensor_tensor(S[other, h, cols(q)], T[own, cols(q)], S[own, h, cols(q)].bitcast(F32),
                                  ALU.subtract).then_inc(s_ready, 1)

        def ln_split_act(act, n, eps_col, s_free=None):
            for q in range(NQ + 1):
                if q < NQ:
                    ln_act_rstd(act, n, q, eps_col)
                if q >= 1:
                    split_act(act, n, q - 1, s_free)

        def ln_split_dve(dve, n, t_free=None):
            for q in range(NQ + 3):
                if q < NQ:
                    ln_dve_copy(dve, n, q)
                if 2 <= q < NQ + 2:
                    ln_dve_scale(dve, n, q - 2, t_free)
                if q >= 3:
                    split_dve(dve, n, q - 3)

        def pair(name, p, tile=None, n=P):
            c = slice(p * n, (p + 1) * n)
            return w(name, cols=c) if tile is None else part(tile, name, cols=c)

        def two_pass(pe, out, name, p, rhs, start=True, stop=True):
            pe.matmul(out, pair(name, p, WH), rhs, start=start, stop=False)
            return pe.matmul(out, pair(name, p, WL), rhs, start=False, stop=stop)

        def after(eng, i):
            return i + 1 if isinstance(i, int) else eng.snap(i + 1)

        def it_values(eng, i):
            i = i if isinstance(i, int) else eng.snap(i)
            return i, after(eng, i)

        def wait_last(eng, s, n):
            if not (isinstance(n, int) and n == 0):
                eng.wait_ge(s, n)

        HIDDEN_BANK = (5, 6, 7, 0)
        AHEAD = 5
        SHARES_AT = 3

        @block.sync
        def _(sp):
            x_v = x_dram.rearrange("(h b) c y x -> h c b (y x)", h=HALVES)
            for h in range(HALVES):
                sp.dma_start(X[h * C:(h + 1) * C, :].rearrange("c (b n) -> c b n", b=BH), x_v[h]).then_inc(x_in, 16)
            sp.dma_start(WT[:, 0:EARLY], weights_dram[:, 0:EARLY]).then_inc(w_in, 16)
            sp.dma_start(WT[:, EARLY:NCOL], weights_dram[:, EARLY:NCOL]).then_inc(late_in, 16)
            sp.wait_ge(abs_ready, NQ)
            for h in range(HALVES):
                for b in range(BH):
                    g = h * C + b * GROUP
                    sp.dma_start(QT[g:g + GROUP, :].rearrange("j (c n) -> j c n", c=C // GROUP),
                                 AB[h * C:(h + 1) * C, b * N:(b + 1) * N]
                                 ).then_inc(q_in, 16)
            sp.wait_ge(taps_out, NQ)
            for dy in range(3):
                for dx in range(3):
                    tap = 3 * dy + dx
                    off = LEAD + (dy - 1) * PITCH + dx - 1
                    sp.dma_start(SHIFTED[tap:18:TAPS, :], PADDED[tap:18:TAPS, off:off + FLAT]).then_inc(shifted_in, 16)
            o_v = out_dram.rearrange("(h b) c y x -> h b c (y x)", h=HALVES)
            with sp.Fori(0, BH) as b0:
                b = sp.snap(b0)
                sp.wait_ge(x4_ready, b + 1)
                for h in range(HALVES):
                    sp.dma_start(o_v[h, bass.ds(b, 1)].rearrange("b c n -> (b c) n"), X[h * C:(h + 1) * C, bass.ds(b * N, N)]).then_inc(out_done, 16)
            sp.wait_ge(out_done, 16 * B)

        @block.tensor
        def _(pe):
            pe.wait_ge(w_in, 16)
            ln_pe(pe, 0, lambda q: pe.wait_ge(x_in, 32))
            for q in range(NQ):
                pe.wait_ge(t_ready, q + 1)
                if q >= 2:
                    pe.wait_ge(th_out, q - 1)
                    pe.wait_ge(taps_out, q - 1)
                pe.matmul(PS[0:40, 4 + q % 2], w("tap_th"), T[:, cols(q)], start=True, stop=True).then_inc(taps_ready, 1)
                pe.wait_ge(th_out, q + 1)
                if q >= 2:
                    pe.wait_ge(rel_out, q - 1)
                pe.matmul(PS[:, 6 + q % 2], w("tp_w2", slice(32, 40)), TH[32:40, cols(q)], start=True, stop=True).then_inc(rel_ready, 1)
            pe.wait_ge(pooled_ready, 1)
            pe.wait_ge(xc_copied, NQ)
            pe.matmul(PS[0:8, 0, 0:BH], w("ca_w1"), pooled[:, :], start=True, stop=True).then_inc(ca1_ready, 1)
            pe.wait_ge(ca1_out, 1)
            pe.matmul(PS[:, 1, 0:BH], w("ca_w2", slice(0, 8)), ca_h[:, :], start=True, stop=True).then_inc(ca2_ready, 1)
            for q in range(NQ):
                pe.wait_ge(shifted_in, 16 * TAPS)
                bank = 4 + q % 4
                if bank < 6:
                    pe.wait_ge(th_out, NQ)
                    pe.wait_ge(taps_out, NQ)
                else:
                    pe.wait_ge(rel_out, NQ)
                pe.matmul(maps(PS[:, bank]), w("tap_sum", slice(0, 18)), padded_maps(SHIFTED, q),
                          start=True, stop=True).then_inc(sw_ready, 1)
            def sum_counts(r):
                pe.wait_ge(dve_counted, r + 1)
                pe.wait_ge(act_counted, r + 1)
                pe.matmul(PS[:, 0, 0:2], group16[:, :], counts[:, :], start=True, stop=True).then_inc(counted, 1)

            pe.wait_ge(group_ready, 1)
            with pe.Fori(0, VALUE_BITS) as r:
                sum_counts(pe.snap(r))
            pe.wait_ge(above_ready, 1)
            pe.wait_ge(cw_ready, 1)
            pe.matmul(PS[:, 1, 0:8], w("group"), above8[:, :], start=True, stop=True).then_inc(above_spread, 1)
            pe.wait_ge(top_counted, 1)
            pe.wait_ge(thr_ready, VALUE_BITS + 1)
            pe.matmul(PS[:, 0, 0:2], group16[:, :], counts[:, :], start=True, stop=True).then_inc(top_summed, 1)
            pe.wait_ge(gt_ready, 1)
            pe.matmul(PS[:, 2, 0:BH], w("mean"), gt8[:, :], start=True, stop=True).then_inc(gt_spread, 1)

            pe.wait_ge(top_used, 1)
            ln_pe(pe, 1, lambda q: None)
            pe.wait_ge(split_low, 2)
            pe.wait_ge(sw_out, NQ)

            def route(q):
                pe.wait_ge(s_ready, 2 * q + 2)
                for j in range(4 * q, 4 * q + 4):
                    for h in range(HALVES):
                        t = 2 * j + h
                        last = pe.matmul(PS[:, 4, 16 * t:16 * t + 16], S[:, h, cols(j, P)], router2[:, :], start=True, stop=True)
                last.then_inc(logits_ready, 1)

            def moe_up(it, n1, p):
                wait_last(pe, gelu_done[p], it)
                two_pass(pe, PS[:, HIDDEN_BANK[p]], "w1", p, S[:, :, bass.ds(it * N, N)]).then_inc(z_ready[p], 1)

            def moe_share(it, n1, p):
                if isinstance(it, int) and it % 2 == 0 and p == 0:
                    pe.wait_ge(ct_out, it // 2 + 1)
                wait_last(pe, hs_ready[(p + 2) % PAIRS], it if p < 2 else n1)
                for h in range(HALVES):
                    last = pe.matmul(PS[:, 1 + p % 2, cols(h, N)], part(WH, "sel", cols=cols(h * PAIRS + p, P)),
                                     CT[:, bass.ds(it * N, N)], start=True, stop=True)
                last.then_inc(cb_ready[p], 1)

            def moe_down(it, n1, p):
                if p == 0:
                    wait_last(pe, y_taken, it)
                pe.wait_ge(hs_ready[p], n1)
                for h in range(HALVES):
                    last = pe.matmul(PS[h * C:(h + 1) * C, 3, 0:N], pair("w2", p, n=C), HS[:, p, cols(h, N)], start=p == 0, stop=p == PAIRS - 1)
                if p == 0:
                    pe.matmul(PS[:, 3, 0:N], part(WH, "b2"), CT[:, bass.ds(it * N, N)], start=False, stop=False)
                    last = pe.matmul(PS[:, 3, 0:N], part(WL, "b2"), CT[:, bass.ds(it * N, N)], start=False, stop=False)
                last.then_inc(w2_done[p], 1)

            def moe_mix(i, up=False, last=False):
                it, n1 = it_values(pe, i)
                n2 = None if last else after(pe, n1)
                ahead = [it + AHEAD, it + AHEAD + 1] if isinstance(it, int) else [pe.snap(it + AHEAD), pe.snap(it + AHEAD + 1)]
                for p in range(PAIRS):
                    if up:
                        moe_up(*ahead, p)
                    if p < 2:
                        moe_share(it, n1, p + 2)
                    elif not last:
                        moe_share(n1, n2, p - 2)
                    moe_down(it, n1, p)

            route(0)
            pe.wait_ge(xc_copied, 2 * NQ)
            for p in range(PAIRS):
                moe_up(0, 1, p)
            for q in range(1, NQ):
                route(q)
            with pe.Fori(1, AHEAD) as i:
                it, n1 = it_values(pe, i)
                for p in range(PAIRS):
                    moe_up(it, n1, p)
            pe.wait_ge(combine_ready, 2)
            pe.wait_ge(ln_taken, 2 * NQ)
            for q in range(NQ):
                for j in range(4 * q, 4 * q + 4):
                    last = pe.transpose(PS[0:32, 1 + q, cols(j % 4, P)], combine2[:, 2 * j:2 * j + 2].rearrange("p t s e -> p (t s e)").bitcast(F32), w("ident"))
                last.then_inc(ct_ready, 1)
            pe.wait_ge(ct_out, 2)
            moe_share(0, 1, 0)
            moe_share(0, 1, 1)
            for it in range(BH - AHEAD):
                moe_mix(it, up=True)
            pe.wait_ge(ct_out, NQ)
            with pe.Fori(BH - AHEAD, BH - 1) as i:
                moe_mix(i)
            moe_mix(BH - 1, last=True)

            for p in range(PAIRS):
                pe.wait_ge(gelu_done[p], BH)
                pe.wait_ge(hs_ready[p], BH)
            ln_pe(pe, 2, lambda q: pe.wait_ge(y_taken, 2 * q + 2))
            for q in range(NQ):
                pe.wait_ge(t_ready, 2 * NQ + q + 1)
                if q >= 2:
                    pe.wait_ge(ek_exp, 2 * (q - 1))
                    pe.wait_ge(v_out, q - 1)
                pe.matmul(PS[0:4 * KD, 6 + q % 2], w("wkv"), T[:, cols(q)], start=True, stop=True).then_inc(kv_ready, 1)

            def queries(it):
                if it >= 2:
                    pe.wait_ge(q_biased, it - 1)
                for h in range(HALVES):
                    last = pe.matmul(PS[:, it % 2, cols(h, N)], w("wq", cols=cols(h, P)), T[:, cols(it, N)], start=True, stop=True)
                last.then_inc(q_ready, 1)

            pe.wait_ge(xc_copied, 3 * NQ)
            queries(0)
            queries(1)
            for g in range(2):
                pe.wait_ge(ek_ready, 2 * g + 2)
                pe.wait_ge(v_out, 2 * g + 2)
                for t in range(8):
                    last = pe.transpose(PS[:, 4 + g, cols(t, 4 * KD)], EKV[:, cols(8 * g + t, P)], w("ident", slice(0, 4 * KD), slice(0, 4 * KD)))
                last.then_inc(ekt_ready, 1)
            pe.wait_ge(ln_taken, 3 * NQ)
            for it in range(BH):
                if it % 4 == 0:
                    pe.wait_ge(ekt_out, it // 4 + 1)
                for jj in range(2):
                    tile = (2 * it + jj) * 4 * KD
                    last = pe.matmul(PS[0:32, 2, cols(it, 32)], EKVT[:, tile + 32:tile + 64], EKVT[:, tile:tile + 32], start=jj == 0, stop=jj == 1)
            last.then_inc(cx_ready, 1)
            pe.wait_ge(cx_out, 1)
            for h in range(HALVES):
                last = pe.matmul(PS[:, 3, cols(h, P)], w("to_heads", slice(0, 32), cols(h, P)),
                                 CTX[:, :].rearrange("p (b h d) -> p h b d", b=BH, h=HALVES)[:, h], start=True, stop=True)
            last.then_inc(heads_ready, 1)
            queries(2)
            for h in range(HALVES):
                pe.wait_ge(bd_ready, h + 1)
                for b in range(BH):
                    last = pe.matmul(PS[:, 4 + h, cols(b, C)], BD[:, h * BH + b], w("wo"), start=True, stop=True)
                last.then_inc(mb_ready, 1)
            queries(3)
            pe.wait_ge(mb_out, HALVES)
            pe.wait_ge(ek_exp, BH)
            for it in range(BH):
                pe.wait_ge(qs_ready, it + 1)
                if it >= 2:
                    pe.wait_ge(x3_ready, it - 1)
                for h in range(HALVES):
                    last = pe.matmul(PS[h * C:(h + 1) * C, 6 + it % 2, 0:N], MB[:, h, it], QS[:, it % 2, cols(h, N)], start=True, stop=True)
                last.then_inc(a_ready, 1)
                if it + 4 < BH:
                    queries(it + 4)

            ln_pe(pe, 3, lambda q: pe.wait_ge(x3_ready, 2 * q + 2))
            for jj in range(2):
                for b in range(BH):
                    pe.wait_ge(s_ready, 2 * NQ + 2 * (b // 2) + 2)
                    for h in range(HALVES):
                        last = pe.matmul(PS[:, 4, 16 * jj:16 * jj + 16], S[:, h, cols(2 * b + jj, P)], f_wr2[:, :],
                                         start=b == 0 and h == 0, stop=b == BH - 1 and h == 1)
            last.then_inc(fl_ready, 1)
            pe.wait_ge(fw_ready, 1)
            for jj in range(2):
                last = pe.transpose(PS[0:E, 5, cols(jj, P)], f_logits[:, jj], w("ident"))
            last.then_inc(ft_ready, 1)
            pe.wait_ge(ft_out, 1)
            for p in range(PAIRS):
                pe.matmul(PS[:, 6 + p // 2, cols(p % 2, N)], w("sel", slice(0, E), cols(p, P)), fT[:, :], start=True, stop=True).then_inc(fb_ready, 1)
            pe.wait_ge(fl_chain, 1)
            pe.matmul(PS[:, 4, 0:N], w("f_bo", slice(0, E)), fT[:, :], start=True, stop=True).then_inc(fb_ready, 1)

            def f_up(it, n1, p):
                wait_last(pe, h1_ready[(p + 2) % PAIRS], it if p < 2 else n1)
                two_pass(pe, PS[:, p % 2], "f_w1", p, S[:, :, bass.ds(it * N, N)]).then_inc(z1_ready[p], 1)

            def f_mid(it, n1, p):
                pe.wait_ge(h1_ready[p], n1)
                wait_last(pe, h2_ready[(p + 2) % PAIRS], it if p < 2 else n1)
                pe.matmul(PS[:, 2 + p % 2], pair("f_w2", p), H1[:, p], start=True, stop=True).then_inc(z2_ready[p], 1)

            def f_down(it, n1, p):
                if p == 0:
                    wait_last(pe, x4_ready, it)
                pe.wait_ge(hw_ready[p], n1)
                for h in range(HALVES):
                    last = pe.matmul(PS[h * C:(h + 1) * C, 4, 0:N], pair("f_wo", p, n=C), HW[:, p, cols(h, N)], start=p == 0, stop=p == PAIRS - 1)
                last.then_inc(wo_done[p], 1)

            def f_body(i, last=False):
                it, n1 = it_values(pe, i)
                n2 = None if last else after(pe, n1)
                f_up(it, n1, 2)
                f_mid(it, n1, 1)
                f_down(it, n1, 0)
                f_up(it, n1, 3)
                f_mid(it, n1, 2)
                f_down(it, n1, 1)
                if not last:
                    f_up(n1, n2, 0)
                f_mid(it, n1, 3)
                f_down(it, n1, 2)
                if not last:
                    f_up(n1, n2, 1)
                    f_mid(n1, n2, 0)
                f_down(it, n1, 3)

            pe.wait_ge(ln_taken, 4 * NQ)
            pe.wait_ge(xc_copied, 4 * NQ)
            pe.wait_ge(fb_out, PAIRS + 1)
            f_up(0, 1, 0)
            f_up(0, 1, 1)
            f_mid(0, 1, 0)
            f_body(0)
            with pe.Fori(1, BH - 1) as i:
                f_body(i)
            f_body(BH - 1, last=True)

        @block.scalar
        def _(act):
            act.preload_act_table_set("natural_log_exp_and_others")
            act.wait_ge(w_in, 16)
            ln_act(act, 0, 0)
            for q in range(NQ):
                act.wait_ge(t_ready, q + 1)
                act.activation(AB[:, cols(q)], T[:, cols(q)], ACT.Abs, scale=SCALE).then_inc(abs_ready, 1)
            act.wait_ge(padded_zero, 1)
            for q in range(NQ):
                act.wait_ge(taps_ready, q + 1)
                act.activation(TH[32:40, cols(q)], PS[32:40, 4 + q % 2], ACT.Relu, bias=w("tp_b1", slice(32, 40))).then_inc(th_out, 1)
                act.activation(padded_maps(PADDED[:, LEAD:LEAD + FLAT], q), maps(PS[0:18, 4 + q % 2]), ACT.Copy).then_inc(taps_out, 1)
                act.wait_ge(rel_ready, q + 1)
                act.activation(REL[:, cols(q)], PS[:, 6 + q % 2], ACT.Sigmoid, bias=w("tp_b2")).then_inc(rel_out, 1)
            act.wait_ge(ca1_ready, 1)
            act.activation(ca_h[:, :], PS[0:8, 0, 0:BH], ACT.Relu, bias=w("ca_b1", slice(0, 8)), scale=1.0 / N).then_inc(ca1_out, 1)
            act.wait_ge(ca2_ready, 1)
            act.activation(CW[:, :], PS[:, 1, 0:BH], ACT.Sigmoid, bias=w("ca_b2")).then_inc(cw_ready, 1)
            for q in range(NQ):
                act.wait_ge(sw_ready, q + 1)
                act.activation(SW[:, cols(q)], PS[:, 4 + q % 4], ACT.Sigmoid, bias=w("sa_b")).then_inc(sw_out, 1)
            act.wait_ge(rounded_ready, 1)
            act.wait_ge(var_ready, NQ)
            with act.Fori(0, VALUE_BITS) as r0:
                r = act.snap(r0)
                act.wait_ge(thr_ready, r + 1)
                with nc.allow_low_precision(reason="whole numbers up to 2048"):
                    act.activation(SQ[:, 0:ACT_COLS], QT[:, DVE_COLS:COLS], ACT.Sigmoid, bias=thr[:, 0:1], scale=-1.0,
                                   accum_out=counts[:, 1:2]).then_inc(act_counted, 1)
            act.wait_ge(top_ready, 1)
            with nc.allow_low_precision(reason="whole numbers up to 2048"):
                act.activation(SQ[:, :], QT[:, :], ACT.Sigmoid, bias=thr_top[:, 0:1], scale=-1.0,
                               accum_out=counts[:, 1:2]).then_inc(top_counted, 1)
            for q in range(NQ):
                act.wait_ge(diff_ready, 2 * q + 2)
                act.activation(AB[:, cols(q)], AB[:, cols(q)], ACT.Sigmoid, scale=10.0 / SCALE).then_inc(mask_ready, 1)

            act.preload_act_table_set("natural_log_exp_and_others")
            act.wait_ge(top_counted, 1)
            ln_split_act(act, 1, 1)
            act.preload_act_table(ACT.Gelu)

            def moe_gelu(i):
                it, n1 = it_values(act, i)
                for p in range(PAIRS):
                    act.wait_ge(z_ready[p], n1)
                    act.activation(HID[:, bass.ds(it * COLS + p * Q, Q)], PS[:, HIDDEN_BANK[p]], ACT.Gelu, bias=w("b1", cols=slice(p, p + 1))).then_inc(gelu_done[p], 1)

            with act.Fori(0, SHARES_AT) as i:
                moe_gelu(i)
            act.wait_ge(lead_ready, 1)
            act.activation(lead[:, :], lead[:, :], ACT.Tanh, scale=0.5).then_inc(tanh_ready, 1)
            with act.Fori(SHARES_AT, BH) as i:
                moe_gelu(i)

            act.preload_act_table_set("natural_log_exp_and_others")
            for q in range(NQ + 3):
                if q < NQ:
                    ln_act_square(act, 2, q)
                if 1 <= q <= NQ:
                    ln_act_rstd(act, 2, q - 1, 0)
                if q >= 3:
                    r = q - 3
                    act.wait_ge(kv_ready, r + 1)
                    act.activation(EKV[32:64, cols(r)], PS[32:64, 6 + r % 2], ACT.Identity, bias=w("kv_bias", slice(32, 64))).then_inc(v_out, 1)
                    act.wait_ge(kb_chain, 2 * r + 2)
                    for b in (2 * r, 2 * r + 1):
                        act.activation(EKV[0:32, cols(b, N)], PS[0:32, 6 + r % 2, cols(b % 2, N)], ACT.Exp, bias=kbias[:, b:b + 1],
                                       accum_out=ksum[:, b:b + 1]).then_inc(ek_exp, 1)

            def queries_out(it):
                act.wait_ge(q_ready, it + 1)
                if it >= 2:
                    act.wait_ge(qb_ready, it - 1)
                act.activation(Q0[:, it % 2], PS[:, it % 2], ACT.Identity, bias=w("bq")).then_inc(q_biased, 1)

            def queries_exp(it):
                act.wait_ge(qsub_ready, it + 1)
                act.activation(QB[:, it % 4], QB[:, it % 4], ACT.Exp).then_inc(qexp_ready, 1)

            queries_out(0)
            queries_out(1)
            for g in range(2):
                act.wait_ge(ekt_ready, g + 1)
                act.activation(EKVT[:, cols(g)], PS[:, 4 + g], ACT.Copy).then_inc(ekt_out, 1)
            queries_exp(0)
            act.wait_ge(cx_ready, 1)
            act.activation(CTX[:, :], PS[0:32, 2, 0:N], ACT.Copy).then_inc(cx_out, 1)
            queries_out(2)
            queries_exp(1)
            for h in range(HALVES):
                act.wait_ge(mb_ready, h + 1)
                act.activation(MB[:, h], PS[:, 4 + h].rearrange("p (b c) -> p b c", b=BH), ACT.Copy).then_inc(mb_out, 1)
            queries_out(3)
            for it in range(2, BH):
                queries_exp(it)
                if it + 2 < BH:
                    queries_out(it + 2)

            act.wait_ge(late_in, 16)
            act.activation(bn_a[:, :], w("bn_v"), ACT.Ln, bias=w("eps", cols=slice(2, 3))).then_inc(bn_rs, 1)
            act.wait_ge(bn_rs, 1)
            act.activation(bn_a[:, :], bn_a[:, :], ACT.Exp, scale=-0.5).then_inc(bn_rs, 1)
            ln_split_act(act, 3, 1)
            act.wait_ge(fl_chain, 5)
            act.activation(f_logits[:, :], f_logits[:, :], ACT.Exp).then_inc(fe_ready, 1)
            act.wait_ge(ft_ready, 1)
            act.activation(fT[:, :], PS[0:E, 5, 0:N], ACT.Copy).then_inc(ft_out, 1)
            for p in range(PAIRS):
                act.wait_ge(fb_ready, p + 1)
                if p % 2 == 0:
                    act.wait_ge(fb_ready, p + 2)
                act.activation(FW[:, p], PS[:, 6 + p // 2, cols(p % 2, N)], ACT.Copy).then_inc(fb_out, 1)
            act.wait_ge(fb_ready, PAIRS + 1)
            act.activation(FB[:, :], PS[:, 4, 0:N], ACT.Copy).then_inc(fb_out, 1)

            def bn_relu(out, bank, p, layer):
                n = layer * PAIRS + p
                return act.activation(out, PS[:, bank + p % 2], ACT.Relu, bias=bn_c[:, n:n + 1], scale=bn_a[:, n:n + 1])

            def f_h1(it, n1, p):
                act.wait_ge(z1_ready[p], n1)
                wait_last(act, z2_ready[p], it)
                bn_relu(H1[:, p], 0, p, 0).then_inc(h1_ready[p], 1)

            def f_h2(it, n1, p):
                act.wait_ge(z2_ready[p], n1)
                wait_last(act, hw_ready[p], it)
                bn_relu(H2[:, p], 2, p, 1).then_inc(h2_ready[p], 1)

            def f_act_body(i, last=False):
                it, n1 = it_values(act, i)
                f_h1(it, n1, 2)
                f_h2(it, n1, 1)
                f_h1(it, n1, 3)
                f_h2(it, n1, 2)
                n2 = None if last else after(act, n1)
                if not last:
                    f_h1(n1, n2, 0)
                f_h2(it, n1, 3)
                if not last:
                    f_h1(n1, n2, 1)
                    f_h2(n1, n2, 0)

            act.wait_ge(bn_chain, 3)
            act.wait_ge(hs_ready[3], BH)
            f_h1(0, 1, 0)
            f_h1(0, 1, 1)
            f_h2(0, 1, 0)
            f_act_body(0)
            with act.Fori(1, BH - 1) as i:
                f_act_body(i)
            f_act_body(BH - 1, last=True)

        @block.vector
        def _(dve):
            chain = Chain(dve, chain_v)
            dve.wait_ge(w_in, 16)
            ln_dve(dve, 0)
            dve.wait_ge(t_ready, NQ)
            dve.tensor_reduce(pooled[:, :], T[:, :].rearrange("p (b n) -> p b n", b=BH), AX_X, ALU.add).then_inc(pooled_ready, 1)
            dve.wait_ge(q_in, 16 * B)
            dve.tensor_scalar(QT[:, :], QT[:, :], TOP, TOP, ALU.add, ALU.subtract).then_inc(rounded_ready, 1)
            dve.memset(step[:, :], TOP).then_inc(chain_v, 1)
            dve.wait_ge(chain_v, 1)
            dve.memset(thr[:, :], TOP / 2 - STEP / 2).then_inc(thr_ready, 1)
            dve.tensor_copy(group16[:, :], w("group")).then_inc(group_ready, 1)
            dve.wait_ge(rounded_ready, 1)
            dve.wait_ge(xc_copied, NQ)

            def count_below(n):
                dve.wait_ge(thr_ready, n)
                with nc.allow_low_precision(reason="whole numbers up to 2048"):
                    dve.tensor_scalar(XC[:, 0:DVE_COLS], QT[:, 0:DVE_COLS], thr[:, 0:1], None, ALU.is_lt, ALU.add,
                                      accum_out=counts[:, 0:1]).then_inc(dve_counted, 1)
                dve.tensor_scalar(step[:, :], step[:, :], 0.5, None, ALU.mult).then_inc(step_ready, 1)
                dve.wait_ge(step_ready, n)
                dve.scalar_tensor_tensor(thr_half[:, :], step[:, :], -0.5, thr[:, :], ALU.mult, ALU.add).then_inc(half_ready, 1)

            def set_bit(n):
                dve.wait_ge(counted, n)
                dve.tensor_scalar(bit[:, :], PS[:, 0, 0:1], PS[:, 0, 1:2], C * N - RANK + 0.5, ALU.add, ALU.is_lt).then_inc(bit_ready, 1)
                dve.wait_ge(bit_ready, n)
                dve.wait_ge(half_ready, n)
                dve.scalar_tensor_tensor(thr[:, :], bit[:, :], step[:, 0:1], thr_half[:, :], ALU.mult, ALU.add).then_inc(thr_ready, 1)

            count_below(1)
            with dve.Fori(1, VALUE_BITS) as r0:
                r = dve.snap(r0)
                set_bit(r)
                count_below(dve.snap(r + 1))
            set_bit(VALUE_BITS)
            dve.wait_ge(thr_ready, VALUE_BITS + 1)
            dve.tensor_scalar(thr_top[:, :], thr[:, :], STEP / 2, None, ALU.add).then_inc(top_ready, 1)
            dve.tensor_scalar(XC[:, :], QT[:, :], thr[:, 0:1], None, ALU.is_gt).then_inc(chain_v, 1)
            dve.wait_ge(chain_v, 2)
            dve.wait_ge(comp_ready, 1)
            dve.tensor_tensor_reduce(out=XC[:, :], in0=XC[:, :], in1=QX[:, :], scale=1.0, scalar=0.0, op0=ALU.mult, op1=ALU.max,
                                     accum_out=above[:, :]).then_inc(chain_v, 1)
            dve.wait_ge(chain_v, 3)
            dve.tensor_scalar(above8[:, :], w("mask8"), above[:, 0:1], None, ALU.mult).then_inc(above_ready, 1)
            dve.wait_ge(above_spread, 1)
            dve.reduce_max(above[:, :], PS[:, 1, 0:8], AX_X).then_inc(chain_v, 1)
            dve.wait_ge(chain_v, 4)
            dve.tensor_scalar(upper[:, :], above[:, :], -1.0, TOP, ALU.mult, ALU.add).then_inc(chain_v, 1)
            dve.wait_ge(top_summed, 1)
            dve.tensor_scalar(flag[:, :], PS[:, 0, 1:2], C * N - RANK + 1.5, None, ALU.is_lt).then_inc(chain_v, 1)
            dve.wait_ge(chain_v, 6)
            dve.tensor_tensor(upper[:, :], upper[:, :], thr[:, :], ALU.subtract).then_inc(chain_v, 1)
            dve.wait_ge(chain_v, 7)
            dve.scalar_tensor_tensor(upper[:, :], upper[:, :], flag[:, 0:1], thr[:, :], ALU.mult, ALU.add).then_inc(chain_v, 1)
            dve.tensor_scalar(gt[:, :], thr[:, :], W_LOW, None, ALU.mult).then_inc(chain_v, 1)
            dve.wait_ge(chain_v, 9)
            dve.scalar_tensor_tensor(gt[:, :], upper[:, :], W_HIGH, gt[:, :], ALU.mult, ALU.add).then_inc(chain_v, 1)
            dve.wait_ge(chain_v, 10)
            dve.tensor_scalar(gt8[:, :], w("gt_sel"), gt[:, 0:1], None, ALU.mult).then_inc(gt_ready, 1)
            dve.wait_ge(gt_spread, 1)
            dve.tensor_scalar(neg_gt[:, :], PS[:, 2, 0:BH], -1.0, None, ALU.mult).then_inc(top_used, 1)
            dve.wait_ge(top_used, 1)
            dve.wait_ge(rel_out, NQ)
            dve.wait_ge(q_in, 16 * B)
            for b in range(BH):
                c = cols(b, N)
                dve.scalar_tensor_tensor(AB[:, c], REL[:, c], neg_gt[:, b:b + 1], AB[:, c], ALU.mult, ALU.add).then_inc(diff_ready, 1)
            dve.wait_ge(u_ready, NQ)
            for q in range(NQ):
                dve.wait_ge(mask_ready, q + 1)
                dve.tensor_tensor(U[:, cols(q)], U[:, cols(q)], AB[:, cols(q)], ALU.mult).then_inc(gated_ready, 1)

            ln_split_dve(dve, 1)
            dve.wait_ge(logits_ready, NQ)
            top = Chain(dve, top_v)

            def by_token(ap, n=E):
                return ap[:, :].unsqueeze(2).to_broadcast([P, TILES, n])

            rank = w("expert_rank").unsqueeze(1).to_broadcast([P, TILES, E])
            top(dve.tensor_reduce(logits[:, :, :], PS[:, 4].rearrange("p (t s e) -> p t e s", s=2, e=E), AX_X, ALU.add))
            for n, (m, chosen) in enumerate(((best, is_best), (second, is_second))):
                top.wait()
                top(dve.reduce_max(m[:, :], logits[:, :, :], AX_X))
                top.wait()
                top(dve.tensor_tensor(key[:, :, :], logits[:, :, :], by_token(m), ALU.is_equal))
                top.wait()
                top(dve.tensor_tensor(key[:, :, :], key[:, :, :], rank, ALU.mult))
                top.wait()
                top(dve.reduce_max(key_max[:, :], key[:, :, :], AX_X))
                top.wait()
                top(dve.tensor_tensor(chosen[:, :, :], by_token(key_max), rank, ALU.is_equal))
                top.wait()
                if n == 0:
                    top(dve.scalar_tensor_tensor(logits[:, :, :], chosen[:, :, :], -1e30, logits[:, :, :], ALU.mult, ALU.add))
            dve.tensor_tensor(lead[:, :], best[:, :], second[:, :], ALU.subtract).then_inc(lead_ready, 1)
            dve.wait_ge(tanh_ready, 1)
            top(dve.tensor_scalar(share1[:, :], lead[:, :], 0.5, 0.5, ALU.mult, ALU.add))
            top(dve.tensor_scalar(share2[:, :], lead[:, :], -0.5, 0.5, ALU.mult, ALU.add))
            top.wait()
            top(dve.tensor_tensor(combine[:, :, :], is_best[:, :, :], by_token(share1), ALU.mult))
            top.wait()
            top(dve.tensor_tensor(is_second[:, :, :], is_second[:, :, :], by_token(share2), ALU.mult))
            top.wait()
            top(dve.tensor_tensor(combine[:, :, :], combine[:, :, :], is_second[:, :, :], ALU.add))
            top.wait()
            dve.tensor_copy(combine2[:, :, 0], combine[:, :, :]).then_inc(combine_ready, 1)
            dve.wait_ge(combine_ready, 1)
            dve.tensor_tensor(combine2[:, :, 1], combine[:, :, :], combine2[:, :, 0].bitcast(F32), ALU.subtract).then_inc(combine_ready, 1)
            dve.wait_ge(rows_zero, 1)
            for q in range(NQ):
                dve.wait_ge(ct_ready, q + 1)
                dve.tensor_copy(CT[0:32, cols(q)], PS[0:32, 1 + q]).then_inc(ct_out, 1)

            def moe_scale(it, n1, p):
                dve.wait_ge(gelu_done[p], n1)
                dve.wait_ge(cb_ready[p], n1)
                wait_last(dve, w2_done[p], it)
                dve.tensor_tensor(HS[:, p], HID[:, bass.ds(it * COLS + p * Q, Q)], PS[:, 1 + p % 2], ALU.mult).then_inc(hs_ready[p], 1)

            def moe_add(it, n1):
                dve.wait_ge(w2_done[PAIRS - 1], n1)
                x_it = X[:, bass.ds(it * N, N)]
                dve.tensor_tensor(x_it, PS[:, 3, 0:N], x_it, ALU.add).then_inc(y_taken, 1)

            dve.wait_ge(x_added, NQ)
            for p in range(PAIRS):
                moe_scale(0, 1, p)
            with dve.Fori(1, BH) as i:
                it, n1 = it_values(dve, i)
                moe_scale(it, n1, 0)
                moe_add(dve.snap(it - 1), it)
                moe_scale(it, n1, 1)
                moe_scale(it, n1, 2)
                moe_scale(it, n1, 3)
            moe_add(BH - 1, BH)

            for q in range(NQ + 4):
                if q < NQ:
                    ln_dve_copy(dve, 2, q)
                if 2 <= q < NQ + 2:
                    ln_dve_scale(dve, 2, q - 2, lambda _: dve.wait_ge(x_added, NQ))
                if 3 <= q < NQ + 3:
                    r = q - 3
                    dve.wait_ge(kv_ready, r + 1)
                    dve.reduce_max(kmax[:, 2 * r:2 * r + 2], PS[0:32, 6 + r % 2].rearrange("p (b n) -> p b n", b=2), AX_X).then_inc(kmax_ready, 1)
                    dve.wait_ge(kmax_ready, r + 1)
                    dve.tensor_scalar(kmax[:, 2 * r:2 * r + 2], kmax[:, 2 * r:2 * r + 2], w("kv_bias", slice(0, 32)), None, ALU.add).then_inc(kb_chain, 1)
                    dve.wait_ge(kb_chain, 2 * r + 1)
                    dve.tensor_scalar(kbias[:, 2 * r:2 * r + 2], kmax[:, 2 * r:2 * r + 2], -1.0, w("kv_bias", slice(0, 32)), ALU.mult, ALU.add).then_inc(kb_chain, 1)
                if q >= 4:
                    r = q - 4
                    dve.wait_ge(ek_exp, 2 * r + 2)
                    dve.reciprocal(krec[:, 2 * r:2 * r + 2], ksum[:, 2 * r:2 * r + 2]).then_inc(krec_ready, 1)
                    dve.wait_ge(krec_ready, r + 1)
                    ek = EKV[0:32, cols(r)].rearrange("p (b n) -> p b n", b=2)
                    dve.tensor_tensor(ek, ek, krec[:, 2 * r:2 * r + 2].unsqueeze(2).to_broadcast([32, 2, N]), ALU.mult).then_inc(ek_ready, 1)

            def by_head(ap):
                return ap.rearrange("p (g d) -> p g d", d=KD)

            def queries_max(it):
                dve.wait_ge(q_biased, it + 1)
                if it >= 4:
                    dve.wait_ge(qs_ready, it - 3)
                dve.transpose(QB[:, it % 4], Q0[:, it % 2]).then_inc(qb_ready, 1)
                dve.wait_ge(qb_ready, it + 1)
                if it >= 2:
                    dve.wait_ge(qsub_ready, it - 1)
                dve.reduce_max(qmax[:, it % 2], by_head(QB[:, it % 4]), AX_X).then_inc(qmax_ready, 1)

            def queries_sum(it):
                dve.wait_ge(qexp_ready, it + 1)
                dve.tensor_reduce(qsum[:, it % 2], by_head(QB[:, it % 4]), AX_X, ALU.add).then_inc(qsum_ready, 1)
                dve.wait_ge(qsum_ready, it + 1)
                if it >= 2:
                    dve.wait_ge(qn_ready, it - 1)
                dve.reciprocal(qrec[:, it % 2], qsum[:, it % 2]).then_inc(qrec_ready, 1)

            def queries_back(it):
                dve.wait_ge(qn_ready, it + 1)
                if it >= 2:
                    dve.wait_ge(a_ready, it - 1)
                dve.transpose(QS[:, it % 2], QB[:, it % 4]).then_inc(qs_ready, 1)

            def attn_add(it):
                dve.wait_ge(a_ready, it + 1)
                dve.scalar_tensor_tensor(X[:, cols(it, N)], PS[:, 6 + it % 2, 0:N], w("bo"), X[:, cols(it, N)], ALU.add, ALU.add).then_inc(x3_ready, 1)

            for s in range(BH + 3):
                if s < BH:
                    queries_max(s)
                if s == 1:
                    dve.wait_ge(heads_ready, 1)
                    for h in range(HALVES):
                        dve.tensor_tensor(BD[:, h * BH:(h + 1) * BH].rearrange("p b (g d) -> p b g d", d=KD),
                                          PS[:, 3, cols(h, P)].rearrange("p (b d) -> p b d", b=BH).unsqueeze(2).to_broadcast([P, BH, HEADS, KD]),
                                          w("head_mask").rearrange("p (g d) -> p g d", d=KD).unsqueeze(1).to_broadcast([P, BH, HEADS, KD]),
                                          ALU.mult).then_inc(bd_ready, 1)
                if 1 <= s < BH + 1:
                    queries_sum(s - 1)
                if 2 <= s < BH + 2:
                    queries_back(s - 2)
                if s >= 3:
                    attn_add(s - 3)

            dve.wait_ge(bn_rs, 2)
            dve.tensor_tensor(bn_a[:, :], bn_a[:, :], w("bn_g"), ALU.mult).then_inc(bn_chain, 1)
            dve.tensor_tensor(bn_c[:, :], w("bn_b"), w("bn_m"), ALU.subtract).then_inc(bn_chain, 1)
            dve.wait_ge(bn_chain, 2)
            dve.tensor_tensor(bn_c[:, :], bn_c[:, :], bn_a[:, :], ALU.mult).then_inc(bn_chain2, 1)
            dve.wait_ge(bn_chain2, 1)
            dve.tensor_tensor(bn_c[:, :], bn_c[:, :], w("bn_be"), ALU.add).then_inc(bn_chain, 1)
            ln_split_dve(dve, 3, lambda _: dve.wait_ge(q_ready, BH))
            f = Chain(dve, fl_chain)
            dve.wait_ge(fl_ready, 1)
            f(dve.tensor_reduce(f_logits[:, :, :], PS[:, 4, 0:32].rearrange("p (t s e) -> p t e s", s=2, e=E), AX_X, ALU.add))
            f.wait()
            br = w("f_br").unsqueeze(1).to_broadcast([P, 2, E])
            f(dve.tensor_scalar(f_logits[:, :, :], f_logits[:, :, :], 1.0 / B, None, ALU.mult))
            f.wait()
            f(dve.tensor_tensor(f_logits[:, :, :], f_logits[:, :, :], br, ALU.add))
            f.wait()
            f(dve.reduce_max(f_max[:, :], f_logits[:, :, :], AX_X))
            f.wait()
            f(dve.tensor_tensor(f_logits[:, :, :], f_logits[:, :, :], f_max[:, :].unsqueeze(2).to_broadcast([P, 2, E]), ALU.subtract))
            dve.wait_ge(fe_ready, 1)
            f(dve.reduce_sum(f_sum[:, :], f_logits[:, :, :], AX_X))
            f.wait()
            f(dve.reciprocal(f_sum[:, :], f_sum[:, :]))
            f.wait()
            dve.tensor_tensor(f_logits[:, :, :], f_logits[:, :, :], f_sum[:, :].unsqueeze(2).to_broadcast([P, 2, E]), ALU.mult).then_inc(fw_ready, 1)

            def f_scale(it, n1, p):
                dve.wait_ge(h2_ready[p], n1)
                wait_last(dve, wo_done[p], it)
                dve.tensor_tensor(HW[:, p].rearrange("p (h n) -> p h n", h=HALVES), H2[:, p].rearrange("p (h n) -> p h n", h=HALVES),
                                  FW[:, p].unsqueeze(1).to_broadcast([P, HALVES, N]), ALU.mult).then_inc(hw_ready[p], 1)

            def f_add(it, n1):
                dve.wait_ge(wo_done[PAIRS - 1], n1)
                x_it = X[:, bass.ds(it * N, N)]
                dve.tensor_tensor(x_it, PS[:, 4, 0:N], x_it, ALU.add).then_inc(x4_ready, 1)

            dve.wait_ge(fb_out, PAIRS + 1)
            dve.wait_ge(bias_added, NQ)
            for p in range(PAIRS):
                dve.wait_ge(w2_done[p], BH)
            for p in range(PAIRS):
                f_scale(0, 1, p)
            with dve.Fori(1, BH) as i:
                it, n1 = it_values(dve, i)
                f_add(dve.snap(it - 1), it)
                f_scale(it, n1, 0)
                f_scale(it, n1, 1)
                f_scale(it, n1, 2)
                f_scale(it, n1, 3)
            f_add(BH - 1, BH)

        @block.gpsimd
        def _(pool):
            pool.memset(PADDED[:, :], 0.0).then_inc(padded_zero, 1)
            pool.memset(CT[:, :].bitcast(F32), 0.0).then_inc(rows_zero, 1)
            pool.wait_ge(rounded_ready, 1)
            pool.tensor_scalar(QX[:, :], QT[:, :], -1.0, TOP, ALU.mult, ALU.add).then_inc(comp_ready, 1)
            pool.wait_ge(late_in, 16)
            pool.tensor_copy(WH[:, :], WT[:, SPLIT0:SPLIT1]).then_inc(split_high, 1)
            pool.wait_ge(split_high, 1)
            pool.tensor_tensor(WL[:, :], WT[:, SPLIT0:SPLIT1], WH[:, :].bitcast(F32), ALU.subtract).then_inc(split_low, 1)
            pool.wait_ge(split_low, 1)
            for both, name in ((router2, "router"), (f_wr2, "f_wr")):
                pool.tensor_copy(both[:, 0:E], part(WH, name))
                last = pool.tensor_copy(both[:, E:2 * E], part(WL, name))
            last.then_inc(split_low, 1)
            pool.wait_ge(cw_ready, 1)
            pool.wait_ge(t_ready, NQ)
            pool.wait_ge(sw_out, NQ)
            for q in range(NQ):
                pool.tensor_tensor(U[:, cols(q)].rearrange("p (b n) -> p b n", n=N), T[:, cols(q)].rearrange("p (b n) -> p b n", n=N),
                                   CW[:, 2 * q:2 * q + 2].unsqueeze(2).to_broadcast([P, 2, N]), ALU.mult).then_inc(chain_g, 1)
                pool.wait_ge(chain_g, q + 1)
                pool.tensor_tensor(U[:, cols(q)], U[:, cols(q)], SW[:, cols(q)], ALU.mult).then_inc(u_ready, 1)
            for q in range(NQ):
                ln_pool_square(pool, 1, q)
            for q in range(NQ):
                pool.tensor_tensor(X[:, cols(q)], X[:, cols(q)], U[:, cols(q)], ALU.add).then_inc(x1_ready, 1)
            for q in range(NQ):
                pool.wait_ge(t_ready, NQ + q + 1)
                pool.wait_ge(x1_ready, q + 1)
                pool.tensor_tensor(X[:, cols(q)], X[:, cols(q)], T[:, cols(q)], ALU.add).then_inc(x_added, 1)
            for s in range(BH + 1):
                if s < BH:
                    pool.wait_ge(qmax_ready, s + 1)
                    q3 = QB[:, s % 4].rearrange("p (g d) -> p g d", d=KD)
                    pool.tensor_tensor(q3, q3, qmax[:, s % 2].unsqueeze(2).to_broadcast([P, 32, KD]), ALU.subtract).then_inc(qsub_ready, 1)
                if s >= 1:
                    pool.wait_ge(qrec_ready, s)
                    q3 = QB[:, (s - 1) % 4].rearrange("p (g d) -> p g d", d=KD)
                    pool.tensor_tensor(q3, q3, qrec[:, (s - 1) % 2].unsqueeze(2).to_broadcast([P, 32, KD]), ALU.mult).then_inc(qn_ready, 1)
            for q in range(NQ):
                ln_pool_square(pool, 3, q)
            pool.wait_ge(fb_out, PAIRS + 1)
            for q in range(NQ):
                pool.wait_ge(xc_ready, 3 * NQ + q + 1)
                pool.wait_ge(x3_ready, BH)
                x_q = X[:, cols(q)].rearrange("p (b n) -> p b n", n=N)
                pool.tensor_tensor(x_q, x_q, FB[:, :].unsqueeze(1).to_broadcast([P, 2, N]), ALU.add).then_inc(bias_added, 1)


def pack_weights(v):
    a = np.zeros((P, NCOL), np.float32)

    def put(name, rows, value, cols=slice(None)):
        lo, hi = AT[name]
        a[rows, lo:hi][:, cols] = value

    half = [slice(0, C), slice(C, P)]
    eye = np.eye(C, dtype=np.float32)
    put("eps", slice(None), np.array([1e-6, 1e-5, 1e-3, 0], np.float32))
    put("ident", slice(None), np.eye(P, dtype=np.float32))
    group = np.kron(np.eye(P // GROUP), np.ones((GROUP, GROUP))).astype(np.float32)
    put("group", slice(None), group)
    put("mask8", slice(None), np.tile(np.eye(8), (P // 8, 1)))
    put("gt_sel", slice(None), np.tile(np.kron(np.eye(BH), np.full((GROUP, 1), 8.0)), (HALVES, 1)))
    for h, rows in enumerate(half):
        put("center", rows, eye - 1 / C, slice(h * C, (h + 1) * C))
        put("mean", rows, 1 / C, slice(h * C, (h + 1) * C))
        put("tap_th", rows, v["L0_conv_sa_w"].reshape(C, TAPS), slice(h * TAPS, (h + 1) * TAPS))
        put("tap_th", rows, v["L0_conv_tp_w1"].T, slice(32 + h * CR, 32 + (h + 1) * CR))
        put("tp_b1", slice(32 + h * CR, 32 + (h + 1) * CR), v["L0_conv_tp_b1"][:, None])
        put("tp_w2", slice(32 + h * CR, 32 + (h + 1) * CR), v["L0_conv_tp_w2"].T, slice(h * C, (h + 1) * C))
        put("tap_sum", slice(h * TAPS, (h + 1) * TAPS), 1.0, slice(h * C, (h + 1) * C))
        put("ca_w1", rows, v["L0_conv_ca_w1"].T, slice(h * CR, (h + 1) * CR))
        put("ca_b1", slice(h * CR, (h + 1) * CR), v["L0_conv_ca_b1"][:, None])
        put("ca_w2", slice(h * CR, (h + 1) * CR), v["L0_conv_ca_w2"].T, slice(h * C, (h + 1) * C))
        put("ca_b2", rows, v["L0_conv_ca_b2"][:, None])
        put("router", rows, v["L0_ffn_router_w"].T)
        put("f_wr", rows, v["L1_ffn_Wr"])
        put("w1", rows, v["L0_ffn_w1"].transpose(1, 0, 2).reshape(C, E * C))
        put("f_w1", rows, v["L1_ffn_W1"].transpose(1, 0, 2).reshape(C, E * C))
        for part in range(2):
            for e in range(E):
                row = slice(16 * h + E * part + e, 16 * h + E * part + e + 1)
                put("sel", row, 1.0, slice((h * PAIRS + e // 2) * P + e % 2 * C, (h * PAIRS + e // 2) * P + e % 2 * C + C))
                put("b2", row, v["L0_ffn_b2"][e], slice(h * C, (h + 1) * C))
        put("wq", rows, v["L1_conv_Wq"].T, slice(h * P, (h + 1) * P))
        for part, (k_w, k_b) in enumerate((("L1_conv_Wk", "L1_conv_bk"), ("L1_conv_Wv", "L1_conv_bv"))):
            at = slice((2 * part + h) * KD, (2 * part + h + 1) * KD)
            put("wkv", rows, v[k_w].T, at)
            put("kv_bias", at, v[k_b][:, None])
        put("to_heads", slice(h * KD, (h + 1) * KD), np.tile(np.eye(KD), (1, HEADS)), slice(h * P, (h + 1) * P))
        put("bo", rows, v["L1_conv_bo"][:, None])
        put("f_bo", slice(0, E), v["L1_ffn_bo"], slice(h * C, (h + 1) * C))

    def pairs(x):
        return x.reshape(PAIRS, P).T

    put("tp_b2", slice(None), v["L0_conv_tp_b2"][0])
    put("sa_b", slice(None), v["L0_conv_sa_b"][0])
    put("ident2", slice(None), np.eye(P))
    put("bq", slice(None), v["L1_conv_bq"][:, None])
    put("b1", slice(None), pairs(v["L0_ffn_b1"]))
    put("expert_rank", slice(None), np.arange(E, 0, -1))
    put("w2", slice(None), v["L0_ffn_w2"].reshape(PAIRS, P, C).transpose(1, 0, 2).reshape(P, PAIRS * C))
    put("wo", slice(None), v["L1_conv_Wo"].T)
    put("head_mask", slice(None), np.kron(np.eye(HEADS), np.ones((KD, KD))))
    for name, k in (("bn_g", "g"), ("bn_b", "b"), ("bn_be", "be"), ("bn_m", "m"), ("bn_v", "v")):
        for layer in range(2):
            put(name, slice(None), pairs(v[f"L1_ffn_{k}{layer + 1}"]), slice(layer * PAIRS, (layer + 1) * PAIRS))
    for e in range(E):
        rows = half[e % 2]
        put("f_w2", rows, v["L1_ffn_W2"][e], slice(e * C, (e + 1) * C))
    put("f_wo", slice(None), v["L1_ffn_Wo"].reshape(PAIRS, P, C).transpose(1, 0, 2).reshape(P, PAIRS * C))
    put("f_br", slice(None), v["L1_ffn_br"])
    return a


def kernel(**inputs):
    import concourse.bacc as bacc
    from concourse.bass_utils import run_bass_kernel_spmd

    v = {k: np.asarray(a) for k, a in inputs.items()}
    arrays = {"in_x": np.ascontiguousarray(v["x"]), "in_weights": pack_weights(v)}
    nc = bacc.Bacc("TRN2", target_bir_lowering=False, num_devices=1)
    aps = [nc.dram_tensor(n, a.shape, F32, kind="ExternalInput").ap() for n, a in arrays.items()]
    out = nc.dram_tensor("out_x", v["x"].shape, F32, kind="ExternalOutput").ap()
    metaformer_kernel(nc, *aps, out)
    return run_bass_kernel_spmd(nc, [arrays], core_ids=[0]).results[0]["out_x"]
```

```python
from contextlib import ExitStack

import numpy as np

import concourse.bass as bass
from concourse import mybir

F32 = mybir.dt.float32
F32R = mybir.dt.float32r
F16 = mybir.dt.float16
ALU = mybir.AluOpType
ACT = mybir.ActivationFunctionType
AX_X = mybir.AxisListType.X

P = 128
C = 64
B, H, W = 16, 16, 16
N = H * W
HALVES = 2
BH = B // HALVES
COLS = BH * N
Q = 512
NQ = COLS // Q
CR = 4
TAPS = 9
E = 8
PAIRS = E // 2
HEADS, KD = 8, 16

PITCH = W + 1
MAP = PITCH * (H + 1)
LEAD = PITCH + 1
FLAT = BH * MAP

STEP = 256.0
SCALE = STEP * 2 ** 20
TOP = STEP * 2 ** 23
QUANT = 0.85
POS = np.float32(QUANT) * np.float32(C * N - 1)
LOW = int(np.floor(POS))
W_HIGH = float(np.float32(POS - np.floor(POS)))
W_LOW = float(np.float32(1) - np.float32(W_HIGH))
RANK = C * N - LOW
assert C * N < 4 ** 2 * RANK
SEARCH = TOP / 2
SEARCH_BITS = 22
COARSE_BITS = 12
WINDOW = 2.5
KEPT = 8
GROUP = 8
ACT_COLS = 1024
DVE_COLS = COLS - ACT_COLS


def weight_columns():
    return [
        ("center", P), ("mean", P), ("eps", 4), ("tap_th", 40), ("tp_b1", 1), ("tp_w2", P), ("tp_b2", 1),
        ("sa_b", 1), ("tap_sum", P), ("ca_w1", 8), ("ca_b1", 1), ("ca_w2", P), ("ca_b2", 1),
        ("mask8", 8), ("gt_sel", 8), ("ones", 1), ("half_sel", P), ("ident", P), ("group", P),
        ("router", E), ("f_wr", E), ("sel", HALVES * PAIRS * P), ("w1", PAIRS * P), ("b2", P),
        ("f_w1", PAIRS * P),
        ("b1", PAIRS), ("expert_rank", E), ("w2", PAIRS * C),
        ("wkv", 4 * KD), ("kv_bias", 1), ("wq", HALVES * P), ("bq", 1), ("to_heads", HALVES * P), ("wo", C), ("bo", 1),
        ("head_mask", P),
        ("bn_g", 2 * PAIRS), ("bn_b", 2 * PAIRS), ("bn_be", 2 * PAIRS), ("bn_m", 2 * PAIRS), ("bn_v", 2 * PAIRS),
        ("f_w2", PAIRS * P), ("f_wo", PAIRS * C), ("f_bo", P), ("f_br", E),
    ]


AT = {}
NCOL = 0
for _name, _n in weight_columns():
    AT[_name] = (NCOL, NCOL + _n)
    NCOL += _n
SPLIT0, SPLIT1 = AT["router"][0], AT["f_w1"][1]
EARLY = SPLIT0
FIRST = AT["tap_th"][0]


def metaformer_kernel(nc, x_dram, weights_dram, out_dram):
    ctx = ExitStack()
    with ctx:
        def sb(name, shape, dt=F32):
            return ctx.enter_context(nc.sbuf_tensor(name, shape, dt))

        def sem(name):
            return ctx.enter_context(nc.semaphore(name))

        WT = sb("weights", [P, NCOL])

        def w(name, rows=slice(0, P), cols=None):
            a, b = AT[name]
            if cols is not None:
                a, b = a + cols.start, a + cols.stop
            return WT[rows, a:b]

        X = sb("x_resid", [P, COLS])
        HID = sb("hidden_of_all_tokens", [P, BH * COLS])
        QX, QT, SW, REL, AB, SQ, XC, RS = (HID[:, i * COLS:(i + 1) * COLS] for i in range(BH))
        T = sb("x_normed", [P, COLS])
        S = sb("x_split", [P, HALVES, COLS], F32R)

        PADDED = sb("taps_padded", [18, FLAT + 2 * LEAD])
        SHIFTED = sb("taps_shifted", [18, FLAT])
        TH = sb("threshold_hidden", [40, COLS])
        U = sb("gated_x", [P, COLS])
        pooled = sb("pooled", [P, BH])
        ca_h = sb("channel_hidden", [8, BH])
        CW = sb("channel_weights", [P, BH])
        thr = sb("threshold", [P, 1])
        thr_half = sb("threshold_less_half_step", [P, 1])
        thr_top = sb("threshold_above", [P, 1])
        step = sb("bit_step", [P, 1])
        bit = sb("bit_stays", [P, 1])
        counts = sb("partial_counts", [P, 2], F16)
        group16 = sb("group_f16", [P, P], F16)
        low, high = sb("window_low", [P, 1]), sb("window_high", [P, 1])
        kept = sb("kept_values", [P, KEPT])
        below = sb("kept_below", [P, KEPT])
        spread = sb("kept_spread", [P, GROUP * KEPT + 2])
        less = XC[:, 0:KEPT * GROUP * KEPT].rearrange("p (i j) -> p i j", i=KEPT)
        ranks = sb("kept_rank", [P, KEPT])
        aim = sb("rank_wanted", [P, 2])
        picked = sb("kept_picked", [P, 2, KEPT])
        picked1 = sb("kept_picked_max", [P, 2])
        spread2 = sb("picked_spread", [P, 2, GROUP])
        both = sb("order_statistics", [P, 2])
        fail = sb("failed", [P, 1])
        fail_int = sb("failed_any", [1, 1], mybir.dt.int32)
        above = sb("above_max", [P, 1])
        above8 = sb("above_max_spread", [P, 8])
        upper = sb("upper_value", [P, 1])
        flag = sb("upper_is_next", [P, 1])
        gt = sb("quantile", [P, 1])
        gt8 = sb("quantile_spread", [P, BH])
        neg_gt = sb("neg_quantile", [P, BH])

        WH = sb("weights_high", [P, SPLIT1 - SPLIT0], F32R)
        WL = sb("weights_low", [P, SPLIT1 - SPLIT0], F32R)
        router2 = sb("router_parts", [P, 2 * E], F32R)
        f_wr2 = sb("f_router_parts", [P, 2 * E], F32R)

        def part(tile, name, rows=slice(0, P), cols=None):
            a, b = (n - SPLIT0 for n in AT[name])
            if cols is not None:
                a, b = a + cols.start, a + cols.stop
            return tile[rows, a:b]

        TILES = B * N // P
        logits = sb("logits", [P, TILES, E])
        best = sb("best_logit", [P, TILES])
        second = sb("second_logit", [P, TILES])
        is_best = sb("is_best", [P, TILES, E])
        is_second = sb("is_second", [P, TILES, E])
        key = sb("tie_key", [P, TILES, E])
        key_max = sb("tie_key_max", [P, TILES])
        lead = sb("share_lead", [P, TILES])
        share1 = sb("best_share", [P, TILES])
        share2 = sb("second_share", [P, TILES])
        combine = sb("combine", [P, TILES, E])
        combine2 = sb("combine_parts", [P, TILES, 2, E], F32R)
        CT = sb("combine_rows", [P, COLS], F32R)
        G, HS, H2 = (t[:, :].rearrange("p (g q) -> p g q", g=PAIRS) for t in (QT, U, QX))

        EKV = REL[0:4 * KD, :]
        EKVT = AB[:, 0:1024]
        MB = AB[:, 1024:2048].rearrange("p (h b c) -> p h b c", h=HALVES, b=BH)
        BD = H2.rearrange("p g (b n) -> p (g b) n", n=P)
        Q0 = G[:, 0:2]
        QB = HS
        QS = G[:, 2:4]
        kmax = sb("key_max", [32, BH])
        kbias = sb("key_bias", [32, BH])
        ksum = sb("key_sum", [32, BH])
        krec = sb("key_reciprocal", [32, BH])
        CTX = sb("contexts", [32, BH * 32])
        qmax = sb("query_max", [P, 2, 32])
        qsum = sb("query_sum", [P, 2, 32])
        qrec = sb("query_reciprocal", [P, 2, 32])

        bn_a = sb("bn_scale", [P, 2 * PAIRS])
        bn_c = sb("bn_shift", [P, 2 * PAIRS])
        f_logits = sb("f_logits", [P, 2, E])
        f_max = sb("f_max", [P, 2])
        f_sum = sb("f_sum", [P, 2])
        fl_rows = sb("f_logits_rows", [2 * E, N])
        fT = sb("f_weights_rows", [E, N])
        FW = SW[:, 0:PAIRS * N].rearrange("p (g n) -> p g n", g=PAIRS)
        FB = SW[:, PAIRS * N:(PAIRS + 1) * N]
        H1 = G
        HW = HS

        PS = ctx.enter_context(nc.psum_tensor("ps", [P, 8, Q], F32))

        w_in, w2_in, late_in = sem("weights_in"), sem("weights2_in"), sem("late_weights_in")
        x_in = [sem(f"x_in{q}") for q in range(NQ)]
        xc_ready, xc_copied, sq_ready, var_ready = sem("xc_ready"), sem("xc_copied"), sem("sq_ready"), sem("var_ready")
        ln_taken, rs_ready, t_ready = sem("ln_taken"), sem("rs_ready"), sem("t_ready")
        abs_ready, q_in, rounded_ready = sem("abs_ready"), sem("quantile_in"), sem("rounded_ready")
        half_ready, bit_ready = sem("half_ready"), sem("bit_ready")
        step_ready, group_ready = sem("step_ready"), sem("group_ready")
        zeroed, taps_ready, taps_out, th_out, shifted_in = sem("zeroed"), sem("taps_ready"), sem("taps_out"), sem("th_out"), sem("shifted_in")
        rel_ready, rel_out, sw_ready, sw_out = sem("rel_ready"), sem("rel_out"), sem("sw_ready"), sem("sw_out")
        pooled_ready, ca_ready, ca1_out, cw_ready = (sem(n) for n in ("pooled_ready", "ca_ready", "ca1_out", "cw_ready"))
        u_ready, comp_ready = sem("u_ready"), sem("complement_ready")
        thr_ready, dve_counted, act_counted, counted = sem("thr_ready"), sem("dve_counted"), sem("act_counted"), sem("counted")
        chain_v, chain_g = sem("vector_chain"), sem("gpsimd_chain")
        tail_ready, top_counted, tail_spread = sem("tail_ready"), sem("top_counted"), sem("tail_spread")
        gt_ready, gt_spread = sem("gt_ready"), sem("gt_spread")
        split_high, split_low = sem("split_high"), sem("split_low")
        hi_ready, s_ready = sem("hi_ready"), sem("s_ready")
        logits_ready, lead_ready, tanh_ready, combine_ready = sem("logits_ready"), sem("lead_ready"), sem("tanh_ready"), sem("combine_ready")
        ct_ready, ct_out, x_added = sem("ct_ready"), sem("ct_out"), sem("x_added")
        z_ready, gelu_done, cb_ready = ([sem(f"{n}{p}") for p in range(PAIRS)] for n in ("z_ready", "gelu_done", "cb_ready"))
        hs_ready, w2_done = ([sem(f"{n}{p}") for p in range(PAIRS)] for n in ("hs_ready", "w2_done"))
        y_taken, top_used = sem("y_taken"), sem("top_used")
        kv_ready, kmax_ready, kb_chain, ek_exp, ek_ready = (sem(n) for n in ("kv_ready", "kmax_ready", "kb_chain", "ek_exp", "ek_ready"))
        krec_ready, v_out, ekt_ready, ekt_out = (sem(n) for n in ("krec_ready", "v_out", "ekt_ready", "ekt_out"))
        q_ready, q_biased, qb_ready, qmax_ready, qsub_ready = (sem(n) for n in ("q_ready", "q_biased", "qb_ready", "qmax_ready", "qsub_ready"))
        qexp_ready, qsum_ready, qrec_ready, qn_ready, qs_ready = (sem(n) for n in ("qexp_ready", "qsum_ready", "qrec_ready", "qn_ready", "qs_ready"))
        cx_ready, cx_out, heads_ready, bd_ready, mb_ready, mb_out = (sem(n) for n in ("cx_ready", "cx_out", "heads_ready", "bd_ready", "mb_ready", "mb_out"))
        a_ready, x3_ready = sem("a_ready"), sem("x3_ready")
        bn_chain, bn_rs, fl_ready, fl_chain, fe_ready, fw_ready = (sem(n) for n in ("bn_chain", "bn_rs", "fl_ready", "fl_chain", "fe_ready", "fw_ready"))
        ft_ready, ft_out, fb_ready, fb_out, bias_added = (sem(n) for n in ("ft_ready", "ft_out", "fb_ready", "fb_out", "bias_added"))
        z1_ready, h1_ready, z2_ready = ([sem(f"{n}{p}") for p in range(PAIRS)] for n in ("z1_ready", "h1_ready", "z2_ready"))
        h2_ready, hw_ready, wo_done = ([sem(f"{n}{p}") for p in range(PAIRS)] for n in ("h2_ready", "hw_ready", "wo_done"))
        low_ready, below_ready, pick_chain, pick_ready, pick_spread, branch_ready = (sem(n) for n in ("low_ready", "below_ready", "pick_chain", "pick_ready", "pick_spread", "branch_ready"))
        fl_out, fl_turned = sem("fl_out"), sem("fl_turned")
        warm_ready = sem("warm_ready")
        x4_ready = sem("x4_ready")
        diff_ready, mask_ready, gated_ready, x1_ready = sem("diff_ready"), sem("mask_ready"), sem("gated_ready"), sem("x1_ready")
        out_done = sem("out_done")

        def cols(q, n=Q):
            return slice(q * n, (q + 1) * n)

        def maps(ap):
            return ap.rearrange("p (b y x) -> p b y x", b=2, y=H)

        def padded_maps(ap, q):
            return ap[:, 2 * q * MAP:2 * (q + 1) * MAP].rearrange("p (b y x) -> p b y x", b=2, x=PITCH)[:, :, 0:H, 0:W]

        class Chain:

            def __init__(self, eng, s):
                self.eng, self.s, self.n = eng, s, 0

            def __call__(self, ins):
                self.n += 1
                ins.then_inc(self.s, 1)

            def wait(self):
                self.eng.wait_ge(self.s, self.n)

        block = ctx.enter_context(nc.Block())

        def center_bank(n, q):
            return (0, 1, 4, 5)[q] if n == 2 else (0, 1, 5, 6)[q]

        def ln_pe_center(pe, n, q, x_wait):
            x_wait(q)
            pe.matmul(PS[:, center_bank(n, q)], w("center"), X[:, cols(q)], start=True, stop=True).then_inc(xc_ready, 1)

        def ln_pe_var(pe, n, q):
            pe.wait_ge(sq_ready, 4 * n + q + 1)
            if 4 * n + q >= 2:
                pe.wait_ge(ln_taken, 4 * n + q - 1)
            pe.matmul(PS[:, 2 + q % 2], w("mean"), SQ[:, cols(q)], start=True, stop=True).then_inc(var_ready, 1)

        def ln_pool_square(pool, n, q):
            pool.wait_ge(xc_copied, 4 * n + q + 1)
            pool.tensor_tensor(SQ[:, cols(q)], XC[:, cols(q)], XC[:, cols(q)], ALU.mult).then_inc(sq_ready, 1)

        def ln_act_rstd(act, n, q, eps_col):
            act.wait_ge(var_ready, 4 * n + q + 1)
            if n:
                act.wait_ge(t_ready, 4 * n)
            act.activation(RS[:, cols(q)], PS[:, 2 + q % 2], ACT.Ln, bias=w("eps", cols=slice(eps_col, eps_col + 1))).then_inc(ln_taken, 1)
            act.wait_ge(ln_taken, 4 * n + q + 1)
            act.activation(RS[:, cols(q)], RS[:, cols(q)], ACT.Exp, scale=-0.5).then_inc(rs_ready, 1)

        def ln_dve_copy(dve, n, q):
            dve.wait_ge(xc_ready, 4 * n + q + 1)
            if n:
                dve.wait_ge(t_ready, 4 * n)
            dve.tensor_copy(XC[:, cols(q)], PS[:, center_bank(n, q)]).then_inc(xc_copied, 1)

        def ln_dve_scale(dve, n, q, t_free=None):
            dve.wait_ge(rs_ready, 4 * n + q + 1)
            dve.wait_ge(xc_copied, 4 * n + q + 1)
            if t_free:
                t_free(q)
            dve.tensor_tensor(T[:, cols(q)], XC[:, cols(q)], RS[:, cols(q)], ALU.mult).then_inc(t_ready, 1)

        def ln_dve(dve, n, t_free=None):
            for q in range(NQ + 3):
                if q < NQ:
                    ln_dve_copy(dve, n, q)
                if q >= 3:
                    ln_dve_scale(dve, n, q - 3, t_free)

        def split_act(act, n, q):
            act.wait_ge(t_ready, 4 * n + q + 1)
            act.activation(S[0:C, 0, cols(q)], T[0:C, cols(q)], ACT.Copy).then_inc(hi_ready, 1)
            act.activation(S[C:P, 1, cols(q)], T[C:P, cols(q)], ACT.Copy).then_inc(hi_ready, 1)

        def split_dve(dve, n, q):
            for h, (own, other) in enumerate(((slice(0, C), slice(C, P)), (slice(C, P), slice(0, C)))):
                dve.wait_ge(hi_ready, 2 * NQ * (n // 2) + 2 * q + h + 1)
                dve.tensor_tensor(S[other, h, cols(q)], T[own, cols(q)], S[own, h, cols(q)].bitcast(F32),
                                  ALU.subtract).then_inc(s_ready, 1)

        def ln_split_act(act, n, eps_col):
            for q in range(NQ + 1):
                if q < NQ:
                    ln_act_rstd(act, n, q, eps_col)
                if q >= 1:
                    split_act(act, n, q - 1)

        def ln_split_dve(dve, n, t_free=None):
            for q in range(NQ + 3):
                if q < NQ:
                    ln_dve_copy(dve, n, q)
                if 2 <= q < NQ + 2:
                    ln_dve_scale(dve, n, q - 2, t_free)
                if q >= 3:
                    split_dve(dve, n, q - 3)

        def pair(name, p, tile=None, n=P):
            c = slice(p * n, (p + 1) * n)
            return w(name, cols=c) if tile is None else part(tile, name, cols=c)

        def two_pass(pe, out, name, p, rhs, start=True, stop=True):
            pe.matmul(out, pair(name, p, WH), rhs, start=start, stop=False)
            return pe.matmul(out, pair(name, p, WL), rhs, start=False, stop=stop)

        def after(eng, i):
            return i + 1 if isinstance(i, int) else eng.snap(i + 1)

        def keep_clock(pe, ap, bank, n):
            for _ in range(n):
                pe.matmul(PS[:, bank, 0:N], ap[:, 0:P], ap[:, 0:N], start=True, stop=True)

        def it_values(eng, i):
            i = i if isinstance(i, int) else eng.snap(i)
            return i, after(eng, i)

        def wait_last(eng, s, n):
            if not (isinstance(n, int) and n == 0):
                eng.wait_ge(s, n)

        WARM = 6
        HIDDEN_BANK = (5, 6, 7, 0)
        AHEAD = 5
        SHARES_AT = 3

        @block.sync
        def _(sp):
            x_v = x_dram.rearrange("(h b) c y x -> h c b (y x)", h=HALVES)
            sp.dma_start(WT[:, 0:FIRST], weights_dram[:, 0:FIRST]).then_inc(w_in, 16)
            for q in range(NQ):
                sp.dma_start(X[0:C, cols(q)].rearrange("c (b n) -> c b n", n=N), x_v[0, :, 2 * q:2 * q + 2]).then_inc(x_in[q], 16)
            sp.dma_start(WT[:, FIRST:EARLY], weights_dram[:, FIRST:EARLY]).then_inc(w2_in, 16)
            sp.dma_start(WT[:, EARLY:NCOL], weights_dram[:, EARLY:NCOL]).then_inc(late_in, 16)
            for b in range(BH):
                if b % 2 == 0:
                    sp.wait_ge(abs_ready, b // 2 + 1)
                g = b * HALVES * GROUP
                sp.dma_start(QT[g:g + HALVES * GROUP, :].rearrange("j (c n) -> j c n", c=C // GROUP), AB[:, b * N:(b + 1) * N]).then_inc(q_in, 16)
            sp.wait_ge(taps_out, NQ)
            for dy in range(3):
                for dx in range(3):
                    tap = 3 * dy + dx
                    off = LEAD + (dy - 1) * PITCH + dx - 1
                    sp.dma_start(SHIFTED[tap:18:TAPS, :], PADDED[tap:18:TAPS, off:off + FLAT]).then_inc(shifted_in, 16)
            o_v = out_dram.rearrange("(h b) c y x -> h b c (y x)", h=HALVES)
            with sp.Fori(0, BH) as b0:
                b = sp.snap(b0)
                sp.wait_ge(x4_ready, b + 1)
                for h in range(HALVES):
                    sp.dma_start(o_v[h, bass.ds(b, 1)].rearrange("b c n -> (b c) n"), X[h * C:(h + 1) * C, bass.ds(b * N, N)]).then_inc(out_done, 16)
            sp.wait_ge(out_done, 16 * B)

        @block.tensor
        def _(pe):
            pe.wait_ge(warm_ready, 1)
            keep_clock(pe, XC, 7, 3)
            pe.wait_ge(w_in, 16)
            for q in range(3):
                ln_pe_center(pe, 0, q, lambda q: pe.wait_ge(x_in[q], 32))
            for q in range(NQ + 3):
                if 1 <= q <= NQ:
                    ln_pe_var(pe, 0, q - 1)
                if q == 1:
                    ln_pe_center(pe, 0, 3, lambda q: pe.wait_ge(x_in[q], 32))
                if q == 3:
                    pe.wait_ge(w2_in, 16)
                if q >= 3:
                    pe.wait_ge(xc_copied, NQ)
                    pe.wait_ge(t_ready, q - 2)
                    pe.matmul(PS[0:40, 4 + q - 3], w("tap_th"), T[:, cols(q - 3)], start=True, stop=True).then_inc(taps_ready, 1)

            def channel_hidden(_):
                pe.wait_ge(pooled_ready, 1)
                pe.wait_ge(xc_copied, NQ)
                pe.matmul(PS[0:8, 1, 0:BH], w("ca_w1"), pooled[:, :], start=True, stop=True).then_inc(ca_ready, 1)

            def channel_weights(_):
                pe.wait_ge(ca1_out, 1)
                pe.matmul(PS[:, 1, 0:BH], w("ca_w2", slice(0, 8)), ca_h[:, :], start=True, stop=True).then_inc(ca_ready, 1)

            def relative_threshold(q):
                pe.wait_ge(ln_taken, NQ)
                pe.wait_ge(th_out, q + 1)
                if q >= 2:
                    pe.wait_ge(rel_out, q - 1)
                pe.matmul(PS[:, 2 + q % 2], w("tp_w2", slice(32, 40)), TH[32:40, cols(q)], start=True, stop=True).then_inc(rel_ready, 1)

            def spatial_weights(q):
                pe.wait_ge(shifted_in, 16 * TAPS)
                pe.wait_ge(th_out, q + 1)
                pe.wait_ge(taps_out, q + 1)
                pe.matmul(maps(PS[:, 4 + q]), w("tap_sum", slice(0, 18)), padded_maps(SHIFTED, q),
                          start=True, stop=True).then_inc(sw_ready, 1)

            def sum_counts(r):
                pe.wait_ge(dve_counted, r + 1)
                pe.wait_ge(act_counted, r + 1)
                pe.matmul(PS[:, 0, 0:2], group16[:, :], counts[:, :], start=True, stop=True).then_inc(counted, 1)

            gates = [(channel_hidden, 0), (channel_weights, 0), *((relative_threshold, q) for q in range(NQ)),
                     *((spatial_weights, q) for q in range(NQ))]
            pe.wait_ge(group_ready, 1)
            pe.wait_ge(xc_copied, NQ)
            for r in range(COARSE_BITS):
                sum_counts(r)
                if r < len(gates):
                    piece, q = gates[r]
                    piece(q)
            keep_clock(pe, T, 3, WARM)
            pe.wait_ge(pick_ready, 1)
            pe.wait_ge(below_ready, 1)
            pe.wait_ge(cw_ready, 1)
            pe.matmul(PS[:, 1, 0:GROUP * KEPT + 2], w("group"), spread[:, :], start=True, stop=True).then_inc(pick_spread, 1)
            pe.wait_ge(pick_ready, 2)
            pe.matmul(PS[:, 2, 0:2 * GROUP], w("group"), spread2[:, :, :].rearrange("p s j -> p (s j)"), start=True, stop=True).then_inc(pick_spread, 1)
            pe.wait_ge(pick_ready, 3)
            pe.matmul(PS[0:1, 3, 0:1], w("ones"), fail[:, :], start=True, stop=True).then_inc(pick_spread, 1)
            pe.wait_ge(branch_ready, 1)
            with pe.If(pe.value_load(fail_int[0:1, 0:1], min_val=0, max_val=P * P) > 0):
                with pe.Fori(COARSE_BITS, SEARCH_BITS) as r:
                    sum_counts(pe.snap(r))
                pe.wait_ge(tail_ready, 2)
                pe.wait_ge(cw_ready, 1)
                pe.matmul(PS[:, 1, 0:8], w("group"), above8[:, :], start=True, stop=True).then_inc(tail_spread, 1)
                pe.wait_ge(top_counted, 1)
                pe.wait_ge(thr_ready, SEARCH_BITS + 1)
                pe.matmul(PS[:, 0, 0:2], group16[:, :], counts[:, :], start=True, stop=True).then_inc(tail_spread, 1)
            pe.wait_ge(gt_ready, 1)
            pe.matmul(PS[:, 2, 0:BH], w("half_sel"), gt8[:, :], start=True, stop=True).then_inc(gt_spread, 1)

            pe.wait_ge(top_used, 1)
            pe.wait_ge(sw_out, NQ)
            for q in range(NQ):
                pe.matmul(PS[:, center_bank(1, q)], w("center"), X[:, cols(q)], start=True, stop=False)
            for q in range(NQ + 1):
                if q < NQ:
                    pe.wait_ge(gated_ready, q + 1)
                    pe.matmul(PS[:, center_bank(1, q)], w("center"), U[:, cols(q)], start=False, stop=True).then_inc(xc_ready, 1)
                if q >= 1:
                    ln_pe_var(pe, 1, q - 1)
            pe.wait_ge(split_low, 2)
            pe.wait_ge(sw_out, NQ)

            def route(q):
                pe.wait_ge(s_ready, 2 * q + 2)
                for j in range(4 * q, 4 * q + 4):
                    for h in range(HALVES):
                        t = 2 * j + h
                        last = pe.matmul(PS[:, 4, 16 * t:16 * t + 16], S[:, h, cols(j, P)], router2[:, :], start=True, stop=True)
                last.then_inc(logits_ready, 1)

            def moe_up(it, n1, p):
                wait_last(pe, gelu_done[p], it)
                two_pass(pe, PS[:, HIDDEN_BANK[p]], "w1", p, S[:, :, bass.ds(it * N, N)]).then_inc(z_ready[p], 1)

            def moe_share(it, n1, p):
                if isinstance(it, int) and it % 2 == 0 and p == 0:
                    pe.wait_ge(ct_out, it // 2 + 1)
                wait_last(pe, hs_ready[(p + 2) % PAIRS], it if p < 2 else n1)
                for h in range(HALVES):
                    last = pe.matmul(PS[:, 1 + p % 2, cols(h, N)], part(WH, "sel", cols=cols(h * PAIRS + p, P)),
                                     CT[:, bass.ds(it * N, N)], start=True, stop=True)
                last.then_inc(cb_ready[p], 1)

            def moe_down(it, n1, p):
                if p == 0:
                    wait_last(pe, y_taken, it)
                pe.wait_ge(hs_ready[p], n1)
                for h in range(HALVES):
                    last = pe.matmul(PS[h * C:(h + 1) * C, 3, 0:N], pair("w2", p, n=C), HS[:, p, cols(h, N)], start=p == 0, stop=p == PAIRS - 1)
                if p == 0:
                    pe.matmul(PS[:, 3, 0:N], part(WH, "b2"), CT[:, bass.ds(it * N, N)], start=False, stop=False)
                    last = pe.matmul(PS[:, 3, 0:N], part(WL, "b2"), CT[:, bass.ds(it * N, N)], start=False, stop=False)
                last.then_inc(w2_done[p], 1)

            def moe_mix(i, up=False, last=False):
                it, n1 = it_values(pe, i)
                n2 = None if last else after(pe, n1)
                ahead = [it + AHEAD, it + AHEAD + 1] if isinstance(it, int) else [pe.snap(it + AHEAD), pe.snap(it + AHEAD + 1)]
                for p in range(PAIRS):
                    if up:
                        moe_up(*ahead, p)
                    if p < 2:
                        moe_share(it, n1, p + 2)
                    elif not last:
                        moe_share(n1, n2, p - 2)
                    moe_down(it, n1, p)

            route(0)
            pe.wait_ge(xc_copied, 2 * NQ)
            for p in range(PAIRS):
                moe_up(0, 1, p)
            for q in range(1, NQ):
                route(q)
            with pe.Fori(1, AHEAD) as i:
                it, n1 = it_values(pe, i)
                for p in range(PAIRS):
                    moe_up(it, n1, p)
            pe.wait_ge(combine_ready, 2)
            pe.wait_ge(ln_taken, 2 * NQ)
            for q in range(NQ):
                for j in range(4 * q, 4 * q + 4):
                    last = pe.transpose(PS[0:32, 1 + q, cols(j % 4, P)], combine2[:, 2 * j:2 * j + 2].rearrange("p t s e -> p (t s e)").bitcast(F32), w("ident"))
                last.then_inc(ct_ready, 1)
            pe.wait_ge(ct_out, 2)
            moe_share(0, 1, 0)
            moe_share(0, 1, 1)
            for it in range(BH - AHEAD):
                moe_mix(it, up=True)
            pe.wait_ge(ct_out, NQ)
            with pe.Fori(BH - AHEAD, BH - 1) as i:
                moe_mix(i)
            moe_mix(BH - 1, last=True)

            for p in range(PAIRS):
                pe.wait_ge(gelu_done[p], BH)
                pe.wait_ge(hs_ready[p], BH)
            for q in range(NQ + 1):
                if q < NQ:
                    ln_pe_center(pe, 2, q, lambda q: pe.wait_ge(y_taken, 2 * q + 2))
                if q >= 1:
                    ln_pe_var(pe, 2, q - 1)
            for q in range(NQ):
                pe.wait_ge(t_ready, 2 * NQ + q + 1)
                if q >= 2:
                    pe.wait_ge(ek_exp, 2 * (q - 1))
                    pe.wait_ge(v_out, q - 1)
                pe.matmul(PS[0:4 * KD, 6 + q % 2], w("wkv"), T[:, cols(q)], start=True, stop=True).then_inc(kv_ready, 1)

            def queries(it):
                if it >= 2:
                    pe.wait_ge(q_biased, it - 1)
                for h in range(HALVES):
                    last = pe.matmul(PS[:, it % 2, cols(h, N)], w("wq", cols=cols(h, P)), T[:, cols(it, N)], start=True, stop=True)
                last.then_inc(q_ready, 1)

            pe.wait_ge(xc_copied, 3 * NQ)
            queries(0)
            queries(1)
            for g in range(2):
                pe.wait_ge(ek_ready, 2 * g + 2)
                pe.wait_ge(v_out, 2 * g + 2)
                for t in range(8):
                    last = pe.transpose(PS[:, 4 + g, cols(t, 4 * KD)], EKV[:, cols(8 * g + t, P)], w("ident", slice(0, 4 * KD), slice(0, 4 * KD)))
                last.then_inc(ekt_ready, 1)
            pe.wait_ge(ln_taken, 3 * NQ)
            for it in range(BH):
                if it % 4 == 0:
                    pe.wait_ge(ekt_out, it // 4 + 1)
                for jj in range(2):
                    tile = (2 * it + jj) * 4 * KD
                    last = pe.matmul(PS[0:32, 2, cols(it, 32)], EKVT[:, tile + 32:tile + 64], EKVT[:, tile:tile + 32], start=jj == 0, stop=jj == 1)
            last.then_inc(cx_ready, 1)
            pe.wait_ge(cx_out, 1)
            for h in range(HALVES):
                last = pe.matmul(PS[:, 3, cols(h, P)], w("to_heads", slice(0, 32), cols(h, P)),
                                 CTX[:, :].rearrange("p (b h d) -> p h b d", b=BH, h=HALVES)[:, h], start=True, stop=True)
            last.then_inc(heads_ready, 1)
            queries(2)
            queries(3)
            for h in range(HALVES):
                pe.wait_ge(bd_ready, h + 1)
                for b in range(BH):
                    last = pe.matmul(PS[:, 4 + h, cols(b, C)], BD[:, h * BH + b], w("wo"), start=True, stop=True)
                last.then_inc(mb_ready, 1)
            pe.wait_ge(mb_out, HALVES)
            pe.wait_ge(ek_exp, BH)
            for it in range(BH):
                pe.wait_ge(qs_ready, it + 1)
                if it >= 2:
                    pe.wait_ge(x3_ready, it - 1)
                for h in range(HALVES):
                    last = pe.matmul(PS[h * C:(h + 1) * C, 6 + it % 2, 0:N], MB[:, h, it], QS[:, it % 2, cols(h, N)], start=True, stop=True)
                last.then_inc(a_ready, 1)
                if it + 4 < BH:
                    queries(it + 4)

            def f_route(q):
                pe.wait_ge(s_ready, 2 * NQ + 2 * q + 2)
                for b in (2 * q, 2 * q + 1):
                    for h in range(HALVES):
                        last = pe.matmul(PS[0:2 * E, 4, 0:N], f_wr2[:, :], S[:, h, cols(b, N)],
                                         start=b == 0 and h == 0, stop=b == BH - 1 and h == 1)
                return last

            for q in range(NQ + 3):
                if q < NQ:
                    ln_pe_center(pe, 3, q, lambda q: pe.wait_ge(x3_ready, 2 * q + 2))
                if 1 <= q <= NQ:
                    ln_pe_var(pe, 3, q - 1)
                if q >= 3:
                    last = f_route(q - 3)
            last.then_inc(fl_ready, 1)

            def f_up(it, n1, p):
                wait_last(pe, h1_ready[(p + 2) % PAIRS], it if p < 2 else n1)
                two_pass(pe, PS[:, p % 2], "f_w1", p, S[:, :, bass.ds(it * N, N)]).then_inc(z1_ready[p], 1)

            def f_mid(it, n1, p):
                pe.wait_ge(h1_ready[p], n1)
                wait_last(pe, h2_ready[(p + 2) % PAIRS], it if p < 2 else n1)
                pe.matmul(PS[:, 2 + p % 2], pair("f_w2", p), H1[:, p], start=True, stop=True).then_inc(z2_ready[p], 1)

            def f_down(it, n1, p):
                if p == 0:
                    wait_last(pe, x4_ready, it)
                pe.wait_ge(hw_ready[p], n1)
                for h in range(HALVES):
                    last = pe.matmul(PS[h * C:(h + 1) * C, 4, 0:N], pair("f_wo", p, n=C), HW[:, p, cols(h, N)], start=p == 0, stop=p == PAIRS - 1)
                last.then_inc(wo_done[p], 1)

            def f_body(i, last=False):
                for p in range(PAIRS):
                    if p == 0:
                        it, n1 = it_values(pe, i)
                        n2 = None if last else after(pe, n1)
                    for stage, q in ((f_up, p + 3), (f_mid, p + 2)):
                        if q < PAIRS:
                            stage(it, n1, q)
                        elif not last:
                            stage(n1, n2, q - PAIRS)
                    f_down(it, n1, p)

            def f_weights_1():
                pe.wait_ge(fl_out, 1)
                for jj in range(2):
                    last = pe.transpose(PS[:, 5, 16 * jj:16 * jj + 16], fl_rows[:, cols(jj, P)], w("ident", slice(0, 2 * E), slice(0, 2 * E)))
                last.then_inc(fl_turned, 1)

            def f_weights_2():
                pe.wait_ge(fw_ready, 1)
                for jj in range(2):
                    last = pe.transpose(PS[0:E, 5, cols(jj, P)], f_logits[:, jj], w("ident"))
                last.then_inc(ft_ready, 1)

            def f_weights_3():
                pe.wait_ge(ft_out, 1)
                for p in range(PAIRS):
                    pe.matmul(PS[:, 6 + p // 2, cols(p % 2, N)], w("sel", slice(0, E), cols(p, P)), fT[:, :], start=True, stop=True).then_inc(fb_ready, 1)
                pe.matmul(PS[:, 5, 0:N], w("f_bo", slice(0, E)), fT[:, :], start=True, stop=True).then_inc(fb_ready, 1)

            pe.wait_ge(ln_taken, 4 * NQ)
            pe.wait_ge(xc_copied, 4 * NQ)
            f_up(0, 1, 0)
            f_weights_1()
            f_up(0, 1, 1)
            f_mid(0, 1, 0)
            f_up(0, 1, 2)
            f_weights_2()
            f_mid(0, 1, 1)
            f_weights_3()
            f_body(0)
            with pe.Fori(1, BH - 1) as i:
                f_body(i)
            f_body(BH - 1, last=True)

        @block.scalar
        def _(act):
            x_v = x_dram.rearrange("(h b) c y x -> h c b (y x)", h=HALVES)
            for q in range(NQ):
                act.dma_start(X[C:P, cols(q)].rearrange("c (b n) -> c b n", n=N), x_v[1, :, 2 * q:2 * q + 2]).then_inc(x_in[q], 16)
            act.preload_act_table_set("natural_log_exp_and_others")
            act.wait_ge(w_in, 16)
            for q in range(NQ + 1):
                if q < NQ:
                    ln_act_rstd(act, 0, q, 0)
                if q >= 1:
                    act.wait_ge(t_ready, q)
                    act.activation(AB[:, cols(q - 1)], T[:, cols(q - 1)], ACT.Abs, scale=SCALE).then_inc(abs_ready, 1)
            act.preload_act_table(ACT.Sigmoid)
            act.wait_ge(w2_in, 16)
            act.wait_ge(zeroed, 1)
            for q in range(NQ):
                act.wait_ge(taps_ready, q + 1)
                act.activation(TH[32:40, cols(q)], PS[32:40, 4 + q], ACT.Relu, bias=w("tp_b1", slice(32, 40))).then_inc(th_out, 1)
                act.activation(padded_maps(PADDED[:, LEAD:LEAD + FLAT], q), maps(PS[0:18, 4 + q]), ACT.Copy).then_inc(taps_out, 1)

            def relative_threshold(q):
                act.wait_ge(rel_ready, q + 1)
                act.activation(REL[:, cols(q)], PS[:, 2 + q % 2], ACT.Sigmoid, bias=w("tp_b2")).then_inc(rel_out, 1)

            def channel_hidden(_):
                act.wait_ge(ca_ready, 1)
                act.activation(ca_h[:, :], PS[0:8, 1, 0:BH], ACT.Relu, bias=w("ca_b1", slice(0, 8)), scale=1.0 / N).then_inc(ca1_out, 1)

            def channel_weights(_):
                act.wait_ge(ca_ready, 2)
                act.activation(CW[:, :], PS[:, 1, 0:BH], ACT.Sigmoid, bias=w("ca_b2")).then_inc(cw_ready, 1)

            def spatial_weights(q):
                act.wait_ge(sw_ready, q + 1)
                act.activation(SW[:, cols(q)], PS[:, 4 + q], ACT.Sigmoid, bias=w("sa_b")).then_inc(sw_out, 1)

            act.wait_ge(rounded_ready, 1)
            act.wait_ge(var_ready, NQ)

            def count_below_act(r0):
                r = r0 if isinstance(r0, int) else act.snap(r0)
                act.wait_ge(thr_ready, r + 1)
                with nc.allow_low_precision(reason="whole numbers up to 2048"):
                    act.activation(SQ[:, 0:ACT_COLS], QT[:, DVE_COLS:COLS], ACT.Sigmoid, bias=thr[:, 0:1], scale=-1.0,
                                   accum_out=counts[:, 1:2]).then_inc(act_counted, 1)

            gates = [(channel_hidden, 0), (channel_weights, 0), *((relative_threshold, q) for q in range(NQ)),
                     *((spatial_weights, q) for q in range(NQ))]
            for r in range(COARSE_BITS):
                count_below_act(r)
                if 1 <= r <= len(gates):
                    piece, q = gates[r - 1]
                    piece(q)
            assert len(gates) < COARSE_BITS
            act.wait_ge(low_ready, 1)
            act.activation(SQ[:, :], QT[:, :], ACT.Sigmoid, bias=low[:, 0:1], scale=-1.0,
                           accum_out=spread[:, GROUP * KEPT:GROUP * KEPT + 1]).then_inc(below_ready, 1)
            act.wait_ge(branch_ready, 1)
            with act.If(act.value_load(fail_int[0:1, 0:1], min_val=0, max_val=P * P) > 0):
                act.wait_ge(below_ready, 1)
                with act.Fori(COARSE_BITS, SEARCH_BITS) as r0:
                    count_below_act(r0)
                act.wait_ge(tail_ready, 1)
                with nc.allow_low_precision(reason="whole numbers up to 2048"):
                    act.activation(SQ[:, :], QT[:, :], ACT.Sigmoid, bias=thr_top[:, 0:1], scale=-1.0,
                                   accum_out=counts[:, 1:2]).then_inc(top_counted, 1)
            for q in range(NQ):
                act.wait_ge(diff_ready, 2 * q + 2)
                act.activation(AB[:, cols(q)], AB[:, cols(q)], ACT.Sigmoid, scale=10.0 / SCALE).then_inc(mask_ready, 1)

            act.preload_act_table_set("natural_log_exp_and_others")
            act.wait_ge(below_ready, 1)
            ln_split_act(act, 1, 1)
            act.preload_act_table(ACT.Gelu)

            def moe_gelu(i):
                it, n1 = it_values(act, i)
                for p in range(PAIRS):
                    act.wait_ge(z_ready[p], n1)
                    act.activation(HID[:, bass.ds(it * COLS + p * Q, Q)], PS[:, HIDDEN_BANK[p]], ACT.Gelu, bias=w("b1", cols=slice(p, p + 1))).then_inc(gelu_done[p], 1)

            with act.Fori(0, SHARES_AT) as i:
                moe_gelu(i)
            act.wait_ge(lead_ready, 1)
            act.activation(lead[:, :], lead[:, :], ACT.Tanh, scale=0.5).then_inc(tanh_ready, 1)
            with act.Fori(SHARES_AT, BH) as i:
                moe_gelu(i)

            act.preload_act_table_set("natural_log_exp_and_others")
            for q in range(NQ + 2):
                if q < NQ:
                    ln_act_rstd(act, 2, q, 0)
                if q >= 2:
                    r = q - 2
                    act.wait_ge(kv_ready, r + 1)
                    act.activation(EKV[32:64, cols(r)], PS[32:64, 6 + r % 2], ACT.Identity, bias=w("kv_bias", slice(32, 64))).then_inc(v_out, 1)
                    act.wait_ge(kb_chain, 2 * r + 2)
                    for b in (2 * r, 2 * r + 1):
                        act.activation(EKV[0:32, cols(b, N)], PS[0:32, 6 + r % 2, cols(b % 2, N)], ACT.Exp, bias=kbias[:, b:b + 1],
                                       accum_out=ksum[:, b:b + 1]).then_inc(ek_exp, 1)

            def queries_out(it):
                act.wait_ge(q_ready, it + 1)
                if it >= 2:
                    act.wait_ge(qb_ready, it - 1)
                act.activation(Q0[:, it % 2], PS[:, it % 2], ACT.Identity, bias=w("bq")).then_inc(q_biased, 1)

            def queries_exp(it):
                act.wait_ge(qsub_ready, it + 1)
                act.activation(QB[:, it % 4], QB[:, it % 4], ACT.Exp).then_inc(qexp_ready, 1)

            queries_out(0)
            queries_out(1)
            for g in range(2):
                act.wait_ge(ekt_ready, g + 1)
                act.activation(EKVT[:, cols(g)], PS[:, 4 + g], ACT.Copy).then_inc(ekt_out, 1)
            queries_exp(0)
            act.wait_ge(cx_ready, 1)
            act.activation(CTX[:, :], PS[0:32, 2, 0:N], ACT.Copy).then_inc(cx_out, 1)
            queries_out(2)
            queries_exp(1)
            queries_out(3)
            for h in range(HALVES):
                act.wait_ge(mb_ready, h + 1)
                act.activation(MB[:, h], PS[:, 4 + h].rearrange("p (b c) -> p b c", b=BH), ACT.Copy).then_inc(mb_out, 1)
            for it in range(2, BH):
                queries_exp(it)
                if it + 2 < BH:
                    queries_out(it + 2)

            act.wait_ge(late_in, 16)
            act.activation(bn_a[:, :], w("bn_v"), ACT.Ln, bias=w("eps", cols=slice(2, 3))).then_inc(bn_rs, 1)
            act.wait_ge(bn_rs, 1)
            act.activation(bn_a[:, :], bn_a[:, :], ACT.Exp, scale=-0.5).then_inc(bn_rs, 1)
            ln_split_act(act, 3, 1)

            def bn_relu(out, bank, p, layer):
                n = layer * PAIRS + p
                return act.activation(out, PS[:, bank + p % 2], ACT.Relu, bias=bn_c[:, n:n + 1], scale=bn_a[:, n:n + 1])

            def f_h1(it, n1, p):
                act.wait_ge(z1_ready[p], n1)
                wait_last(act, z2_ready[p], it)
                bn_relu(H1[:, p], 0, p, 0).then_inc(h1_ready[p], 1)

            def f_h2(it, n1, p):
                act.wait_ge(z2_ready[p], n1)
                wait_last(act, hw_ready[p], it)
                bn_relu(H2[:, p], 2, p, 1).then_inc(h2_ready[p], 1)

            def f_act_body(i, last=False):
                it, n1 = it_values(act, i)
                n2 = None if last else after(act, n1)
                for p in range(PAIRS):
                    for stage, q in ((f_h1, p + 3), (f_h2, p + 2)):
                        if q < PAIRS:
                            stage(it, n1, q)
                        elif not last:
                            stage(n1, n2, q - PAIRS)

            act.wait_ge(bn_chain, 4)
            act.wait_ge(hs_ready[3], BH)
            act.wait_ge(fl_ready, 1)
            act.activation(fl_rows[:, :], PS[0:2 * E, 4, 0:N], ACT.Copy).then_inc(fl_out, 1)
            f_h1(0, 1, 0)
            act.wait_ge(fl_chain, 5)
            act.activation(f_logits[:, :], f_logits[:, :], ACT.Exp).then_inc(fe_ready, 1)
            f_h1(0, 1, 1)
            f_h2(0, 1, 0)
            f_h1(0, 1, 2)
            f_h2(0, 1, 1)
            f_act_body(0)
            with act.Fori(1, BH - 1) as i:
                f_act_body(i)
            f_act_body(BH - 1, last=True)

        @block.vector
        def _(dve):
            dve.memset(XC[:, 0:Q], 0.0).then_inc(warm_ready, 1)
            dve.wait_ge(w_in, 16)
            ln_dve(dve, 0)
            dve.wait_ge(t_ready, NQ)
            dve.wait_ge(w2_in, 16)
            dve.tensor_copy(group16[:, :], w("group")).then_inc(group_ready, 1)
            dve.tensor_reduce(pooled[:, :], T[:, :].rearrange("p (b n) -> p b n", b=BH), AX_X, ALU.add).then_inc(pooled_ready, 1)
            dve.wait_ge(q_in, 16 * BH)
            dve.tensor_scalar(QT[:, :], QT[:, :], TOP, TOP, ALU.add, ALU.subtract).then_inc(rounded_ready, 1)
            dve.memset(step[:, :], SEARCH).then_inc(chain_v, 1)
            dve.wait_ge(chain_v, 1)
            dve.memset(thr[:, :], SEARCH / 2 - STEP / 2).then_inc(thr_ready, 1)
            dve.wait_ge(rounded_ready, 1)
            dve.wait_ge(xc_copied, NQ)

            def count_below(n):
                dve.wait_ge(thr_ready, n)
                with nc.allow_low_precision(reason="whole numbers up to 2048"):
                    dve.tensor_scalar(XC[:, 0:DVE_COLS], QT[:, 0:DVE_COLS], thr[:, 0:1], None, ALU.is_lt, ALU.add,
                                      accum_out=counts[:, 0:1]).then_inc(dve_counted, 1)
                dve.tensor_scalar(step[:, :], step[:, :], 0.5, None, ALU.mult).then_inc(step_ready, 1)
                dve.wait_ge(step_ready, n)
                dve.scalar_tensor_tensor(thr_half[:, :], step[:, :], -0.5, thr[:, :], ALU.mult, ALU.add).then_inc(half_ready, 1)

            def set_bit(n):
                dve.wait_ge(counted, n)
                dve.tensor_scalar(bit[:, :], PS[:, 0, 0:1], PS[:, 0, 1:2], C * N - RANK + 0.5, ALU.add, ALU.is_lt).then_inc(bit_ready, 1)
                dve.wait_ge(bit_ready, n)
                dve.wait_ge(half_ready, n)
                dve.scalar_tensor_tensor(thr[:, :], bit[:, :], step[:, 0:1], thr_half[:, :], ALU.mult, ALU.add).then_inc(thr_ready, 1)

            def search(first, last):
                count_below(first + 1)
                with dve.Fori(first + 1, last) as r0:
                    r = dve.snap(r0)
                    set_bit(r)
                    count_below(dve.snap(r + 1))
                set_bit(last)

            search(0, COARSE_BITS)
            pick = Chain(dve, pick_chain)
            dve.wait_ge(thr_ready, COARSE_BITS + 1)
            dve.scalar_tensor_tensor(low[:, :], step[:, :], -0.5, thr[:, :], ALU.mult, ALU.add).then_inc(low_ready, 1)
            pick(dve.scalar_tensor_tensor(high[:, :], step[:, :], WINDOW - 0.5, thr[:, :], ALU.mult, ALU.add))
            pick.wait()
            pick(dve.scalar_tensor_tensor(XC[:, :], QT[:, :], high[:, 0:1], QT[:, :], ALU.is_lt, ALU.mult))
            pick.wait()
            pick(dve.max(kept[:, :], XC[:, :]))
            pick.wait()
            dve.wait_ge(low_ready, 1)
            pick(dve.tensor_scalar(spread[:, GROUP * KEPT + 1:GROUP * KEPT + 2], kept[:, KEPT - 1:KEPT], low[:, 0:1], None, ALU.is_ge))
            pick(dve.tensor_scalar(below[:, :], kept[:, :], low[:, 0:1], TOP, ALU.is_lt, ALU.mult))
            pick.wait()
            pick(dve.tensor_tensor(kept[:, :], kept[:, :], below[:, :], ALU.max))
            pick.wait()
            dve.tensor_tensor(spread[:, 0:GROUP * KEPT].rearrange("p (g k) -> p g k", k=KEPT), w("mask8").unsqueeze(2).to_broadcast([P, GROUP, KEPT]),
                              kept[:, :].unsqueeze(1).to_broadcast([P, GROUP, KEPT]), ALU.mult).then_inc(pick_ready, 1)
            dve.wait_ge(pick_spread, 1)
            for n in range(2):
                pick(dve.tensor_scalar(aim[:, n:n + 1], PS[:, 1, GROUP * KEPT:GROUP * KEPT + 1], -1.0, float(LOW + n), ALU.mult, ALU.add))
            pick(dve.tensor_tensor(less, PS[:, 1, 0:GROUP * KEPT].unsqueeze(1).to_broadcast([P, KEPT, GROUP * KEPT]),
                                   kept[:, :].unsqueeze(2).to_broadcast([P, KEPT, GROUP * KEPT]), ALU.is_lt))
            pick.wait()
            pick(dve.tensor_reduce(ranks[:, :], less, AX_X, ALU.add))
            pick.wait()
            for n in range(2):
                pick(dve.scalar_tensor_tensor(picked[:, n], ranks[:, :], aim[:, n:n + 1], kept[:, :], ALU.is_le, ALU.mult))
            pick.wait()
            pick(dve.reduce_max(picked1[:, :], picked[:, :, :], AX_X))
            pick.wait()
            dve.tensor_tensor(spread2[:, :, :], w("mask8").unsqueeze(1).to_broadcast([P, 2, GROUP]),
                              picked1[:, :].unsqueeze(2).to_broadcast([P, 2, GROUP]), ALU.mult).then_inc(pick_ready, 1)
            dve.wait_ge(pick_spread, 2)
            pick(dve.reduce_max(both[:, :], PS[:, 2, 0:2 * GROUP].rearrange("p (s j) -> p s j", s=2), AX_X))
            pick.wait()
            dve.scalar_tensor_tensor(fail[:, :], both[:, 1:2], TOP, PS[:, 1, GROUP * KEPT + 1:GROUP * KEPT + 2], ALU.is_ge, ALU.add).then_inc(pick_ready, 1)
            pick(dve.tensor_scalar(gt[:, :], both[:, 0:1], W_LOW, None, ALU.mult))
            pick.wait()
            pick(dve.scalar_tensor_tensor(gt[:, :], both[:, 1:2], W_HIGH, gt[:, :], ALU.mult, ALU.add))
            dve.wait_ge(pick_spread, 3)
            dve.tensor_copy(fail_int[:, :], PS[0:1, 3, 0:1]).then_inc(branch_ready, 1)
            dve.wait_ge(branch_ready, 1)
            pick.wait()
            with dve.If(dve.value_load(fail_int[0:1, 0:1], min_val=0, max_val=P * P) > 0):
                search(COARSE_BITS, SEARCH_BITS)
                dve.wait_ge(thr_ready, SEARCH_BITS + 1)
                dve.tensor_scalar(thr_top[:, :], thr[:, :], STEP / 2, None, ALU.add).then_inc(tail_ready, 1)
                dve.tensor_scalar(XC[:, :], QT[:, :], thr[:, 0:1], None, ALU.is_gt).then_inc(chain_v, 1)
                dve.wait_ge(chain_v, 2)
                dve.wait_ge(comp_ready, 1)
                dve.tensor_tensor_reduce(out=XC[:, :], in0=XC[:, :], in1=QX[:, :], scale=1.0, scalar=0.0, op0=ALU.mult, op1=ALU.max,
                                         accum_out=above[:, :]).then_inc(chain_v, 1)
                dve.wait_ge(chain_v, 3)
                dve.tensor_scalar(above8[:, :], w("mask8"), above[:, 0:1], None, ALU.mult).then_inc(tail_ready, 1)
                dve.wait_ge(tail_spread, 1)
                dve.reduce_max(above[:, :], PS[:, 1, 0:8], AX_X).then_inc(chain_v, 1)
                dve.wait_ge(chain_v, 4)
                dve.tensor_scalar(upper[:, :], above[:, :], -1.0, TOP, ALU.mult, ALU.add).then_inc(chain_v, 1)
                dve.wait_ge(tail_spread, 2)
                dve.tensor_scalar(flag[:, :], PS[:, 0, 1:2], C * N - RANK + 1.5, None, ALU.is_lt).then_inc(chain_v, 1)
                dve.wait_ge(chain_v, 6)
                dve.tensor_tensor(upper[:, :], upper[:, :], thr[:, :], ALU.subtract).then_inc(chain_v, 1)
                dve.wait_ge(chain_v, 7)
                dve.scalar_tensor_tensor(upper[:, :], upper[:, :], flag[:, 0:1], thr[:, :], ALU.mult, ALU.add).then_inc(chain_v, 1)
                dve.tensor_scalar(gt[:, :], thr[:, :], W_LOW, None, ALU.mult).then_inc(chain_v, 1)
                dve.wait_ge(chain_v, 9)
                dve.scalar_tensor_tensor(gt[:, :], upper[:, :], W_HIGH, gt[:, :], ALU.mult, ALU.add).then_inc(chain_v, 1)
                dve.wait_ge(chain_v, 10)
            dve.tensor_scalar(gt8[:, :], w("gt_sel"), gt[:, 0:1], None, ALU.mult).then_inc(gt_ready, 1)
            dve.wait_ge(gt_spread, 1)
            dve.tensor_scalar(neg_gt[:, :], PS[:, 2, 0:BH], -1.0, None, ALU.mult).then_inc(top_used, 1)
            dve.wait_ge(top_used, 1)
            dve.wait_ge(rel_out, NQ)
            dve.wait_ge(q_in, 16 * BH)
            dve.wait_ge(u_ready, NQ)
            for q in range(NQ + 1):
                if q < NQ:
                    for b in (2 * q, 2 * q + 1):
                        c = cols(b, N)
                        dve.scalar_tensor_tensor(AB[:, c], REL[:, c], neg_gt[:, b:b + 1], AB[:, c], ALU.mult, ALU.add).then_inc(diff_ready, 1)
                if q >= 1:
                    dve.wait_ge(mask_ready, q)
                    dve.tensor_tensor(U[:, cols(q - 1)], U[:, cols(q - 1)], AB[:, cols(q - 1)], ALU.mult).then_inc(gated_ready, 1)

            ln_split_dve(dve, 1)
            dve.wait_ge(logits_ready, NQ)
            top = pick

            def by_token(ap, n=E):
                return ap[:, :].unsqueeze(2).to_broadcast([P, TILES, n])

            rank = w("expert_rank").unsqueeze(1).to_broadcast([P, TILES, E])
            top(dve.tensor_reduce(logits[:, :, :], PS[:, 4].rearrange("p (t s e) -> p t e s", s=2, e=E), AX_X, ALU.add))
            for n, (m, chosen) in enumerate(((best, is_best), (second, is_second))):
                top.wait()
                top(dve.reduce_max(m[:, :], logits[:, :, :], AX_X))
                top.wait()
                top(dve.tensor_tensor(key[:, :, :], logits[:, :, :], by_token(m), ALU.is_equal))
                top.wait()
                top(dve.tensor_tensor(key[:, :, :], key[:, :, :], rank, ALU.mult))
                top.wait()
                top(dve.reduce_max(key_max[:, :], key[:, :, :], AX_X))
                top.wait()
                top(dve.tensor_tensor(chosen[:, :, :], by_token(key_max), rank, ALU.is_equal))
                top.wait()
                if n == 0:
                    top(dve.scalar_tensor_tensor(logits[:, :, :], chosen[:, :, :], -1e30, logits[:, :, :], ALU.mult, ALU.add))
            dve.tensor_tensor(lead[:, :], best[:, :], second[:, :], ALU.subtract).then_inc(lead_ready, 1)
            dve.wait_ge(tanh_ready, 1)
            top(dve.tensor_scalar(share1[:, :], lead[:, :], 0.5, 0.5, ALU.mult, ALU.add))
            top(dve.tensor_scalar(share2[:, :], lead[:, :], -0.5, 0.5, ALU.mult, ALU.add))
            top.wait()
            top(dve.tensor_tensor(combine[:, :, :], is_best[:, :, :], by_token(share1), ALU.mult))
            top.wait()
            top(dve.tensor_tensor(is_second[:, :, :], is_second[:, :, :], by_token(share2), ALU.mult))
            top.wait()
            top(dve.tensor_tensor(combine[:, :, :], combine[:, :, :], is_second[:, :, :], ALU.add))
            top.wait()
            dve.tensor_copy(combine2[:, :, 0], combine[:, :, :]).then_inc(combine_ready, 1)
            dve.wait_ge(combine_ready, 1)
            dve.tensor_tensor(combine2[:, :, 1], combine[:, :, :], combine2[:, :, 0].bitcast(F32), ALU.subtract).then_inc(combine_ready, 1)
            dve.wait_ge(zeroed, 2)
            for q in range(NQ):
                dve.wait_ge(ct_ready, q + 1)
                dve.tensor_copy(CT[0:32, cols(q)], PS[0:32, 1 + q]).then_inc(ct_out, 1)

            def moe_scale(it, n1, p):
                dve.wait_ge(gelu_done[p], n1)
                dve.wait_ge(cb_ready[p], n1)
                wait_last(dve, w2_done[p], it)
                dve.tensor_tensor(HS[:, p], HID[:, bass.ds(it * COLS + p * Q, Q)], PS[:, 1 + p % 2], ALU.mult).then_inc(hs_ready[p], 1)

            def moe_add(it, n1):
                dve.wait_ge(w2_done[PAIRS - 1], n1)
                x_it = X[:, bass.ds(it * N, N)]
                dve.tensor_tensor(x_it, PS[:, 3, 0:N], x_it, ALU.add).then_inc(y_taken, 1)

            dve.wait_ge(x_added, NQ)
            for p in range(PAIRS):
                moe_scale(0, 1, p)
            with dve.Fori(1, BH) as i:
                it, n1 = it_values(dve, i)
                moe_scale(it, n1, 0)
                moe_add(dve.snap(it - 1), it)
                moe_scale(it, n1, 1)
                moe_scale(it, n1, 2)
                moe_scale(it, n1, 3)
            moe_add(BH - 1, BH)

            for q in range(NQ + 4):
                if q < NQ:
                    ln_dve_copy(dve, 2, q)
                if 2 <= q < NQ + 2:
                    ln_dve_scale(dve, 2, q - 2, lambda _: dve.wait_ge(x_added, NQ))
                if 3 <= q < NQ + 3:
                    r = q - 3
                    dve.wait_ge(kv_ready, r + 1)
                    dve.reduce_max(kmax[:, 2 * r:2 * r + 2], PS[0:32, 6 + r % 2].rearrange("p (b n) -> p b n", b=2), AX_X).then_inc(kmax_ready, 1)
                    dve.wait_ge(kmax_ready, r + 1)
                    dve.tensor_scalar(kmax[:, 2 * r:2 * r + 2], kmax[:, 2 * r:2 * r + 2], w("kv_bias", slice(0, 32)), None, ALU.add).then_inc(kb_chain, 1)
                    dve.wait_ge(kb_chain, 2 * r + 1)
                    dve.tensor_scalar(kbias[:, 2 * r:2 * r + 2], kmax[:, 2 * r:2 * r + 2], -1.0, w("kv_bias", slice(0, 32)), ALU.mult, ALU.add).then_inc(kb_chain, 1)
                if q >= 4:
                    r = q - 4
                    dve.wait_ge(ek_exp, 2 * r + 2)
                    dve.reciprocal(krec[:, 2 * r:2 * r + 2], ksum[:, 2 * r:2 * r + 2]).then_inc(krec_ready, 1)
                    dve.wait_ge(krec_ready, r + 1)
                    ek = EKV[0:32, cols(r)].rearrange("p (b n) -> p b n", b=2)
                    dve.tensor_tensor(ek, ek, krec[:, 2 * r:2 * r + 2].unsqueeze(2).to_broadcast([32, 2, N]), ALU.mult).then_inc(ek_ready, 1)

            def by_head(ap):
                return ap.rearrange("p (g d) -> p g d", d=KD)

            def queries_turn(it):
                dve.wait_ge(q_biased, it + 1)
                if it >= 4:
                    dve.wait_ge(qs_ready, it - 3)
                dve.transpose(QB[:, it % 4], Q0[:, it % 2]).then_inc(qb_ready, 1)

            def queries_max(it):
                dve.wait_ge(qb_ready, it + 1)
                if it >= 2:
                    dve.wait_ge(qsub_ready, it - 1)
                dve.reduce_max(qmax[:, it % 2], by_head(QB[:, it % 4]), AX_X).then_inc(qmax_ready, 1)

            def queries_sum(it):
                dve.wait_ge(qexp_ready, it + 1)
                dve.tensor_reduce(qsum[:, it % 2], by_head(QB[:, it % 4]), AX_X, ALU.add).then_inc(qsum_ready, 1)

            def queries_reciprocal(it):
                dve.wait_ge(qsum_ready, it + 1)
                if it >= 2:
                    dve.wait_ge(qn_ready, it - 1)
                dve.reciprocal(qrec[:, it % 2], qsum[:, it % 2]).then_inc(qrec_ready, 1)

            def queries_back(it):
                dve.wait_ge(qn_ready, it + 1)
                if it >= 2:
                    dve.wait_ge(a_ready, it - 1)
                dve.transpose(QS[:, it % 2], QB[:, it % 4]).then_inc(qs_ready, 1)

            def attn_add(it):
                dve.wait_ge(a_ready, it + 1)
                dve.scalar_tensor_tensor(X[:, cols(it, N)], PS[:, 6 + it % 2, 0:N], w("bo"), X[:, cols(it, N)], ALU.add, ALU.add).then_inc(x3_ready, 1)

            for s in range(BH + 3):
                if s < BH:
                    queries_turn(s)
                if 1 <= s < BH + 1:
                    queries_sum(s - 1)
                if s < BH:
                    queries_max(s)
                if 1 <= s < BH + 1:
                    queries_reciprocal(s - 1)
                if s == 1:
                    dve.wait_ge(heads_ready, 1)
                    for h in range(HALVES):
                        dve.tensor_tensor(BD[:, h * BH:(h + 1) * BH].rearrange("p b (g d) -> p b g d", d=KD),
                                          PS[:, 3, cols(h, P)].rearrange("p (b d) -> p b d", b=BH).unsqueeze(2).to_broadcast([P, BH, HEADS, KD]),
                                          w("head_mask").rearrange("p (g d) -> p g d", d=KD).unsqueeze(1).to_broadcast([P, BH, HEADS, KD]),
                                          ALU.mult).then_inc(bd_ready, 1)
                if 2 <= s < BH + 2:
                    queries_back(s - 2)
                if s >= 3:
                    attn_add(s - 3)

            dve.wait_ge(bn_rs, 2)
            dve.tensor_tensor(bn_a[:, :], bn_a[:, :], w("bn_g"), ALU.mult).then_inc(bn_chain, 1)
            dve.tensor_tensor(bn_c[:, :], w("bn_b"), w("bn_m"), ALU.subtract).then_inc(bn_chain, 1)
            dve.wait_ge(bn_chain, 2)
            dve.tensor_tensor(bn_c[:, :], bn_c[:, :], bn_a[:, :], ALU.mult).then_inc(bn_chain, 1)
            dve.wait_ge(bn_chain, 3)
            dve.tensor_tensor(bn_c[:, :], bn_c[:, :], w("bn_be"), ALU.add).then_inc(bn_chain, 1)
            ln_split_dve(dve, 3, lambda _: dve.wait_ge(q_ready, BH))
            f = Chain(dve, fl_chain)
            dve.wait_ge(fl_turned, 1)
            f(dve.tensor_reduce(f_logits[:, :, :], PS[:, 5, 0:32].rearrange("p (t s e) -> p t e s", s=2, e=E), AX_X, ALU.add))
            f.wait()
            br = w("f_br").unsqueeze(1).to_broadcast([P, 2, E])
            f(dve.tensor_scalar(f_logits[:, :, :], f_logits[:, :, :], 1.0 / B, None, ALU.mult))
            f.wait()
            f(dve.tensor_tensor(f_logits[:, :, :], f_logits[:, :, :], br, ALU.add))
            f.wait()
            f(dve.reduce_max(f_max[:, :], f_logits[:, :, :], AX_X))
            f.wait()
            f(dve.tensor_tensor(f_logits[:, :, :], f_logits[:, :, :], f_max[:, :].unsqueeze(2).to_broadcast([P, 2, E]), ALU.subtract))
            dve.wait_ge(fe_ready, 1)
            f(dve.reduce_sum(f_sum[:, :], f_logits[:, :, :], AX_X))
            f.wait()
            f(dve.reciprocal(f_sum[:, :], f_sum[:, :]))
            f.wait()
            dve.tensor_tensor(f_logits[:, :, :], f_logits[:, :, :], f_sum[:, :].unsqueeze(2).to_broadcast([P, 2, E]), ALU.mult).then_inc(fw_ready, 1)

            def f_scale(it, n1, p):
                dve.wait_ge(h2_ready[p], n1)
                wait_last(dve, wo_done[p], it)
                dve.tensor_tensor(HW[:, p].rearrange("p (h n) -> p h n", h=HALVES), H2[:, p].rearrange("p (h n) -> p h n", h=HALVES),
                                  FW[:, p].unsqueeze(1).to_broadcast([P, HALVES, N]), ALU.mult).then_inc(hw_ready[p], 1)

            def f_add(it, n1):
                dve.wait_ge(wo_done[PAIRS - 1], n1)
                dve.wait_ge(bias_added, n1)
                x_it = X[:, bass.ds(it * N, N)]
                dve.tensor_tensor(x_it, PS[:, 4, 0:N], x_it, ALU.add).then_inc(x4_ready, 1)

            dve.wait_ge(ft_ready, 1)
            dve.tensor_copy(fT[:, :], PS[0:E, 5, 0:N]).then_inc(ft_out, 1)
            for g in range(2):
                dve.wait_ge(fb_ready, 2 * g + 2)
                dve.tensor_copy(FW[:, 2 * g:2 * g + 2], PS[:, 6 + g].rearrange("p (g n) -> p g n", g=2)).then_inc(fb_out, 1)
            dve.wait_ge(fb_ready, PAIRS + 1)
            dve.tensor_copy(FB[:, :], PS[:, 5, 0:N]).then_inc(fb_out, 1)
            dve.wait_ge(fb_out, 3)
            for p in range(PAIRS):
                dve.wait_ge(w2_done[p], BH)
            for p in range(PAIRS):
                f_scale(0, 1, p)
            with dve.Fori(1, BH) as i:
                it, n1 = it_values(dve, i)
                f_scale(it, n1, 0)
                f_add(dve.snap(it - 1), it)
                f_scale(it, n1, 1)
                f_scale(it, n1, 2)
                f_scale(it, n1, 3)
            f_add(BH - 1, BH)

        @block.gpsimd
        def _(pool):
            pool.memset(PADDED[:, :], 0.0).then_inc(zeroed, 1)
            pool.memset(CT[:, :].bitcast(F32), 0.0).then_inc(zeroed, 1)
            for q in range(NQ):
                ln_pool_square(pool, 0, q)
            pool.wait_ge(late_in, 16)
            pool.tensor_copy(WH[:, :], WT[:, SPLIT0:SPLIT1]).then_inc(split_high, 1)
            pool.wait_ge(split_high, 1)
            pool.tensor_tensor(WL[:, :], WT[:, SPLIT0:SPLIT1], WH[:, :].bitcast(F32), ALU.subtract).then_inc(split_low, 1)
            pool.wait_ge(split_low, 1)
            for both, name in ((router2, "router"), (f_wr2, "f_wr")):
                pool.tensor_copy(both[:, 0:E], part(WH, name))
                last = pool.tensor_copy(both[:, E:2 * E], part(WL, name))
            last.then_inc(split_low, 1)
            pool.wait_ge(rounded_ready, 1)
            pool.tensor_scalar(QX[:, :], QT[:, :], -1.0, TOP, ALU.mult, ALU.add).then_inc(comp_ready, 1)
            pool.wait_ge(cw_ready, 1)
            pool.wait_ge(t_ready, NQ)
            pool.wait_ge(sw_out, NQ)
            for q in range(NQ):
                pool.tensor_tensor(U[:, cols(q)].rearrange("p (b n) -> p b n", n=N), T[:, cols(q)].rearrange("p (b n) -> p b n", n=N),
                                   CW[:, 2 * q:2 * q + 2].unsqueeze(2).to_broadcast([P, 2, N]), ALU.mult).then_inc(chain_g, 1)
                pool.wait_ge(chain_g, q + 1)
                pool.tensor_tensor(U[:, cols(q)], U[:, cols(q)], SW[:, cols(q)], ALU.mult).then_inc(u_ready, 1)
            for q in range(NQ):
                ln_pool_square(pool, 1, q)
            for q in range(NQ):
                pool.tensor_tensor(X[:, cols(q)], X[:, cols(q)], U[:, cols(q)], ALU.add).then_inc(x1_ready, 1)
            for q in range(NQ):
                pool.wait_ge(t_ready, NQ + q + 1)
                pool.wait_ge(x1_ready, q + 1)
                pool.tensor_tensor(X[:, cols(q)], X[:, cols(q)], T[:, cols(q)], ALU.add).then_inc(x_added, 1)
            for q in range(NQ):
                ln_pool_square(pool, 2, q)
            for s in range(BH + 1):
                if s < BH:
                    pool.wait_ge(qmax_ready, s + 1)
                    q3 = QB[:, s % 4].rearrange("p (g d) -> p g d", d=KD)
                    pool.tensor_tensor(q3, q3, qmax[:, s % 2].unsqueeze(2).to_broadcast([P, 32, KD]), ALU.subtract).then_inc(qsub_ready, 1)
                if s >= 1:
                    pool.wait_ge(qrec_ready, s)
                    q3 = QB[:, (s - 1) % 4].rearrange("p (g d) -> p g d", d=KD)
                    pool.tensor_tensor(q3, q3, qrec[:, (s - 1) % 2].unsqueeze(2).to_broadcast([P, 32, KD]), ALU.mult).then_inc(qn_ready, 1)
            for q in range(NQ):
                ln_pool_square(pool, 3, q)
            pool.wait_ge(fb_out, 3)
            pool.wait_ge(x3_ready, BH)
            pool.wait_ge(xc_ready, 4 * NQ)
            for b in range(BH):
                pool.tensor_tensor(X[:, cols(b, N)], X[:, cols(b, N)], FB[:, :], ALU.add).then_inc(bias_added, 1)


def pack_weights(v):
    a = np.zeros((P, NCOL), np.float32)

    def put(name, rows, value, cols=slice(None)):
        lo, hi = AT[name]
        a[rows, lo:hi][:, cols] = value

    half = [slice(0, C), slice(C, P)]
    eye = np.eye(C, dtype=np.float32)
    put("eps", slice(None), np.array([1e-6, 1e-5, 1e-3, 0], np.float32))
    put("ident", slice(None), np.eye(P, dtype=np.float32))
    group = np.kron(np.eye(P // GROUP), np.ones((GROUP, GROUP))).astype(np.float32)
    put("group", slice(None), group)
    put("mask8", slice(None), np.tile(np.eye(8), (P // 8, 1)))
    put("ones", slice(None), 1.0)
    put("gt_sel", slice(None), np.kron(np.eye(BH), np.ones((HALVES * GROUP, 1))))
    put("half_sel", slice(None), np.tile(np.kron(np.eye(HALVES), np.full((GROUP, C), 1 / GROUP)), (BH, 1)))
    for h, rows in enumerate(half):
        put("center", rows, eye - 1 / C, slice(h * C, (h + 1) * C))
        put("mean", rows, 1 / C, slice(h * C, (h + 1) * C))
        put("tap_th", rows, v["L0_conv_sa_w"].reshape(C, TAPS), slice(h * TAPS, (h + 1) * TAPS))
        put("tap_th", rows, v["L0_conv_tp_w1"].T, slice(32 + h * CR, 32 + (h + 1) * CR))
        put("tp_b1", slice(32 + h * CR, 32 + (h + 1) * CR), v["L0_conv_tp_b1"][:, None])
        put("tp_w2", slice(32 + h * CR, 32 + (h + 1) * CR), v["L0_conv_tp_w2"].T, slice(h * C, (h + 1) * C))
        put("tap_sum", slice(h * TAPS, (h + 1) * TAPS), 1.0, slice(h * C, (h + 1) * C))
        put("ca_w1", rows, v["L0_conv_ca_w1"].T, slice(h * CR, (h + 1) * CR))
        put("ca_b1", slice(h * CR, (h + 1) * CR), v["L0_conv_ca_b1"][:, None])
        put("ca_w2", slice(h * CR, (h + 1) * CR), v["L0_conv_ca_w2"].T, slice(h * C, (h + 1) * C))
        put("ca_b2", rows, v["L0_conv_ca_b2"][:, None])
        put("router", rows, v["L0_ffn_router_w"].T)
        put("f_wr", rows, v["L1_ffn_Wr"])
        put("w1", rows, v["L0_ffn_w1"].transpose(1, 0, 2).reshape(C, E * C))
        put("f_w1", rows, v["L1_ffn_W1"].transpose(1, 0, 2).reshape(C, E * C))
        for part in range(2):
            for e in range(E):
                row = slice(16 * h + E * part + e, 16 * h + E * part + e + 1)
                put("sel", row, 1.0, slice((h * PAIRS + e // 2) * P + e % 2 * C, (h * PAIRS + e // 2) * P + e % 2 * C + C))
                put("b2", row, v["L0_ffn_b2"][e], slice(h * C, (h + 1) * C))
        put("wq", rows, v["L1_conv_Wq"].T, slice(h * P, (h + 1) * P))
        for part, (k_w, k_b) in enumerate((("L1_conv_Wk", "L1_conv_bk"), ("L1_conv_Wv", "L1_conv_bv"))):
            at = slice((2 * part + h) * KD, (2 * part + h + 1) * KD)
            put("wkv", rows, v[k_w].T, at)
            put("kv_bias", at, v[k_b][:, None])
        put("to_heads", slice(h * KD, (h + 1) * KD), np.tile(np.eye(KD), (1, HEADS)), slice(h * P, (h + 1) * P))
        put("bo", rows, v["L1_conv_bo"][:, None])
        put("f_bo", slice(0, E), v["L1_ffn_bo"], slice(h * C, (h + 1) * C))

    def pairs(x):
        return x.reshape(PAIRS, P).T

    put("tp_b2", slice(None), v["L0_conv_tp_b2"][0])
    put("sa_b", slice(None), v["L0_conv_sa_b"][0])
    put("bq", slice(None), v["L1_conv_bq"][:, None])
    put("b1", slice(None), pairs(v["L0_ffn_b1"]))
    put("expert_rank", slice(None), np.arange(E, 0, -1))
    put("w2", slice(None), v["L0_ffn_w2"].reshape(PAIRS, P, C).transpose(1, 0, 2).reshape(P, PAIRS * C))
    put("wo", slice(None), v["L1_conv_Wo"].T)
    put("head_mask", slice(None), np.kron(np.eye(HEADS), np.ones((KD, KD))))
    for name, k in (("bn_g", "g"), ("bn_b", "b"), ("bn_be", "be"), ("bn_m", "m"), ("bn_v", "v")):
        for layer in range(2):
            put(name, slice(None), pairs(v[f"L1_ffn_{k}{layer + 1}"]), slice(layer * PAIRS, (layer + 1) * PAIRS))
    for e in range(E):
        rows = half[e % 2]
        put("f_w2", rows, v["L1_ffn_W2"][e], slice(e * C, (e + 1) * C))
    put("f_wo", slice(None), v["L1_ffn_Wo"].reshape(PAIRS, P, C).transpose(1, 0, 2).reshape(P, PAIRS * C))
    put("f_br", slice(None), v["L1_ffn_br"])
    return a


def kernel(**inputs):
    import concourse.bacc as bacc
    from concourse.bass_utils import run_bass_kernel_spmd

    v = {k: np.asarray(a) for k, a in inputs.items()}
    arrays = {"in_x": np.ascontiguousarray(v["x"]), "in_weights": pack_weights(v)}
    nc = bacc.Bacc("TRN2", target_bir_lowering=False, num_devices=1)
    aps = [nc.dram_tensor(n, a.shape, F32, kind="ExternalInput").ap() for n, a in arrays.items()]
    out = nc.dram_tensor("out_x", v["x"].shape, F32, kind="ExternalOutput").ap()
    metaformer_kernel(nc, *aps, out)
    return run_bass_kernel_spmd(nc, [arrays], core_ids=[0]).results[0]["out_x"]
```
